# Optimizing a Trainium2 kernel written in Bass

```python
import numpy as np
import jax
import jax.numpy as jnp

def _softmax(x, axis=-1):
    return jax.nn.softmax(x, axis=axis)

def _gelu(x):
    return jax.nn.gelu(x, approximate=True)

def _silu(x):
    return jax.nn.silu(x)

def _sigmoid(x):
    return jax.nn.sigmoid(x)

def _layernorm(x, axis=-1, eps=1e-05):
    m = jnp.mean(x, axis=axis, keepdims=True)
    v = jnp.var(x, axis=axis, keepdims=True)
    return (x - m) / jnp.sqrt(v + eps)

def _scatter_add(tgt, idx, src, axis=0):
    return tgt.at[idx].add(src)

def _segment_sum(src, seg, n):
    return jax.ops.segment_sum(src, seg, n)
kernel_name = 'mk_flamingo_gated_d2_seqx_r4_7be636'

def setup_inputs(seed: int=0):
    np.random.seed(seed)
    _w = jnp.asarray

    def _rec_inputs():
        import jax
        import jax.numpy as jnp
        _rk = jax.random.key(seed)
        x = -0.000125 + 0.9999 * jax.random.normal(jax.random.fold_in(_rk, 1), (16, 112, 256), jnp.float32)
        _lenS = 112 - jax.random.randint(jax.random.fold_in(_rk, 7), (16,), 0, max(1, 112 // 4) + 1, jnp.int32)
        _lenS2 = 375 - jax.random.randint(jax.random.fold_in(_rk, 8), (16,), 0, max(1, 375 // 4) + 1, jnp.int32)
        _ctx_1024P = jax.random.normal(jax.random.fold_in(_rk, 11), (16, 16, 256), jnp.float32)
        _ctx_1024c = jax.random.dirichlet(jax.random.fold_in(_rk, 511), 0.3 * jnp.ones((16,), jnp.float32), (16, 375))
        _ctx_1024t = jnp.einsum('bsk,bkd->bsd', _ctx_1024c, _ctx_1024P)
        _ctx_1024t = _ctx_1024t * jax.lax.rsqrt(jnp.mean(jnp.square(_ctx_1024t)) + 1e-12) * 0.953939
        ctx_1024 = -5.72187e-05 + 0.999849 * (_ctx_1024t + 0.3 * jax.random.normal(jax.random.fold_in(_rk, 611), (16, 375, 256), jnp.float32))
        _validS = jnp.arange(112)[None, :] < _lenS[:, None]
        _validS2 = jnp.arange(375)[None, :] < _lenS2[:, None]
        _causal = jnp.tril(jnp.ones((112, 112), dtype=bool))
        mask_BxS2_ik0 = jnp.where(jnp.broadcast_to(_validS2[:, :], (16, 375)), 0, 1).astype(jnp.int32)
        _g = jax.random.normal(jax.random.fold_in(_rk, 9001), (2, 2), jnp.float32)
        _g = jnp.sign(_g) * jnp.maximum(jnp.abs(_g), 1.0) + (_g == 0) * 1.0
        g_xattn = _g[0]
        g_ffn = _g[1]
        return (x, ctx_1024, mask_BxS2_ik0, g_xattn, g_ffn)
    x, ctx_1024, mask_BxS2_ik0, g_xattn, g_ffn = _rec_inputs()

    def _L0_xattn_setup():
        import jax, jax.numpy as jnp
        import numpy as np
        D = 256

        def _layernorm(x, g, b, eps=1e-05):
            m = jnp.mean(x, axis=-1, keepdims=True)
            v = jnp.var(x, axis=-1, keepdims=True)
            return (x - m) / jnp.sqrt(v + eps) * g + b
        key = jax.random.key(seed)
        ks = jax.random.split(key, 12)
        B, Lt, La = (32, 256, 512)
        s = 1.0 / np.sqrt(D)
        return {'text': jax.random.normal(ks[0], (B, Lt, D), jnp.float32), 'audio': jax.random.normal(ks[1], (B, La, D), jnp.float32), 'audio_masks': jax.random.randint(ks[2], (B, La), 0, 2, jnp.int32), 'ln_t_g': jnp.ones((D,), jnp.float32), 'ln_t_b': jnp.zeros((D,), jnp.float32), 'ln_a_g': jnp.ones((D,), jnp.float32), 'ln_a_b': jnp.zeros((D,), jnp.float32), 'Wq': jax.random.normal(ks[3], (D, D), jnp.float32) * s, 'bq': jnp.zeros((D,), jnp.float32), 'Wk': jax.random.normal(ks[4], (D, D), jnp.float32) * s, 'bk': jnp.zeros((D,), jnp.float32), 'Wv': jax.random.normal(ks[5], (D, D), jnp.float32) * s, 'bv': jnp.zeros((D,), jnp.float32), 'ln_p_g': jnp.ones((D,), jnp.float32), 'ln_p_b': jnp.zeros((D,), jnp.float32)}
    _L0_xattn_all = _L0_xattn_setup()
    _L0_xattn_in = {k: v for k, v in _L0_xattn_all.items() if k in ('ln_t_g', 'ln_t_b', 'ln_a_g', 'ln_a_b', 'Wq', 'bq', 'Wk', 'bk', 'Wv', 'bv', 'ln_p_g', 'ln_p_b')}
    del _L0_xattn_all

    def _L0_ffn_setup():
        import jax, jax.numpy as jnp
        import numpy as np
        B, S, D, E, F, K = (4, 256, 256, 8, 704, 1)
        key = jax.random.key(seed)
        ks = jax.random.split(key, 8)
        sc = 0.02
        return {'x_bsD': jax.random.normal(ks[0], (B, S, D), jnp.float32), 'router_DE': jax.random.normal(ks[1], (D, E), jnp.float32) * sc, 'w1_eDF': jax.random.normal(ks[2], (E, D, F), jnp.float32) * sc, 'w3_eDF': jax.random.normal(ks[3], (E, D, F), jnp.float32) * sc, 'w2_eFD': jax.random.normal(ks[4], (E, F, D), jnp.float32) * sc, 'ws1_DF': jax.random.normal(ks[5], (D, F), jnp.float32) * sc, 'ws3_DF': jax.random.normal(ks[6], (D, F), jnp.float32) * sc, 'ws2_FD': jax.random.normal(ks[7], (F, D), jnp.float32) * sc}
    _L0_ffn_all = _L0_ffn_setup()
    _L0_ffn_in = {k: v for k, v in _L0_ffn_all.items() if k in ('router_DE', 'w1_eDF', 'w3_eDF', 'w2_eFD', 'ws1_DF', 'ws3_DF', 'ws2_FD')}
    del _L0_ffn_all

    def _L1_xattn_setup():
        import jax, jax.numpy as jnp
        import numpy as np
        import math
        B, SQ, SK, DQ, DK = (16, 512, 512, 256, 256)
        key = jax.random.key(seed)
        ks = jax.random.split(key, 6)
        return {'bert_feature': jax.random.normal(ks[0], (B, SQ, DQ), dtype=jnp.float32), 'knowledge_feature': jax.random.normal(ks[1], (B, SK, DK), dtype=jnp.float32), 'w1_w': jax.random.normal(ks[2], (DK, DQ), dtype=jnp.float32) * 0.02, 'w1_b': jax.random.normal(ks[3], (DK,), dtype=jnp.float32) * 0.02, 'w2_w': jax.random.normal(ks[4], (DQ, DQ + DK), dtype=jnp.float32) * 0.02, 'w2_b': jax.random.normal(ks[5], (DQ,), dtype=jnp.float32) * 0.02}
    _L1_xattn_all = _L1_xattn_setup()
    _L1_xattn_in = {k: v for k, v in _L1_xattn_all.items() if k in ('w1_w', 'w1_b', 'w2_w', 'w2_b')}
    del _L1_xattn_all

    def _L1_ffn_setup():
        import jax, jax.numpy as jnp
        import numpy as np
        B, S, D = (2, 512, 256)
        H = 512
        E = 8
        K = 2
        HS = 512 * 1
        SCALE = 1.0 / float(np.sqrt(D))
        key = jax.random.key(seed)
        ks = jax.random.split(key, 9)
        init = 0.02
        return {'x': jax.random.normal(ks[0], (B, S, D), dtype=jnp.float32), 'Wr': jax.random.normal(ks[1], (D, E), dtype=jnp.float32) * init, 'rb': jnp.zeros((E,), dtype=jnp.float32), 'W1': jax.random.normal(ks[2], (E, D, H), dtype=jnp.float32) * init, 'W2': jax.random.normal(ks[3], (E, H, D), dtype=jnp.float32) * init, 'W3': jax.random.normal(ks[4], (E, D, H), dtype=jnp.float32) * init, 'Ws1': jax.random.normal(ks[5], (D, HS), dtype=jnp.float32) * init, 'Ws2': jax.random.normal(ks[6], (HS, D), dtype=jnp.float32) * init, 'Ws3': jax.random.normal(ks[7], (D, HS), dtype=jnp.float32) * init}
    _L1_ffn_all = _L1_ffn_setup()
    _L1_ffn_in = {k: v for k, v in _L1_ffn_all.items() if k in ('Wr', 'rb', 'W1', 'W2', 'W3', 'Ws1', 'Ws2', 'Ws3')}
    del _L1_ffn_all
    return {'x': x, 'ctx_1024': ctx_1024, 'mask_BxS2_ik0': mask_BxS2_ik0, 'g_xattn': g_xattn, 'g_ffn': g_ffn, 'L0_xattn_ln_t_g': _L0_xattn_in['ln_t_g'], 'L0_xattn_ln_t_b': _L0_xattn_in['ln_t_b'], 'L0_xattn_ln_a_g': _L0_xattn_in['ln_a_g'], 'L0_xattn_ln_a_b': _L0_xattn_in['ln_a_b'], 'L0_xattn_Wq': _L0_xattn_in['Wq'], 'L0_xattn_bq': _L0_xattn_in['bq'], 'L0_xattn_Wk': _L0_xattn_in['Wk'], 'L0_xattn_bk': _L0_xattn_in['bk'], 'L0_xattn_Wv': _L0_xattn_in['Wv'], 'L0_xattn_bv': _L0_xattn_in['bv'], 'L0_xattn_ln_p_g': _L0_xattn_in['ln_p_g'], 'L0_xattn_ln_p_b': _L0_xattn_in['ln_p_b'], 'L0_ffn_router_DE': _L0_ffn_in['router_DE'], 'L0_ffn_w1_eDF': _L0_ffn_in['w1_eDF'], 'L0_ffn_w3_eDF': _L0_ffn_in['w3_eDF'], 'L0_ffn_w2_eFD': _L0_ffn_in['w2_eFD'], 'L0_ffn_ws1_DF': _L0_ffn_in['ws1_DF'], 'L0_ffn_ws3_DF': _L0_ffn_in['ws3_DF'], 'L0_ffn_ws2_FD': _L0_ffn_in['ws2_FD'], 'L1_xattn_w1_w': _L1_xattn_in['w1_w'], 'L1_xattn_w1_b': _L1_xattn_in['w1_b'], 'L1_xattn_w2_w': _L1_xattn_in['w2_w'], 'L1_xattn_w2_b': _L1_xattn_in['w2_b'], 'L1_ffn_Wr': _L1_ffn_in['Wr'], 'L1_ffn_rb': _L1_ffn_in['rb'], 'L1_ffn_W1': _L1_ffn_in['W1'], 'L1_ffn_W2': _L1_ffn_in['W2'], 'L1_ffn_W3': _L1_ffn_in['W3'], 'L1_ffn_Ws1': _L1_ffn_in['Ws1'], 'L1_ffn_Ws2': _L1_ffn_in['Ws2'], 'L1_ffn_Ws3': _L1_ffn_in['Ws3']}

def reference(x, ctx_1024, mask_BxS2_ik0, g_xattn, g_ffn, L0_xattn_ln_t_g, L0_xattn_ln_t_b, L0_xattn_ln_a_g, L0_xattn_ln_a_b, L0_xattn_Wq, L0_xattn_bq, L0_xattn_Wk, L0_xattn_bk, L0_xattn_Wv, L0_xattn_bv, L0_xattn_ln_p_g, L0_xattn_ln_p_b, L0_ffn_router_DE, L0_ffn_w1_eDF, L0_ffn_w3_eDF, L0_ffn_w2_eFD, L0_ffn_ws1_DF, L0_ffn_ws3_DF, L0_ffn_ws2_FD, L1_xattn_w1_w, L1_xattn_w1_b, L1_xattn_w2_w, L1_xattn_w2_b, L1_ffn_Wr, L1_ffn_rb, L1_ffn_W1, L1_ffn_W2, L1_ffn_W3, L1_ffn_Ws1, L1_ffn_Ws2, L1_ffn_Ws3):
    import jax
    import jax.numpy as jnp

    def _L0_xattn_ref(text, audio, audio_masks, ln_t_g, ln_t_b, ln_a_g, ln_a_b, Wq, bq, Wk, bk, Wv, bv, ln_p_g, ln_p_b):
        import jax, jax.numpy as jnp
        import numpy as np
        D = 256

        def _layernorm(x, g, b, eps=1e-05):
            m = jnp.mean(x, axis=-1, keepdims=True)
            v = jnp.var(x, axis=-1, keepdims=True)
            return (x - m) / jnp.sqrt(v + eps) * g + b
        t = _layernorm(text, ln_t_g, ln_t_b)
        a = _layernorm(audio, ln_a_g, ln_a_b)
        q = t @ Wq + bq
        k = a @ Wk + bk
        v = a @ Wv + bv
        scale = 1.0 / jnp.sqrt(jnp.asarray(audio.shape[-1], t.dtype))
        scores = jnp.einsum('btd,bsd->bts', q, k) * scale
        scores = jnp.where(audio_masks[:, None, :] == 0, jnp.asarray(-1000000000.0, scores.dtype), scores)
        w = jax.nn.softmax(scores, axis=-1)
        cross = jnp.einsum('bts,bsd->btd', w, v)
        return _layernorm(cross, ln_p_g, ln_p_b)

    def _L0_ffn_ref(x_bsD, router_DE, w1_eDF, w3_eDF, w2_eFD, ws1_DF, ws3_DF, ws2_FD):
        import jax, jax.numpy as jnp
        import numpy as np
        B, S, D, E, F, K = (4, 256, 256, 8, 704, 1)
        b, s, d = x_bsD.shape
        a = b * s
        x_aD = x_bsD.reshape(a, d)
        scores_aE = x_aD @ router_DE
        vals_aK, idx_aK = jax.lax.top_k(scores_aE, K)
        masked_aE = jnp.full_like(scores_aE, -jnp.inf).at[jnp.arange(a)[:, None], idx_aK].set(vals_aK)
        gates_Ea = jax.nn.sigmoid(masked_aE).T
        routed_in_EaD = jax.lax.stop_gradient(gates_Ea[:, :, None] * x_aD[None, :, :])
        mid_EaF = jax.nn.silu(jnp.einsum('ead,edf->eaf', routed_in_EaD, w1_eDF)) * jnp.einsum('ead,edf->eaf', routed_in_EaD, w3_eDF)
        routed_out_EaD = jnp.einsum('eaf,efd->ead', mid_EaF, w2_eFD)
        shared_aD = jax.nn.silu(x_aD @ ws1_DF) * (x_aD @ ws3_DF) @ ws2_FD
        out_aD = shared_aD + routed_out_EaD.sum(axis=0)
        return out_aD.reshape(b, s, d)

    def _L1_xattn_ref(bert_feature, knowledge_feature, w1_w, w1_b, w2_w, w2_b):
        import jax, jax.numpy as jnp
        import numpy as np
        import math
        B, SQ, SK, DQ, DK = (16, 512, 512, 256, 256)
        d_k = knowledge_feature.shape[-1]
        bf = jnp.einsum('bqd,kd->bqk', bert_feature, w1_w) + w1_b
        scores = jnp.einsum('bqd,bkd->bqk', bf, knowledge_feature) / math.sqrt(d_k)
        attn = jax.nn.softmax(scores, axis=-1)
        output = jnp.einsum('bqk,bkd->bqd', attn, knowledge_feature)
        fused = jnp.concatenate([bert_feature, output], axis=-1)
        return jnp.einsum('bqf,of->bqo', fused, w2_w) + w2_b

    def _L1_ffn_ref(x, Wr, rb, W1, W2, W3, Ws1, Ws2, Ws3):
        import jax, jax.numpy as jnp
        import numpy as np
        B, S, D = (2, 512, 256)
        H = 512
        E = 8
        K = 2
        HS = 512 * 1
        SCALE = 1.0 / float(np.sqrt(D))
        logits = jnp.einsum('bsd,de->bse', x, Wr) * SCALE
        _, idx = jax.lax.top_k(logits + rb, K)
        gathered = jnp.take_along_axis(logits, idx, axis=-1)
        w = jax.nn.softmax(gathered, axis=-1)
        w_full = jnp.sum(jax.nn.one_hot(idx, E, dtype=x.dtype) * w[..., None], axis=-2)
        h = jnp.einsum('bsd,edh->bseh', x, W1) * jax.nn.silu(jnp.einsum('bsd,edh->bseh', x, W3))
        expert_out = jnp.einsum('bseh,ehd->bsed', h, W2)
        out = jnp.einsum('bsed,bse->bsd', expert_out, w_full)
        hs = jnp.einsum('bsd,dh->bsh', x, Ws1) * jax.nn.silu(jnp.einsum('bsd,dh->bsh', x, Ws3))
        out = out + jnp.einsum('bsh,hd->bsd', hs, Ws2)
        return out
    x = x + jnp.tanh(g_xattn[0]) * _L0_xattn_ref(_layernorm(x, axis=-1), ctx_1024, mask_BxS2_ik0, L0_xattn_ln_t_g, L0_xattn_ln_t_b, L0_xattn_ln_a_g, L0_xattn_ln_a_b, L0_xattn_Wq, L0_xattn_bq, L0_xattn_Wk, L0_xattn_bk, L0_xattn_Wv, L0_xattn_bv, L0_xattn_ln_p_g, L0_xattn_ln_p_b)
    x = x + jnp.tanh(g_ffn[0]) * _L0_ffn_ref(_layernorm(x, axis=-1), L0_ffn_router_DE, L0_ffn_w1_eDF, L0_ffn_w3_eDF, L0_ffn_w2_eFD, L0_ffn_ws1_DF, L0_ffn_ws3_DF, L0_ffn_ws2_FD)
    x = x + jnp.tanh(g_xattn[1]) * _L1_xattn_ref(_layernorm(x, axis=-1), ctx_1024, L1_xattn_w1_w, L1_xattn_w1_b, L1_xattn_w2_w, L1_xattn_w2_b)
    x = x + jnp.tanh(g_ffn[1]) * _L1_ffn_ref(_layernorm(x, axis=-1), L1_ffn_Wr, L1_ffn_rb, L1_ffn_W1, L1_ffn_W2, L1_ffn_W3, L1_ffn_Ws1, L1_ffn_Ws2, L1_ffn_Ws3)
    return x

_drawn_inputs = setup_inputs


def setup_inputs(seed=0):
    import zlib

    import numpy as np

    out = dict(_drawn_inputs(seed))
    spreads = {'g_ffn': (-1.0, 0.6),
     'L0_xattn_ln_t_g': (1.0, 0.2),
     'L0_xattn_ln_t_b': (0.0, 0.355),
     'L0_xattn_ln_a_g': (1.0, 0.2),
     'L0_xattn_ln_a_b': (0.0, 0.1),
     'L0_xattn_bq': (0.0, 0.334),
     'L0_xattn_bk': (0.0, 2.0),
     'L0_xattn_bv': (0.0, 0.1),
     'L0_xattn_ln_p_g': (1.0, 0.2),
     'L0_xattn_ln_p_b': (0.0, 0.1),
     'L1_ffn_rb': (0.0, 0.618)}
    factors = {'L0_ffn_router_DE': 8.0,
     'L0_ffn_w1_eDF': 8.0,
     'L0_ffn_w3_eDF': 8.0,
     'L0_ffn_w2_eFD': 8.0,
     'L0_ffn_ws1_DF': 3.505,
     'L0_ffn_ws3_DF': 3.475,
     'L0_ffn_ws2_FD': 3.477,
     'L1_xattn_w1_w': 29.994,
     'L1_xattn_w1_b': 64.0,
     'L1_xattn_w2_b': 30.56,
     'L1_ffn_Wr': 8.0,
     'L1_ffn_W1': 5.32,
     'L1_ffn_W2': 5.324,
     'L1_ffn_W3': 5.432,
     'L1_ffn_Ws1': 3.806,
     'L1_ffn_Ws2': 3.803,
     'L1_ffn_Ws3': 3.871}
    for name, (base, spread) in spreads.items():
        noise = np.random.default_rng([zlib.crc32(name.encode()), seed]).standard_normal(out[name].shape)
        drawn = base * np.exp(spread * noise) if base else spread * noise
        out[name] = jnp.asarray(drawn.astype(out[name].dtype))
    for name, factor in factors.items():
        out[name] = (out[name] * factor).astype(out[name].dtype)
    return out
```

```python
from contextlib import ExitStack

import concourse.bass as bass
from concourse import mybir

F32 = mybir.dt.float32
I32 = mybir.dt.int32
ACT = mybir.ActivationFunctionType
ALU = mybir.AluOpType
AX_X = mybir.AxisListType.X

P = 128
NB, T, S, D = 16, 112, 375, 256
KD = D // P
SJ = 3
SR = S // SJ
E = 8
SCALE = D ** -0.5
EPS = 1e-5
BIG = 3.0e38
ROW = D + 1
GT = 4
GN = GT * T
FIRST, LOOP_LO, LOOP_HI, LAST = -3, 5, 13, NB + 4


class Layer:
    def __init__(self, n, F, K):
        self.n, self.F, self.K = n, F, K
        self.FC = -(-F // P)
        self.tiles = NB * T * K // P + E - 1
        self.halves = -(-F // 512)
        self.FH = F // self.halves
        self.loop_hi = 4 + (self.tiles - 4) // 4 * 4

    def rows(self, c):
        return min(P, self.F - c * P)


LAYERS = (Layer(0, 704, 1), Layer(1, 512, 2))


class Arena:

    def __init__(self, *parts):
        self.parts = [[t, a, b] for t, a, b in parts]

    def take(self, *shape):
        n = 1
        for s in shape:
            n *= s
        for part in self.parts:
            t, a, b = part
            if a + n <= b:
                part[1] = a + n
                v = t[:, a:a + n]
                if len(shape) == 2:
                    v = v.rearrange("p (a b) -> p a b", a=shape[0])
                if len(shape) == 3:
                    v = v.rearrange("p (a b c) -> p a b c", a=shape[0], b=shape[1])
                if len(shape) == 4:
                    v = v.rearrange("p (a b c d) -> p a b c d", a=shape[0], b=shape[1], c=shape[2])
                return v
        raise ValueError("arena is full")


class Count:

    def __init__(self, sem, start=0):
        self.sem, self.start = sem, start

    def at(self, value):
        return value + self.start if self.start else value


class Steps:

    def __init__(self, count):
        self.sem, self.n, self.base = count.sem if count else None, 0, 0

    def one(self):
        self.n += 1
        return 1

    def total(self):
        return self.n if isinstance(self.base, int) else self.base + self.n


def due(value):
    return not isinstance(value, int) or value > 0


def upto(value, most):
    return min(value, most) if isinstance(value, int) else value


def has(b, n=NB):
    return not isinstance(b, int) or 0 <= b < n


def tile_of(t, b):
    return t[0:T, bass.ds(b, 1), :].rearrange("p a d -> p (a d)")


def flamingo(nc, x, ctx, mask, g_xattn, g_ffn, ln_t_g, ln_t_b, ln_a_g, ln_a_b, Wq, bq, Wk, bk, Wv, bv, ln_p_g,
             ln_p_b, router0, w1_0, w3_0, w2_0, ws1_0, ws3_0, ws2_0, w1_w, w1_b, w2_w, w2_b, router1, rb, w1_1,
             w2_1, w3_1, ws1_1, ws2_1, ws3_1, out):
    expert_w = ((w1_0, w3_0, w2_0), (w3_1, w1_1, w2_1))
    shared_w = ((ws1_0, ws3_0, ws2_0), (ws3_1, ws1_1, ws2_1))
    router_w = (router0, router1)

    stack = ExitStack()
    with stack:
        def sb(name, cols, dt=F32):
            return stack.enter_context(nc.sbuf_tensor(name, [P, cols], dt))

        def sem(name):
            return stack.enter_context(nc.semaphore(name))

        xg = [nc.dram_tensor(f"dispatched{l.n}", [l.tiles * P, ROW], F32, kind="Internal").ap() for l in LAYERS]
        yg = [nc.dram_tensor(f"returned{l.n}", [NB * T * l.K + l.tiles * P, D], F32, kind="Internal").ap()
              for l in LAYERS]
        mask_rows = nc.dram_tensor("mask_rows", [NB, S], F32, kind="Internal").ap()
        xn_rows = [nc.dram_tensor(f"xn_rows{l.n}", [NB, T, D], F32, kind="Internal").ap() for l in LAYERS]

        WCOLS = LAYERS[0].F * 4 * E + LAYERS[0].FC * D * E
        W = sb("expert_weights", WCOLS)
        xs_t = sb("x_stream", NB * D)
        xnT_t = sb("xn_turned", KD * NB * T)
        R = sb("work", 7936)
        KT = sb("layer_constants", 1792)
        fixed = sb("fixed", 800)
        ints = sb("ints", 160, I32)
        ps = stack.enter_context(nc.psum_tensor("ps", [P, 8, 512], F32))

        xs = xs_t[:, :].rearrange("p (b d) -> p b d", b=NB)
        xnT = xnT_t[:, :].rearrange("p (k n) -> p k n", k=KD)

        def expert_views(l):
            n13 = E * 4 * l.F
            gu = W[:, 0:n13].rearrange("p (e m k f) -> p e m k f", e=E, m=2, k=KD)
            back = W[:, n13:n13 + E * l.FC * D].rearrange("p (e c d) -> p e c d", e=E, c=l.FC)
            return gu, back

        wgu, wback = zip(*[expert_views(l) for l in LAYERS])
        l0, l1 = LAYERS
        used1 = E * 4 * l1.F + E * l1.FC * D
        spare = (((W, (E - 1) * 4 * l0.F, E * 4 * l0.F), (W, WCOLS - l0.FC * D, WCOLS)), ((W, used1, WCOLS),))

        f = Arena((fixed, 0, 800))
        ident = f.take(P)
        ones = f.take(P)
        before = f.take(T)
        gt_c, bt_c, ga_c, ba_c = f.take(KD), f.take(KD), f.take(KD), f.take(KD)
        bq_c, bk_c, b1_c = f.take(KD), f.take(KD), f.take(KD)
        wqbk, qbias, c0 = f.take(KD), f.take(KD), f.take(1)
        bqbk = f.take(KD)
        gates_raw, tanh_g = f.take(4), f.take(4)
        route_w = [f.take(KD, E), f.take(KD, E)]
        rb_bc = f.take(E)
        logits = f.take(NB, E)
        mv = f.take(2, 6, 2)
        uvar, rstd, nmr = f.take(2, 6), f.take(2, 6), f.take(2, 3)
        guess, newt = f.take(6), f.take(6)
        bn = f.take(6, 6)
        smax, nbias, rsum, rinv, cq = f.take(1), f.take(4), f.take(4), f.take(4), f.take(4)
        token_w = f.take(NB, 2)
        gate_ring = f.take(4)
        pos_i = ints[:, 0:NB * 2]
        tile_expert = ints[:, 32:32 + 40]
        pos_ring = ints[:, 80:84]
        pad_rows = (ints[:, 88:88 + l0.tiles], ints[:, 112:112 + l1.tiles])

        kept = {}

        def both_layers(name, l, total):
            if name not in kept:
                kept[name] = sem(name)
            return Count(kept[name], total * l.n)

        def one_layer(kind, name, l):
            return Count(sem(f"{kind}{l.n}_{name}"))

        class Attn:
            pass

        class Ffn:
            pass

        A, B = [], []
        for l in LAYERS:
            a = Attn()
            ar = Arena((R, 0, 7936), *spare[l.n])
            a.kv = ar.take(4, SJ, D)
            if l.n == 0:
                a.raw = ar.take(2, SJ, D)
            else:
                a.y = ar.take(2, D)
            a.kT = ar.take(2, KD, S)
            if l.n == 0:
                a.mask_add = ar.take(4, S)
            a.probs = ar.take(S)
            a.pT = ar.take(SJ, T)
            a.crossT = ar.take(KD, T)
            a.tT = ar.take(KD, T)
            a.qT = ar.take(2, KD, T)
            a.xt = ar.take(2, D)
            a.cross = ar.take(D)
            a.xn = ar.take(2, D)
            a.xnTb = ar.take(2, KD, T)
            k = Arena((KT, 0, 1792))
            if l.n == 0:
                a.Aqk, a.Wv, a.gp, a.bp, a.vbias = k.take(KD, D), k.take(KD, D), k.take(D), k.take(D), k.take(D)
                tmp = Arena((xnT_t, 0, KD * NB * T))
                a.Wq_r, a.Wk_r, a.WqT, a.WkT = (tmp.take(KD, D) for _ in range(4))
                a.bvec = tmp.take(KD, P)
                a.mask_i = tmp.take(S).bitcast(I32)
                a.mask_f = tmp.take(S)
                zero = ar.take(D)
            else:
                a.w1T, a.w2T, a.b2 = k.take(KD, D), k.take(2 * KD, D), k.take(D)
                tmp = Arena((xnT_t, 0, KD * NB * T))
                a.w1_r, a.w2_r = tmp.take(KD, D), tmp.take(KD, 2 * D)
            a.consts_in = one_layer("a", "consts_in", l)
            a.setup_pe = one_layer("a", "setup_pe", l)
            a.setup_act = one_layer("a", "setup_act", l)
            a.setup_dve = one_layer("a", "setup_dve", l)
            a.dve_own = one_layer("a", "dve_own", l)
            a.act_own = one_layer("a", "act_own", l)
            if l.n == 0:
                a.x_done = one_layer("a", "x_done", l)
                a.mask_all = one_layer("a", "mask_all", l)
                a.mask_sum = one_layer("a", "mask_sum", l)
                a.mask_stored = one_layer("a", "mask_stored", l)
            else:
                a.raw_in2 = one_layer("a", "raw_in2", l)
                a.raw_in3 = one_layer("a", "raw_in3", l)
                a.y_in0 = one_layer("a", "y_in0", l)
                a.y_in1 = one_layer("a", "y_in1", l)
                a.xpart_done = one_layer("a", "xpart_done", l)
                a.xpart_read = one_layer("a", "xpart_read", l)
                a.x2_done = one_layer("a", "x2_done", l)
                a.b2_in = one_layer("a", "b2_in", l)
            a.normed = both_layers("a_normed", l, NB)
            a.xt_ready = both_layers("a_xt_ready", l, NB)
            a.xb_ready = both_layers("a_xb_ready", l, NB)
            a.turned = both_layers("a_turned", l, NB)
            a.tT_ready = both_layers("a_tT_ready", l, NB)
            a.kT_ready = both_layers("a_kT_ready", l, NB)
            a.q_done = both_layers("a_q_done", l, NB)
            a.q_ready = both_layers("a_q_ready", l, NB)
            a.scores_done = both_layers("a_scores_done", l, NB)
            a.max_ready = both_layers("a_max_ready", l, NB)
            a.probs_ready = both_layers("a_probs_ready", l, NB)
            a.pT_done = both_layers("a_pT_done", l, NB)
            a.pT_ready = both_layers("a_pT_ready", l, NB)
            a.cross_done = both_layers("a_cross_done", l, NB)
            a.crossT_ready = both_layers("a_crossT_ready", l, NB)
            a.final_done = both_layers("a_final_done", l, NB)
            a.final_read = both_layers("a_final_read", l, NB)
            a.xn_ready = both_layers("a_xn_ready", l, NB)
            a.xnturn_done = both_layers("a_xnturn_done", l, NB)
            a.xnTb_ready = both_layers("a_xnTb_ready", l, NB)
            a.router_done = both_layers("a_router_done", l, NB)
            a.logits_ready = both_layers("a_logits_ready", l, NB)
            a.xnT_ready = both_layers("a_xnT_ready", l, NB)
            a.uvar_ready = both_layers("a_uvar_ready", l, NB + 6)
            a.rstd_ready = both_layers("a_rstd_ready", l, NB + 6)
            a.mask_in0 = both_layers("a_mask_in0", l, 4 * NB)
            a.mask_in1 = both_layers("a_mask_in1", l, 4 * NB)
            a.mask_in2 = both_layers("a_mask_in2", l, 4 * NB)
            a.mask_in3 = both_layers("a_mask_in3", l, 4 * NB)
            a.raw_in0 = both_layers("a_raw_in0", l, 16 * NB // 2)
            a.raw_in1 = both_layers("a_raw_in1", l, 16 * NB // 2)
            a.rows_out0 = both_layers("a_rows_out0", l, 16 * NB // 2)
            a.rows_out1 = both_layers("a_rows_out1", l, 16 * NB // 2)
            A.append(a)

            m = Ffn()
            far = Arena((R, 0, 7936)) if l.n == 0 else Arena(*spare[1])
            m.ws_gu = far.take(2, KD, l.F)
            m.ws_back = far.take(l.FC, D)
            m.midT_s = far.take(l.FC, GN)
            m.silu_s = far.take(2, GN)
            sar = Arena(*spare[0]) if l.n == 0 else Arena((R, 0, 7936))
            m.rows = sar.take(4, ROW)
            m.sel, m.eq, m.oh0, m.oh1, m.both, m.acc, m.acc2 = (sar.take(NB, E) for _ in range(7))
            m.mx = sar.take(NB)
            m.lk, m.lw = sar.take(2, NB), sar.take(2, NB)
            m.rev = sar.take(E)
            m.thr = sar.take(14)
            m.cmp = sar.take(E, 14)
            m.ntile, m.cum, m.cum2 = sar.take(E), sar.take(E), sar.take(E)
            m.posf = sar.take(NB)
            m.tile_no = sar.take(l.tiles)
            m.tcmp = sar.take(l.tiles, E)
            m.dest = sar.take(NB * l.K).bitcast(I32)
            m.rev_i, m.thr_i, m.tile_i = (sar.take(n).bitcast(I32) for n in (E, 14, l.tiles))
            rar = Arena((R, 0, 7936))
            if l.n == 1:
                rar.take(7936 // 2)
            m.g = rar.take(4, ROW)
            m.gT = rar.take(2, KD, P)
            m.silu = rar.take(l.F)
            m.mid = rar.take(l.F)
            m.midT = rar.take(l.FC, P)
            m.yo = Arena((R, 0, 3968)).take(2, D) if l.n == 1 else rar.take(2, D)
            m.fin = Arena(*spare[1]).take(4, 2, D)
            m.weights_in = one_layer("f", "weights_in", l)
            m.shared_in = one_layer("f", "shared_in", l)
            m.iota_done = one_layer("f", "iota_done", l)
            m.disp_sel = one_layer("f", "disp_sel", l)
            m.disp_pe = one_layer("f", "disp_pe", l)
            m.disp_ready = one_layer("f", "disp_ready", l)
            m.lk_ready = one_layer("f", "lk_ready", l)
            m.gate_ready = one_layer("f", "gate_ready", l)
            m.own_dve = one_layer("f", "own_dve", l)
            m.own_pool = one_layer("f", "own_pool", l)
            if l.n == 0:
                m.late_in = one_layer("f", "late_in", l)
                m.midT_d = one_layer("f", "midT_d", l)
            else:
                m.fin_in0 = one_layer("f", "fin_in0", l)
                m.fin_in1 = one_layer("f", "fin_in1", l)
                m.fin_in2 = one_layer("f", "fin_in2", l)
                m.fin_in3 = one_layer("f", "fin_in3", l)
                m.fin_ready = one_layer("f", "fin_ready", l)
                m.out_done = one_layer("f", "out_done", l)
            m.rows_in0 = both_layers("f_rows_in0", l, 16 * NB // 4)
            m.rows_in1 = both_layers("f_rows_in1", l, 16 * NB // 4)
            m.rows_in2 = both_layers("f_rows_in2", l, 16 * NB // 4)
            m.rows_in3 = both_layers("f_rows_in3", l, 16 * NB // 4)
            m.scat0 = both_layers("f_scat0", l, 16 * NB // 4)
            m.scat1 = both_layers("f_scat1", l, 16 * NB // 4)
            m.scat2 = both_layers("f_scat2", l, 16 * NB // 4)
            m.scat3 = both_layers("f_scat3", l, 16 * NB // 4)
            m.gate_done = both_layers("f_gate_done", l, NB // GT * l0.FC)
            m.up_done = both_layers("f_up_done", l, NB // GT * l0.FC)
            m.silu_ready = both_layers("f_silu_ready", l, NB // GT * l0.FC)
            m.mid_ready = both_layers("f_mid_ready", l, NB // GT * l0.FC)
            m.shared_done = both_layers("f_shared_done", l, NB // GT)
            m.shared_read = both_layers("f_shared_read", l, NB)
            m.gturn_done = both_layers("f_gturn_done", l, l0.tiles)
            m.gT_ready = both_layers("f_gT_ready", l, l0.tiles)
            m.mturn_done = both_layers("f_mturn_done", l, l0.tiles)
            m.midT_a = both_layers("f_midT_a", l, l0.tiles)
            m.rout_done = both_layers("f_rout_done", l, l0.tiles)
            m.y_ready = both_layers("f_y_ready", l, l0.tiles)
            m.rgate_done = both_layers("f_rgate_done", l, l0.tiles * l0.halves)
            m.rup_done = both_layers("f_rup_done", l, l0.tiles * l0.halves)
            m.rsilu_ready = both_layers("f_rsilu_ready", l, l0.tiles * l0.halves)
            m.rmid_ready = both_layers("f_rmid_ready", l, l0.tiles * l0.halves)
            m.g_in0 = both_layers("f_g_in0", l, 16 * len(range(0, l0.tiles, 4)))
            m.yscat0 = both_layers("f_yscat0", l, 16 * len(range(0, l0.tiles, 4)))
            m.g_in1 = both_layers("f_g_in1", l, 16 * len(range(1, l0.tiles, 4)))
            m.yscat1 = both_layers("f_yscat1", l, 16 * len(range(1, l0.tiles, 4)))
            m.g_in2 = both_layers("f_g_in2", l, 16 * len(range(2, l0.tiles, 4)))
            m.yscat2 = both_layers("f_yscat2", l, 16 * len(range(2, l0.tiles, 4)))
            m.g_in3 = both_layers("f_g_in3", l, 16 * len(range(3, l0.tiles, 4)))
            m.yscat3 = both_layers("f_yscat3", l, 16 * len(range(3, l0.tiles, 4)))
            B.append(m)

        ident_ready = sem("ident_ready")
        x_in = [sem(f"x_in{i}") for i in range(4)]
        small_in = sem("small_in")
        tanh_ready = sem("tanh_ready")
        pads_ready = sem("pads_ready")
        dispatch_zeroed = sem("dispatch_zeroed")
        zeros_ready = sem("zeros_ready")
        init_dve = sem("init_dve")
        dve_last = sem("dve_last")

        def load_expert(eng, l, e4, s):
            g_w, u_w, b_w = expert_w[l.n]
            gu = W[:, 0:E * 4 * l.F].rearrange("p (q f) -> p q f", f=l.F)
            q = l.FC * D // 4
            back = W[:, E * 4 * l.F:E * (4 * l.F + l.FC * D)]
            for m_, w in ((0, g_w), (1, u_w)):
                src = w.rearrange("e d f -> (e d) f")[bass.ds(e4 * (D // 4), D), :].rearrange("(k p) f -> p k f", p=P)
                eng.dma_start(gu[:, bass.ds(e4 + 2 * m_, 2)], src).then_inc(s.sem, 16)
            full = l.F // P
            rows = b_w.rearrange("e f d -> (e f) d")
            eng.dma_start(back[:, bass.ds(e4 * q, full * D)].rearrange("p (c d) -> p c d", d=D),
                          rows[bass.ds(e4 * (l.F // 4), full * P), :].rearrange("(c p) d -> p c d", p=P)
                          ).then_inc(s.sem, 16)
            if full < l.FC:
                r = l.rows(full)
                eng.dma_start(back[0:r, bass.ds(e4 * q + full * D, D)], rows[bass.ds(e4 * (l.F // 4) + full * P, r), :]
                              ).then_inc(s.sem, 16)

        DMAS = [3 + (l.F % P > 0) for l in LAYERS]

        def attention_left(eng, l):
            a = A[l.n]
            eng.wait_ge(a.final_read.sem, a.final_read.at(NB))
            eng.wait_ge(a.logits_ready.sem, a.logits_ready.at(NB))
            eng.wait_ge(a.xnT_ready.sem, a.xnT_ready.at(NB))
            if l.n == 0:
                eng.wait_ge(a.x_done.sem, a.x_done.at(NB))
            eng.wait_ge(a.xb_ready.sem, a.xb_ready.at(NB))
            for s in (a.rows_out0, a.rows_out1):
                eng.wait_ge(s.sem, s.at(16 * NB // 2))

        def i_has_stats(i):
            return not isinstance(i, int) or i < NB + 3

        def loop(eng, body, own, per):
            for i in range(FIRST, LOOP_LO):
                body(i, i % 4)
            n = own.n
            with eng.Fori(LOOP_LO, LOOP_HI - 3, 4) as r:
                own.base = (r - LOOP_LO) * per
                for u in range(4):
                    body(r + u, (LOOP_LO + u) % 4)
            assert own.n == n + 4 * per, (own.n - n, per)
            own.base, own.n = 0, n + (LOOP_HI - LOOP_LO) * per
            for i in range(LOOP_HI, LAST):
                body(i, i % 4)

        def run_tiles(eng, l, body, first):
            for i in range(first, 4):
                body(i, i % 4)
            with eng.Fori(4, l.loop_hi - 3, 4) as r:
                for u in range(4):
                    body(r + u, u)
            for i in range(l.loop_hi, l.tiles + 1):
                body(i, i % 4)

        def load_shared(eng, l):
            m = B[l.n]
            g_w, u_w, b_w = shared_w[l.n]
            for k_, w in ((0, g_w), (1, u_w)):
                eng.dma_start(m.ws_gu[:, k_], w.rearrange("(k p) f -> p k f", p=P)).then_inc(m.shared_in.sem, 16)
            full = l.F // P
            eng.dma_start(m.ws_back[:, 0:full], b_w[0:full * P].rearrange("(c p) d -> p c d", p=P)).then_inc(m.shared_in.sem, 16)
            if full < l.FC:
                eng.dma_start(m.ws_back[0:l.rows(full), full], b_w[full * P:l.F]).then_inc(m.shared_in.sem, 16)

        SMALL = 17
        block = stack.enter_context(nc.Block())

        @block.sync
        def _(sp):
            a = A[0]
            sp.dma_start(xs[0:T, 0:4], x[0:4].rearrange("b t d -> t b d")).then_inc(x_in[0], 16)
            sp.dma_start(a.mask_i[0:NB], mask).then_inc(a.mask_all.sem, 16)

            def ctx_load(l, b, u):
                if not has(b):
                    return
                a = A[l.n]
                if l.n == 0:
                    if due(b - 1):
                        sp.wait_ge(a.normed.sem, a.normed.at(b - 1))
                    sp.dma_start(a.raw[0:SR, u % 2], ctx_tile(b)).then_inc((a.raw_in0, a.raw_in1)[u % 2].sem, 16)
                else:
                    if due(b - 3):
                        sp.wait_ge(a.cross_done.sem, a.cross_done.at(b - 3))
                    sp.dma_start(a.kv[0:SR, u % 4], ctx_tile(b)).then_inc(
                        (a.raw_in0, a.raw_in1, a.raw_in2, a.raw_in3)[u % 4].sem, 16)

            def ctx_tile(b):
                return ctx[bass.ds(b, 1)].rearrange("a (j s) d -> s (a j) d", s=SR)

            def mask_load(l, b, u):
                if l.n == 1 or not has(b):
                    return
                a = A[l.n]
                if isinstance(b, int) and b == 0:
                    sp.wait_ge(a.mask_sum.sem, a.mask_sum.at(1))
                    sp.dma_start(mask_rows, a.mask_f[0:NB]).then_inc(a.mask_stored.sem, 16)
                    sp.wait_ge(a.mask_stored.sem, a.mask_stored.at(16))
                if due(b - 3):
                    sp.wait_ge(a.max_ready.sem, a.max_ready.at(b - 3))
                row = mask_rows[bass.ds(b, 1), :].rearrange("a s -> (a s)")
                mask_in = (a.mask_in0, a.mask_in1, a.mask_in2, a.mask_in3)
                sp.dma_start(a.mask_add[0:T, u % 4], row.partition_broadcast(T)).then_inc(mask_in[u % 4].sem, 16)

            def y_load(l, b, u):
                if l.n == 0 or not has(b):
                    return
                a = A[l.n]
                if due(b - 1):
                    sp.wait_ge(a.x2_done.sem, a.x2_done.at(b - 1))
                sp.dma_start(a.y[0:T, u % 2], yg[0][bass.ds(b * T, T), :]).then_inc((a.y_in0, a.y_in1)[u % 2].sem, 16)

            def rows_store(l, b, u):
                if not has(b):
                    return
                a = A[l.n]
                sp.wait_ge(a.xn_ready.sem, a.xn_ready.at(b + 1))
                dst = xn_rows[l.n][bass.ds(b, 1)].rearrange("a t d -> t (a d)")
                sp.dma_start(dst, a.xn[0:T, u % 2]).then_inc((a.rows_out0, a.rows_out1)[u % 2].sem, 16)

            def attention(l):
                def body(i, u):
                    ctx_load(l, i + (4 if l.n == 0 else 3), u + (4 if l.n == 0 else 3))
                    y_load(l, i + 4, u + 4)
                    mask_load(l, i + 2, u + 2)
                    rows_store(l, i - 3, u - 3)
                for i in range(-4, 4):
                    body(i, i % 4)
                    if i == 0:
                        load_expert(sp, l, 0, B[l.n].weights_in)
                with sp.Fori(4, 9, 4) as r:
                    for u in range(4):
                        body(r + u, u)
                    load_expert(sp, l, r, B[l.n].weights_in)
                for i in range(12, LAST):
                    body(i, i % 4)
                    if i == 12:
                        load_expert(sp, l, 12, B[l.n].weights_in)

            def experts(l):
                a, m = A[l.n], B[l.n]
                attention_left(sp, l)
                per = 4 // l.K
                rows_in = (m.rows_in0, m.rows_in1, m.rows_in2, m.rows_in3)
                scat = (m.scat0, m.scat1, m.scat2, m.scat3)

                def rows(j, first):
                    for u in range(4):
                        if not first:
                            if due(16 * ((j * l.K) // 4) if isinstance(j, int) else j * (4 * l.K)):
                                sp.wait_ge(scat[u].sem, scat[u].at(16 * ((j * l.K) // 4) if isinstance(j, int) else j * (4 * l.K)))
                        src = xn_rows[l.n][bass.ds(j + u // l.K, 1)].rearrange("a t d -> t (a d)")
                        sp.dma_start(m.rows[0:T, u, 0:D], src).then_inc(rows_in[u].sem, 16)
                rows(0, True)
                with sp.Fori(per, NB - per + 1, per) as r:
                    rows(r, False)
                for e in range(E // 2, E - 1 + l.n):
                    load_expert(sp, l, 4 * e, m.weights_in)
                for s in scat:
                    sp.wait_ge(s.sem, s.at(16 * NB * l.K // 4))
                if l.n == 0:
                    load_expert(sp, l, 4 * (E - 1), m.late_in)
                sp.wait_ge(m.shared_done.sem, m.shared_done.at(NB // GT))
                if l.n == 0:
                    b = A[1]
                    sp.dma_start(b.w1_r, w1_w.rearrange("(k p) d -> p k d", p=P)).then_inc(b.consts_in.sem, 16)
                    sp.dma_start(b.w2_r, w2_w.rearrange("(k p) f -> p k f", p=P)).then_inc(b.consts_in.sem, 16)
                g_in = (m.g_in0, m.g_in1, m.g_in2, m.g_in3)
                yscat = (m.yscat0, m.yscat1, m.yscat2, m.yscat3)

                def tile_load(i, u, first):
                    if not has(i, l.tiles):
                        return
                    if not first:
                        if due(16 * (i // 4) if isinstance(i, int) else 4 * (i - u)):
                            sp.wait_ge(yscat[u].sem, yscat[u].at(16 * (i // 4) if isinstance(i, int) else 4 * (i - u)))
                    sp.dma_start(m.g[:, u], xg[l.n][bass.ds(i * P, P), :]).then_inc(g_in[u].sem, 16)
                for i in range(4):
                    tile_load(i, i, True)
                with sp.Fori(4, l.loop_hi - 3, 4) as r:
                    for u in range(4):
                        tile_load(r + u, u, False)
                for i in range(l.loop_hi, l.tiles):
                    tile_load(i, i % 4, False)
                for u in range(4):
                    sp.wait_ge(yscat[u].sem, yscat[u].at(16 * len(range(u, l.tiles, 4))))

            for i in range(1, 4):
                sp.dma_start(xs[0:T, 4 * i:4 * i + 4], x[4 * i:4 * i + 4].rearrange("b t d -> t b d")).then_inc(x_in[i], 16)
            attention(LAYERS[0])
            experts(LAYERS[0])
            attention(LAYERS[1])
            l, m = LAYERS[1], B[1]
            experts(LAYERS[1])
            fin_in = (m.fin_in0, m.fin_in1, m.fin_in2, m.fin_in3)

            def back(j, u):
                if due(j - 3):
                    sp.wait_ge(m.fin_ready.sem, m.fin_ready.at(j - 3))
                src = yg[1][bass.ds(j * (2 * T), 2 * T), :].rearrange("(t k) d -> t k d", k=2)
                sp.dma_start(m.fin[0:T, u], src).then_inc(fin_in[u].sem, 16)

            def store(j, u):
                sp.wait_ge(m.fin_ready.sem, m.fin_ready.at(j + 1))
                sp.dma_start(out[bass.ds(j, 1)].rearrange("a t d -> t (a d)"), tile_of(xs, j)).then_inc(m.out_done.sem, 16)
            for j in range(4):
                back(j, j)
            with sp.Fori(4, NB - 3, 4) as r:
                for u in range(4):
                    store(r + (u - 4), u)
                    back(r + u, u)
            for j in range(NB - 4, NB):
                store(j, j % 4)
            sp.wait_ge(m.out_done.sem, m.out_done.at(16 * NB))

        @block.scalar
        def _(act):
            a0 = A[0]

            def col(dst, v, s):
                act.dma_start(dst, v.rearrange("(k p) -> p k", p=P), allow_slow_non_contiguous=True).then_inc(s, 16)

            act.dma_start(a0.Wq_r, Wq.rearrange("(k p) e -> p k e", p=P)).then_inc(a0.consts_in.sem, 16)
            act.dma_start(a0.Wk_r, Wk.rearrange("(k p) e -> p k e", p=P)).then_inc(a0.consts_in.sem, 16)
            act.dma_start(a0.Wv, Wv.rearrange("(k p) e -> p k e", p=P)).then_inc(a0.consts_in.sem, 16)
            for dst, v in ((gt_c, ln_t_g), (bt_c, ln_t_b), (ga_c, ln_a_g), (ba_c, ln_a_b), (bq_c, bq), (bk_c, bk),
                           (b1_c, w1_b)):
                col(dst, v, small_in)
            for n in range(2):
                act.dma_start(gates_raw[:, n:n + 1], g_xattn[n:n + 1].partition_broadcast(P)).then_inc(small_in, 16)
                act.dma_start(gates_raw[:, 2 + n:3 + n], g_ffn[n:n + 1].partition_broadcast(P)).then_inc(small_in, 16)
                act.dma_start(route_w[n], router_w[n].rearrange("(k p) e -> p k e", p=P)).then_inc(small_in, 16)
            act.dma_start(rb_bc, rb.partition_broadcast(P)).then_inc(small_in, 16)
            act.dma_start(a0.gp, ln_p_g.partition_broadcast(P)).then_inc(small_in, 16)
            act.dma_start(a0.bp, ln_p_b.partition_broadcast(P)).then_inc(small_in, 16)
            act.dma_start(a0.vbias, bv.partition_broadcast(P)).then_inc(small_in, 16)

            act.wait_ge(small_in, 16 * SMALL)
            nc.scalar.activation(tanh_g, gates_raw, ACT.Tanh).then_inc(tanh_ready, 1)

            def setup(l):
                a = A[l.n]
                if l.n == 0:
                    act.wait_ge(a.setup_pe.sem, a.setup_pe.at(1))
                    nc.scalar.copy(a.WqT, ps[:, 0, :].rearrange("p (k d) -> p k d", k=KD)).then_inc(a.setup_act.sem, 1)
                    nc.scalar.copy(a.WkT, ps[:, 1, :].rearrange("p (k d) -> p k d", k=KD)).then_inc(a.setup_act.sem, 1)
                    act.wait_ge(a.setup_pe.sem, a.setup_pe.at(2))
                    nc.scalar.copy(a.Aqk, ps[:, 2, :].rearrange("p (k d) -> p k d", k=KD)).then_inc(a.setup_act.sem, 1)
                    nc.scalar.copy(qbias, ps[:, 3, 0:2]).then_inc(a.setup_act.sem, 1)
                    nc.scalar.copy(wqbk, ps[:, 3, 2:4]).then_inc(a.setup_act.sem, 1)
                    nc.scalar.copy(c0[0:T], ps[0:T, 3, 4:5]).then_inc(a.setup_act.sem, 1)
                else:
                    act.wait_ge(a.setup_pe.sem, a.setup_pe.at(1))
                    nc.scalar.copy(a.w1T, ps[:, 0, :].rearrange("p (k d) -> p k d", k=KD)).then_inc(a.setup_act.sem, 1)
                    for h in range(2):
                        nc.scalar.copy(a.w2T[:, 2 * h:2 * h + 2], ps[:, 1 + h, :].rearrange("p (k d) -> p k d", k=KD)
                                       ).then_inc(a.setup_act.sem, 1)

            def attention(l):
                a = A[l.n]
                own = Steps(a.act_own)

                def body(i, u):
                    b, v = i + 2, (u + 2) % 4
                    if has(b):
                        act.wait_ge(a.turned.sem, a.turned.at(b + 1))
                        if due(b):
                            act.wait_ge(a.q_done.sem, a.q_done.at(b))
                        if l.n == 0:
                            for k in range(KD):
                                ins = nc.scalar.activation(a.tT[:, k], ps[:, 2, k * T:(k + 1) * T], ACT.Identity,
                                                           scale=gt_c[:, k:k + 1], bias=bt_c[:, k:k + 1])
                        else:
                            ins = nc.scalar.copy(a.tT, ps[:, 2, 0:KD * T].rearrange("p (k t) -> p k t", k=KD))
                        ins.then_inc(a.tT_ready.sem, 1)
                    b, v = i - 4, u
                    if has(b):
                        act.wait_ge(a.xnturn_done.sem, a.xnturn_done.at(b + 1))
                        if due(b):
                            act.wait_ge(a.xnT_ready.sem, a.xnT_ready.at(b))
                        nc.scalar.copy(a.xnTb[:, v % 2],
                                       ps[:, 2, KD * T:2 * KD * T].rearrange("p (k t) -> p k t", k=KD)
                                       ).then_inc(a.xnTb_ready.sem, 1)
                    b, v = i, u
                    if has(b):
                        act.wait_ge(a.max_ready.sem, a.max_ready.at(b + 1))
                        if l.n == 1:
                            if due(b):
                                act.wait_ge(a.pT_done.sem, a.pT_done.at(b))
                        raw = a.probs[0:T] if l.n == 0 else ps[0:T, 4, 0:S]
                        nc.scalar.activation(a.probs[0:T], raw, ACT.Exp, scale=SCALE,
                                             bias=nbias[0:T, v:v + 1], accum_out=rsum[0:T, v:v + 1]
                                             ).then_inc(a.probs_ready.sem, 1)
                    b, v = i + 2, (u + 2) % 4
                    if has(b):
                        if due(b - 1):
                            act.wait_ge(a.scores_done.sem, a.scores_done.at(b - 1))
                        for k in range(KD):
                            if l.n == 0:
                                ins = nc.scalar.activation(a.kT[:, v % 2, k], ps[:, k, 0:S], ACT.Identity,
                                                           scale=ga_c[:, k:k + 1], bias=ba_c[:, k:k + 1])
                            else:
                                ins = nc.scalar.copy(a.kT[:, v % 2, k], ps[:, k, 0:S])
                        ins.then_inc(a.kT_ready.sem, 1)
                    b = i - 1
                    if has(b):
                        act.wait_ge(a.cross_done.sem, a.cross_done.at(b + 1))
                        if due(b):
                            act.wait_ge(a.final_done.sem, a.final_done.at(b))
                        nc.scalar.copy(a.crossT, ps[:, 6, 0:KD * T].rearrange("p (k t) -> p k t", k=KD)
                                       ).then_inc(a.crossT_ready.sem, 1)
                    b = i
                    if has(b):
                        act.wait_ge(a.pT_done.sem, a.pT_done.at(b + 1))
                        if due(b):
                            act.wait_ge(a.cross_done.sem, a.cross_done.at(b))
                        nc.scalar.copy(a.pT[0:SR], ps[0:SR, 5, 0:SJ * T].rearrange("p (j t) -> p j t", j=SJ)
                                       ).then_inc(a.pT_ready.sem, 1)
                    b, v = i + 2, (u + 2) % 4
                    if has(b):
                        act.wait_ge(a.q_done.sem, a.q_done.at(b + 1))
                        bias = qbias if l.n == 0 else b1_c
                        for k in range(KD):
                            ins = nc.scalar.activation(a.qT[:, v % 2, k], ps[:, 3, k * T:(k + 1) * T], ACT.Identity,
                                                       bias=bias[:, k:k + 1])
                        if l.n == 0:
                            ins = nc.scalar.activation(cq[0:T, v:v + 1], ps[0:T, 3, 256:257], ACT.Identity,
                                                       bias=c0[0:T])
                        ins.then_inc(a.q_ready.sem, 1)
                    b = i - 4
                    if has(b):
                        act.wait_ge(a.router_done.sem, a.router_done.at(b + 1))
                        nc.scalar.activation(tile_of(logits, b), ps[0:T, 3, 264:264 + E], ACT.Copy,
                                             scale=1.0 if l.n == 0 else SCALE).then_inc(a.logits_ready.sem, 1)
                    b, v = i + 3, (u + 3) % 4
                    if l.n == 0 and has(b):
                        act.wait_ge(a.rstd_ready.sem, a.rstd_ready.at(i + 4))
                        if due(b - 3):
                            act.wait_ge(a.cross_done.sem, a.cross_done.at(b - 3))
                        for j in range(SJ):
                            ins = nc.scalar.activation(a.kv[0:SR, v, j], a.raw[0:SR, v % 2, j], ACT.Identity,
                                                       scale=rstd[0:SR, u % 2, j:j + 1], bias=nmr[0:SR, u % 2, j:j + 1])
                        ins.then_inc(a.normed.sem, 1)
                loop(act, body, own, 0)

            def shared(l):
                m = B[l.n]

                def group(g, first):
                    for c in range(l.FC):
                        n = g * l.FC + c
                        r = l.rows(c)
                        act.wait_ge(m.gate_done.sem, m.gate_done.at(n + 1))
                        if due(n - 1):
                            act.wait_ge(m.mid_ready.sem, m.mid_ready.at(n - 1))
                        nc.scalar.activation(m.silu_s[0:r, c % 2], ps[0:r, c % 2, 0:GN], ACT.Silu
                                             ).then_inc(m.silu_ready.sem, 1)
                group(0, True)
                with act.Fori(1, NB // GT) as g:
                    group(g, False)

            def gates(l):
                m = B[l.n]
                act.wait_ge(m.lk_ready.sem, m.lk_ready.at(1))
                nc.scalar.activation(token_w[0:T].rearrange("p b k -> p k b")[:, 0:l.K], m.lw[0:T, 0:l.K], ACT.Sigmoid
                                     ).then_inc(m.gate_ready.sem, 1)

            def routed(l):
                m = B[l.n]
                C1 = 4

                def turn(i, u):
                    if has(i, l.tiles):
                        act.wait_ge(m.gturn_done.sem, m.gturn_done.at(i + 1))
                        nc.scalar.copy(m.gT[:, u % 2], ps[:, 4, 0:KD * P].rearrange("p (k t) -> p k t", k=KD)
                                       ).then_inc(m.gT_ready.sem, 1)

                def body(i, u):
                    if has(i, l.tiles):
                        for h in range(l.halves):
                            act.wait_ge(m.rgate_done.sem, m.rgate_done.at(i * l.halves + h + 1))
                            if h == 0:
                                if due(i * l.halves):
                                    act.wait_ge(m.rmid_ready.sem, m.rmid_ready.at(i * l.halves))
                            nc.scalar.activation(m.silu[:, h * l.FH:(h + 1) * l.FH], ps[:, h, 0:l.FH], ACT.Silu
                                                 ).then_inc(m.rsilu_ready.sem, 1)
                    turn(i + 1, u + 1)
                    if has(i, l.tiles):
                        act.wait_ge(m.mturn_done.sem, m.mturn_done.at(i + 1))
                        if due(i):
                            act.wait_ge(m.rout_done.sem, m.rout_done.at(i))
                        nc.scalar.copy(m.midT[:, 0:C1], ps[:, 5, :].rearrange("p (c t) -> p c t", c=C1)
                                       ).then_inc(m.midT_a.sem, 1)
                turn(0, 0)
                run_tiles(act, l, body, 0)

            setup(LAYERS[0])
            attention(LAYERS[0])
            gates(LAYERS[0])
            shared(LAYERS[0])
            routed(LAYERS[0])
            act.wait_ge(B[0].rout_done.sem, B[0].rout_done.at(LAYERS[0].tiles))
            a1, l = A[1], LAYERS[1]
            setup(l)
            attention(l)
            attention_left(act, l)
            load_shared(act, l)
            gates(l)
            shared(l)
            routed(l)

        @block.tensor
        def _(pe):
            mm = nc.tensor.matmul

            def setup(l):
                a = A[l.n]
                pe.wait_ge(a.consts_in.sem, a.consts_in.at(16 * (3 if l.n == 0 else 2)))
                if l.n == 0:
                    pe.wait_ge(ident_ready, 4)
                    pe.wait_ge(small_in, 16 * SMALL)
                    for n, w in ((0, a.Wq_r), (1, a.Wk_r)):
                        for r in range(KD):
                            for c in range(KD):
                                ins = nc.tensor.transpose(ps[:, n, c * D + r * P:c * D + (r + 1) * P],
                                                          w[:, r, c * P:(c + 1) * P], ident)
                    ins.then_inc(a.setup_pe.sem, 1)
                    pe.wait_ge(a.setup_act.sem, a.setup_act.at(2))
                    pe.wait_ge(a.setup_dve.sem, a.setup_dve.at(1))
                    for dc in range(KD):
                        for k in range(KD):
                            mm(ps[:, 2, dc * D:(dc + 1) * D], a.WqT[:, k, dc * P:(dc + 1) * P], a.WkT[:, k],
                               start=(k == 0), stop=(k == KD - 1))
                    for dc in range(KD):
                        for k in range(KD):
                            mm(ps[:, 3, dc:dc + 1], a.WkT[:, k, dc * P:(dc + 1) * P], bq_c[:, k:k + 1],
                               start=(k == 0), stop=(k == KD - 1))
                        for k in range(KD):
                            mm(ps[:, 3, 2 + dc:3 + dc], a.WqT[:, k, dc * P:(dc + 1) * P], bk_c[:, k:k + 1],
                               start=(k == 0), stop=(k == KD - 1))
                    for k in range(KD):
                        mm(ps[0:T, 3, 4:5], ones[:, 0:T], bqbk[:, k:k + 1], start=(k == 0), stop=(k == KD - 1))
                    for k in range(KD):
                        ins = mm(ps[0:T, 4, 0:D], a.bvec[:, k, 0:T], a.Wv[:, k], start=(k == 0), stop=(k == KD - 1))
                    ins.then_inc(a.setup_pe.sem, 1)
                    pe.wait_ge(a.setup_act.sem, a.setup_act.at(6))
                else:
                    for r in range(KD):
                        for c in range(KD):
                            nc.tensor.transpose(ps[:, 0, c * D + r * P:c * D + (r + 1) * P],
                                                a.w1_r[:, r, c * P:(c + 1) * P], ident)
                    for r in range(KD):
                        for c in range(2 * KD):
                            ins = nc.tensor.transpose(
                                ps[:, 1 + c // 2, (c % 2) * D + r * P:(c % 2) * D + (r + 1) * P],
                                a.w2_r[:, r, c * P:(c + 1) * P], ident)
                    ins.then_inc(a.setup_pe.sem, 1)
                    pe.wait_ge(a.setup_act.sem, a.setup_act.at(3))

            def attention(l):
                a = A[l.n]

                def body(i, u):
                    b, v = i, u
                    if has(b):
                        if l.n == 0 and isinstance(b, int) and b == 0:
                            pe.wait_ge(a.setup_dve.sem, a.setup_dve.at(3))
                        pe.wait_ge(a.q_ready.sem, a.q_ready.at(b + 1))
                        pe.wait_ge(a.kT_ready.sem, a.kT_ready.at(b + 1))
                        if due(b):
                            pe.wait_ge(a.probs_ready.sem, a.probs_ready.at(b))
                        for k in range(KD):
                            ins = mm(ps[0:T, 4, 0:S], a.qT[:, v % 2, k], a.kT[:, v % 2, k], start=(k == 0),
                                     stop=(k == KD - 1))
                        ins.then_inc(a.scores_done.sem, 1)
                    if due(upto(i + 2, NB)):
                        pe.wait_ge(a.tT_ready.sem, a.tT_ready.at(upto(i + 2, NB)))
                    if due(upto(i - 4, NB)):
                        pe.wait_ge(a.xnTb_ready.sem, a.xnTb_ready.at(upto(i - 4, NB)))
                    b, v = i - 4, u
                    if has(b):
                        pe.wait_ge(a.xn_ready.sem, a.xn_ready.at(b + 1))
                        for k in range(KD):
                            ins = nc.tensor.transpose(ps[:, 2, (KD + k) * T:(KD + k + 1) * T],
                                                      a.xn[0:T, v % 2, k * P:(k + 1) * P], ident[0:T, 0:T])
                        ins.then_inc(a.xnturn_done.sem, 1)
                    b, v = i + 2, (u + 2) % 4
                    if has(b):
                        pe.wait_ge(a.xt_ready.sem, a.xt_ready.at(b + 1))
                        if l.n == 0:
                            pe.wait_ge(a.normed.sem, a.normed.at(b + 1))
                        if l.n == 1:
                            raw_in = (a.raw_in0, a.raw_in1, a.raw_in2, a.raw_in3)
                            pe.wait_ge(raw_in[v].sem, raw_in[v].at(16 * (b // 4 + 1) if isinstance(b, int) else 4 * (b - v) + 16))
                        for k in range(KD):
                            nc.tensor.transpose(ps[:, 2, k * T:(k + 1) * T], a.xt[0:T, v % 2, k * P:(k + 1) * P],
                                                ident[0:T, 0:T])
                        if due(b):
                            pe.wait_ge(a.kT_ready.sem, a.kT_ready.at(b))
                        for k in range(KD):
                            for j in range(SJ):
                                ins = nc.tensor.transpose(ps[:, k, j * SR:(j + 1) * SR],
                                                          a.kv[0:SR, v, j, k * P:(k + 1) * P], ident[0:SR, 0:SR])
                        ins.then_inc(a.turned.sem, 1)
                    b = i - 2
                    if has(b):
                        pe.wait_ge(a.crossT_ready.sem, a.crossT_ready.at(b + 1))
                        if due(b):
                            pe.wait_ge(a.final_read.sem, a.final_read.at(b))
                        if l.n == 1:
                            if due(upto(i + 2, NB)):
                                pe.wait_ge(a.xpart_read.sem, a.xpart_read.at(upto(i + 2, NB)))
                        w = a.Wv if l.n == 0 else a.w2T[:, KD:2 * KD]
                        for k in range(KD):
                            ins = mm(ps[0:T, 7, 0:D], a.crossT[:, k], w[:, k], start=(k == 0), stop=(k == KD - 1))
                        ins.then_inc(a.final_done.sem, 1)
                    b, v = i - 1, (u - 1) % 4
                    if has(b):
                        pe.wait_ge(a.pT_ready.sem, a.pT_ready.at(b + 1))
                        if due(b):
                            pe.wait_ge(a.crossT_ready.sem, a.crossT_ready.at(b))
                        for k in range(KD):
                            for j in range(SJ):
                                ins = mm(ps[:, 6, k * T:(k + 1) * T], a.kv[0:SR, v, j, k * P:(k + 1) * P],
                                         a.pT[0:SR, j], start=(j == 0), stop=(j == SJ - 1))
                        ins.then_inc(a.cross_done.sem, 1)
                    b = i - 4
                    if due(upto(i + 2, NB)):
                        pe.wait_ge(a.q_ready.sem, a.q_ready.at(upto(i + 2, NB)))
                    if due(upto(b, NB)):
                        pe.wait_ge(a.logits_ready.sem, a.logits_ready.at(upto(b, NB)))
                    if has(b):
                        pe.wait_ge(a.xnTb_ready.sem, a.xnTb_ready.at(b + 1))
                        for k in range(KD):
                            ins = mm(ps[0:T, 3, 264:264 + E], a.xnTb[:, u % 2, k], route_w[l.n][:, k], start=(k == 0),
                                     stop=(k == KD - 1))
                        ins.then_inc(a.router_done.sem, 1)
                    b = i + 2
                    if has(b):
                        pe.wait_ge(a.tT_ready.sem, a.tT_ready.at(b + 1))
                        if l.n == 1:
                            if due(i - 1):
                                pe.wait_ge(a.final_read.sem, a.final_read.at(i - 1))
                            if due(b):
                                pe.wait_ge(a.xpart_read.sem, a.xpart_read.at(b))
                            for k in range(KD):
                                ins = mm(ps[0:T, 7, D:2 * D], a.tT[:, k], a.w2T[:, k], start=(k == 0),
                                         stop=(k == KD - 1))
                            ins.then_inc(a.xpart_done.sem, 1)
                        w = a.Aqk if l.n == 0 else a.w1T
                        for h in range(KD):
                            for k in range(KD):
                                ins = mm(ps[:, 3, h * T:(h + 1) * T], w[:, k, h * P:(h + 1) * P], a.tT[:, k],
                                         start=(k == 0), stop=(k == KD - 1))
                        if l.n == 0:
                            for k in range(KD):
                                ins = mm(ps[0:T, 3, 256:257], a.tT[:, k], wqbk[:, k:k + 1], start=(k == 0),
                                         stop=(k == KD - 1))
                        ins.then_inc(a.q_done.sem, 1)
                    b = i
                    if has(b):
                        pe.wait_ge(a.probs_ready.sem, a.probs_ready.at(b + 1))
                        if due(b):
                            pe.wait_ge(a.pT_ready.sem, a.pT_ready.at(b))
                        for j in range(SJ):
                            ins = nc.tensor.transpose(ps[0:SR, 5, j * T:(j + 1) * T],
                                                      a.probs[0:T, j * SR:(j + 1) * SR], ident[0:T, 0:T])
                        ins.then_inc(a.pT_done.sem, 1)
                loop(pe, body, Steps(None), 0)

            def dispatch(l):
                a, m = A[l.n], B[l.n]
                pe.wait_ge(a.logits_ready.sem, a.logits_ready.at(NB))
                pe.wait_ge(m.disp_sel.sem, m.disp_sel.at(1))
                sel = m.both[0:T].rearrange("p b e -> p (b e)")
                mm(ps[0:T, 4, 0:NB * E], before[0:T], sel, start=True, stop=True)
                mm(ps[0:T, 5, 0:NB * E], ones[0:T, 0:T], sel, start=True, stop=True).then_inc(m.disp_pe.sem, 1)

            def shared(l):
                a, m = A[l.n], B[l.n]
                pe.wait_ge(m.shared_in.sem, m.shared_in.at(16 * DMAS[l.n]))
                pe.wait_ge(a.xnT_ready.sem, a.xnT_ready.at(NB))
                pe.wait_ge(m.disp_ready.sem, m.disp_ready.at(1))

                def back(g, c):
                    pe.wait_ge(m.mid_ready.sem, m.mid_ready.at(g * l.FC + c + 1))
                    if c == 0:
                        if due(g * GT):
                            pe.wait_ge(m.shared_read.sem, m.shared_read.at(g * GT))
                    r = l.rows(c)
                    for j in range(GT):
                        ins = mm(ps[0:T, 4 + j, 0:D], m.midT_s[0:r, c, j * T:(j + 1) * T], m.ws_back[0:r, c],
                                 start=(c == 0), stop=(c == l.FC - 1))
                    if c == l.FC - 1:
                        ins.then_inc(m.shared_done.sem, 1)

                def group(g):
                    for c in range(l.FC):
                        n = g * l.FC + c
                        r = l.rows(c)
                        for half, bank, free, done in ((0, c % 2, m.silu_ready, m.gate_done),
                                                       (1, 2 + c % 2, m.mid_ready, m.up_done)):
                            if due(n - 1):
                                pe.wait_ge(free.sem, free.at(n - 1))
                            pe.nop(nofuse=True)
                            for k in range(KD):
                                ins = mm(ps[0:r, bank, 0:GN], m.ws_gu[:, half, k, c * P:c * P + r],
                                         xnT[:, k, bass.ds(g * GN, GN)], start=(k == 0), stop=(k == KD - 1))
                            ins.then_inc(done.sem, 1)
                        if c:
                            back(g, c - 1)
                    back(g, l.FC - 1)
                group(0)
                with pe.Fori(1, NB // GT) as g:
                    group(g)

            def routed(l):
                m = B[l.n]
                g_in = (m.g_in0, m.g_in1, m.g_in2, m.g_in3)
                pe.wait_ge(m.weights_in.sem, m.weights_in.at(16 * DMAS[l.n] * (E - 1 + l.n)))
                if l.n == 0:
                    pe.wait_ge(m.late_in.sem, m.late_in.at(16 * DMAS[0]))
                pe.wait_ge(m.shared_read.sem, m.shared_read.at(NB))
                C1 = 4

                def turn(i, u):
                    if has(i, l.tiles):
                        u = u % 4
                        pe.wait_ge(g_in[u].sem, g_in[u].at(16 * (i // 4 + 1) if isinstance(i, int) else 4 * (i - u) + 16))
                        if due(i):
                            pe.wait_ge(m.gT_ready.sem, m.gT_ready.at(i))
                        for k in range(KD):
                            ins = nc.tensor.transpose(ps[:, 4, k * P:(k + 1) * P], m.g[:, u, k * P:(k + 1) * P], ident)
                        ins.then_inc(m.gturn_done.sem, 1)

                def body(i, u):
                    turn(i + 1, u + 1)
                    if has(i, l.tiles):
                        e = pe.value_load(tile_expert[0:1, bass.ds(i, 1)], min_val=0, max_val=E - 1)
                        pe.wait_ge(m.gT_ready.sem, m.gT_ready.at(i + 1))
                        for half, free, done in ((0, m.rsilu_ready, m.rgate_done), (1, m.rmid_ready, m.rup_done)):
                            for h in range(l.halves):
                                if h == 0:
                                    if due(i * l.halves):
                                        pe.wait_ge(free.sem, free.at(i * l.halves))
                                for k in range(KD):
                                    w = wgu[l.n][:, bass.ds(e, 1), half, k, h * l.FH:(h + 1) * l.FH]
                                    ins = mm(ps[:, 2 * half + h, 0:l.FH], m.gT[:, u % 2, k],
                                             w.rearrange("p a f -> p (a f)"), start=(k == 0), stop=(k == KD - 1))
                                ins.then_inc(done.sem, 1)
                    if has(i - 1, l.tiles):
                        e = pe.value_load(tile_expert[0:1, bass.ds(i - 1, 1)], min_val=0, max_val=E - 1)
                        if due(i):
                            pe.wait_ge(m.midT_a.sem, m.midT_a.at(i))
                        if l.FC > C1:
                            if due(i):
                                pe.wait_ge(m.midT_d.sem, m.midT_d.at(i))
                        if due(i - 1):
                            pe.wait_ge(m.y_ready.sem, m.y_ready.at(i - 1))
                        for c in range(l.FC):
                            r = l.rows(c)
                            w = wback[l.n][0:r, bass.ds(e, 1), c, :].rearrange("p a d -> p (a d)")
                            ins = mm(ps[:, 7, 0:D], m.midT[0:r, c], w, start=(c == 0), stop=(c == l.FC - 1))
                        ins.then_inc(m.rout_done.sem, 1)
                    if has(i, l.tiles):
                        pe.wait_ge(m.rmid_ready.sem, m.rmid_ready.at((i + 1) * l.halves))
                        if due(i):
                            pe.wait_ge(m.midT_a.sem, m.midT_a.at(i))
                        for c in range(l.FC):
                            r = l.rows(c)
                            ins = nc.tensor.transpose(ps[0:r, 5 + c // C1, (c % C1) * P:(c % C1 + 1) * P],
                                                      m.mid[:, c * P:c * P + r], ident)
                        ins.then_inc(m.mturn_done.sem, 1)
                turn(0, 0)
                run_tiles(pe, l, body, 0)

            for l in LAYERS:
                setup(l)
                attention(l)
                dispatch(l)
                shared(l)
                routed(l)

        @block.vector
        def _(dve):
            v_ = nc.vector

            v_.memset(mv, 1.0).then_inc(init_dve, 1)
            v_.memset(uvar, 1.0).then_inc(init_dve, 1)

            def masks(a):
                dve.wait_ge(a.mask_all.sem, a.mask_all.at(16))
                v_.tensor_scalar(a.mask_f[0:NB], a.mask_i[0:NB], 0.0, -BIG, ALU.is_equal, ALU.mult
                                 ).then_inc(a.mask_sum.sem, 1)

            def weights_before(a):
                dve.wait_ge(small_in, 16 * SMALL)
                dve.wait_ge(ident_ready, 4)
                dve.wait_ge(tanh_ready, 1)
                v_.tensor_tensor(bqbk, bq_c, bk_c, ALU.mult)
                for k in range(KD):
                    ins = v_.tensor_scalar(a.bvec[:, k], ones, ba_c[:, k:k + 1], None, ALU.mult)
                ins.then_inc(a.setup_dve.sem, 1)
                v_.tensor_scalar(a.gp, a.gp, tanh_g[:, 0:1], None, ALU.mult)
                v_.tensor_scalar(a.bp, a.bp, tanh_g[:, 0:1], None, ALU.mult).then_inc(a.setup_dve.sem, 1)

            def weights_after(a):
                dve.wait_ge(a.consts_in.sem, a.consts_in.at(48))
                dve.wait_ge(a.setup_pe.sem, a.setup_pe.at(2))
                v_.tensor_tensor(a.vbias[0:T], a.vbias[0:T], ps[0:T, 4, 0:D], ALU.add)
                for k in range(KD):
                    ins = v_.tensor_scalar(a.Wv[:, k], a.Wv[:, k], ga_c[:, k:k + 1], None, ALU.mult)
                ins.then_inc(a.setup_dve.sem, 1)
                dve.wait_ge(a.setup_dve.sem, a.setup_dve.at(3))

            def attention(l):
                own = Steps(A[l.n].dve_own)
                a = A[l.n]
                tanh_a = tanh_g[0:T, l.n:l.n + 1]

                def body(i, u):
                    if l.n == 0 and isinstance(i, int):
                        if i == -2:
                            weights_before(a)
                        if i == -1:
                            masks(a)
                            weights_after(a)
                    it = i + 4
                    w = u % 2
                    b, v = i, u
                    if has(b):
                        dve.wait_ge(a.scores_done.sem, a.scores_done.at(b + 1))
                        if l.n == 1:
                            v_.tensor_reduce(smax[0:T], ps[0:T, 4, 0:S], AX_X, ALU.max).then_inc(own.sem, own.one())
                            dve.wait_ge(own.sem, own.total())
                        else:
                            mask_in = (a.mask_in0, a.mask_in1, a.mask_in2, a.mask_in3)[v]
                            dve.wait_ge(mask_in.sem, mask_in.at(16 * (b // 4 + 1) if isinstance(b, int)
                                                                else 4 * (b - v) + 16))
                            if due(b):
                                dve.wait_ge(a.pT_done.sem, a.pT_done.at(b))
                            dve.nop(nofuse=True)
                            v_.tensor_tensor_reduce(a.probs[0:T], ps[0:T, 4, 0:S], a.mask_add[0:T, v],
                                                    1.0, -BIG, ALU.add, ALU.max, smax[0:T]).then_inc(own.sem, own.one())
                            dve.wait_ge(own.sem, own.total())
                            v_.scalar_tensor_tensor(smax[0:T], smax[0:T], cq[0:T, v:v + 1], cq[0:T, v:v + 1],
                                                    ALU.add, ALU.subtract).then_inc(own.sem, own.one())
                            dve.wait_ge(own.sem, own.total())
                        v_.tensor_scalar(nbias[0:T, v:v + 1], smax[0:T], -SCALE, None, ALU.mult
                                         ).then_inc(a.max_ready.sem, 1)
                    if not i_has_stats(i):
                        tail(i, u)
                        return
                    if l.n == 0:
                        if due(upto(i + 2, NB)):
                            dve.wait_ge(a.normed.sem, a.normed.at(upto(i + 2, NB)))
                        if due(upto(i - 3, NB)):
                            dve.wait_ge(a.x_done.sem, a.x_done.at(upto(i - 3, NB)))
                    b, v = i + 3, (u + 3) % 4
                    if has(b):
                        if l.n == 0:
                            raw_in = (a.raw_in0, a.raw_in1)[v % 2]
                            dve.wait_ge(raw_in.sem, raw_in.at(16 * (b // 2 + 1) if isinstance(b, int) else 8 * (b - v % 2) + 16))
                            for j in range(SJ):
                                v_.bn_stats(bn[0:SR, j], a.raw[0:SR, v % 2, j]).then_inc(own.sem, own.one())
                            if isinstance(b, int):
                                dve.wait_ge(x_in[b // 4], 16)
                            elif v == LOOP_LO + 3 & 3:
                                for s in x_in:
                                    dve.wait_ge(s, 16)
                        else:
                            y_in = (a.y_in0, a.y_in1)[v % 2]
                            dve.wait_ge(y_in.sem, y_in.at(16 * (b // 2 + 1) if isinstance(b, int) else 8 * (b - v % 2) + 16))
                            ins = v_.scalar_tensor_tensor(tile_of(xs, b), a.y[0:T, v % 2], tanh_g[0:T, 2:3],
                                                          tile_of(xs, b), ALU.mult, ALU.add)
                            ins.then_inc(a.x2_done.sem, 1)
                            dve.wait_ge(a.x2_done.sem, a.x2_done.at(b + 1))
                        dve.nop(nofuse=True)
                        v_.bn_stats(bn[0:T, 5], tile_of(xs, b)).then_inc(own.sem, own.one())
                    if has(i - 2):
                        final(i - 2, (u - 2) % 4)
                        if l.n == 0:
                            v_.bn_stats(bn[0:T, 3], a.cross[0:T]).then_inc(own.sem, own.one())
                    b = i - 3
                    if has(b):
                        x_is_final = a.final_read if l.n else a.x_done
                        dve.wait_ge(x_is_final.sem, x_is_final.at(b + 1))
                        dve.nop(nofuse=True)
                        v_.bn_stats(bn[0:T, 4], tile_of(xs, b)).then_inc(own.sem, own.one())
                    dve.wait_ge(own.sem, own.total())
                    dve.nop(nofuse=True)
                    if has(i + 3):
                        if l.n == 0:
                            for j in range(SJ):
                                v_.bn_aggr(mv[0:SR, w, j], bn[0:SR, j]).then_inc(own.sem, own.one())
                        v_.bn_aggr(mv[0:T, w, 5], bn[0:T, 5]).then_inc(own.sem, own.one())
                    if has(i - 2) and l.n == 0:
                        v_.bn_aggr(mv[0:T, w, 3], bn[0:T, 3]).then_inc(own.sem, own.one())
                    if has(i - 3):
                        v_.bn_aggr(mv[0:T, w, 4], bn[0:T, 4]).then_inc(own.sem, own.one())
                    dve.wait_ge(own.sem, own.total())
                    if l.n == 0:
                        v_.tensor_scalar(uvar[:, w, 0:5], mv[:, w, 0:5, 1], EPS, None, ALU.add)
                        ins = v_.tensor_scalar(uvar[:, w, 5:6], mv[:, w, 5:6, 1], 1.0 + EPS, EPS * EPS, ALU.mult,
                                               ALU.add)
                    else:
                        ins = v_.tensor_scalar(uvar[:, w, :], mv[:, w, :, 1], EPS, None, ALU.add)
                    ins.then_inc(a.uvar_ready.sem, 1)
                    dve.wait_ge(a.uvar_ready.sem, a.uvar_ready.at(it))
                    v_.tensor_scalar(guess.bitcast(I32), uvar[:, w, :].bitcast(I32), -0.5, float(0x5f3759df), ALU.mult,
                                     ALU.add).then_inc(own.sem, own.one())
                    dve.wait_ge(own.sem, own.total())
                    for step in range(3):
                        v_.scalar_tensor_tensor(newt, guess, -0.5, guess, ALU.mult, ALU.mult
                                                ).then_inc(own.sem, own.one())
                        dve.wait_ge(own.sem, own.total())
                        v_.tensor_tensor(newt, newt, uvar[:, w, :], ALU.mult).then_inc(own.sem, own.one())
                        dve.wait_ge(own.sem, own.total())
                        if step < 2:
                            v_.scalar_tensor_tensor(guess, newt, 1.5, guess, ALU.add, ALU.mult
                                                    ).then_inc(own.sem, own.one())
                            dve.wait_ge(own.sem, own.total())
                    v_.scalar_tensor_tensor(rstd[:, w, :], newt, 1.5, guess, ALU.add, ALU.mult
                                            ).then_inc(own.sem, own.one())
                    dve.wait_ge(own.sem, own.total())
                    v_.scalar_tensor_tensor(nmr[:, w, :], mv[:, w, 0:SJ, 0], -1.0, rstd[:, w, 0:SJ], ALU.mult, ALU.mult
                                            ).then_inc(a.rstd_ready.sem, 1)
                    dve.wait_ge(a.rstd_ready.sem, a.rstd_ready.at(it))
                    b, v = i + 3, (u + 3) % 4
                    if has(b):
                        if due(b - 1):
                            dve.wait_ge(a.turned.sem, a.turned.at(b - 1))
                        v_.tensor_scalar(a.xt[0:T, v % 2], tile_of(xs, b), mv[0:T, w, 5, 0:1], rstd[0:T, w, 5:6],
                                         ALU.subtract, ALU.mult).then_inc(a.xt_ready.sem, 1)
                    b = i - 2
                    if has(b) and l.n == 0:
                        dve.wait_ge(a.xb_ready.sem, a.xb_ready.at(b + 1))
                        v_.scalar_tensor_tensor(a.cross[0:T], a.cross[0:T], mv[0:T, w, 3, 0:1], a.gp[0:T],
                                                ALU.subtract, ALU.mult).then_inc(own.sem, own.one())
                        dve.wait_ge(own.sem, own.total())
                        v_.scalar_tensor_tensor(tile_of(xs, b), a.cross[0:T], rstd[0:T, w, 3:4], tile_of(xs, b),
                                                ALU.mult, ALU.add).then_inc(a.x_done.sem, 1)
                    b, v = i - 3, (u - 3) % 4
                    if has(b):
                        if due(b - 1):
                            dve.wait_ge(a.xnturn_done.sem, a.xnturn_done.at(b - 1))
                        if not isinstance(b, int) or b >= 2:
                            out_ = (a.rows_out0, a.rows_out1)[v % 2]
                            j = b - 2
                            dve.wait_ge(out_.sem, out_.at(16 * (j // 2 + 1) if isinstance(j, int) else 8 * (j - v % 2) + 16))
                        v_.tensor_scalar(a.xn[0:T, v % 2], tile_of(xs, b), mv[0:T, w, 4, 0:1], rstd[0:T, w, 4:5],
                                         ALU.subtract, ALU.mult).then_inc(a.xn_ready.sem, 1)
                    tail(i, u)

                def final(b, v):
                    dve.wait_ge(a.final_done.sem, a.final_done.at(b + 1))
                    dve.wait_ge(a.probs_ready.sem, a.probs_ready.at(b + 1))
                    if l.n == 0:
                        v_.reciprocal(rinv[0:T, v:v + 1], rsum[0:T, v:v + 1]).then_inc(own.sem, own.one())
                        dve.wait_ge(own.sem, own.total())
                        if due(b):
                            dve.wait_ge(a.x_done.sem, a.x_done.at(b))
                        v_.scalar_tensor_tensor(a.cross[0:T], ps[0:T, 7, 0:D], rinv[0:T, v:v + 1],
                                                a.vbias[0:T], ALU.mult, ALU.add).then_inc(a.final_read.sem, 1)
                        dve.wait_ge(a.final_read.sem, a.final_read.at(b + 1))
                    else:
                        v_.reciprocal(rinv[0:T, v:v + 1], rsum[0:T, v:v + 1]).then_inc(own.sem, own.one())
                        dve.wait_ge(own.sem, own.total())
                        v_.tensor_scalar(rinv[0:T, v:v + 1], rinv[0:T, v:v + 1], tanh_a, None, ALU.mult).then_inc(own.sem, own.one())
                        dve.wait_ge(own.sem, own.total())
                        dve.wait_ge(a.xpart_read.sem, a.xpart_read.at(b + 1))
                        v_.scalar_tensor_tensor(tile_of(xs, b), ps[0:T, 7, 0:D], rinv[0:T, v:v + 1],
                                                tile_of(xs, b), ALU.mult, ALU.add).then_inc(a.final_read.sem, 1)

                def tail(i, u):
                    b = i + 2
                    if l.n == 1 and has(b):
                        dve.wait_ge(a.xpart_done.sem, a.xpart_done.at(b + 1))
                        dve.wait_ge(a.xb_ready.sem, a.xb_ready.at(b + 1))
                        v_.scalar_tensor_tensor(tile_of(xs, b), ps[0:T, 7, D:2 * D], tanh_a, tile_of(xs, b), ALU.mult,
                                                ALU.add).then_inc(a.xpart_read.sem, 1)
                loop(dve, body, own, (26, 17)[l.n])

            def dispatch(l):
                a, m = A[l.n], B[l.n]
                own = Steps(m.own_dve)
                dve.wait_ge(m.iota_done.sem, m.iota_done.at(4))
                attention_left(dve, l)

                def be(v):
                    return v[0:T].rearrange("p b e -> p (b e)")

                def over_e(v):
                    return v.unsqueeze(2).to_broadcast([T, NB, E])

                def over_b(v):
                    return v.unsqueeze(1).to_broadcast([T, NB, E])

                v_.tensor_copy(m.rev[0:T], m.rev_i[0:T]).then_inc(own.sem, own.one())
                (v_.tensor_tensor(m.sel[0:T], logits[0:T], over_b(rb_bc[0:T]), ALU.add) if l.n else
                v_.tensor_copy(m.sel[0:T], logits[0:T])).then_inc(own.sem, own.one())
                dve.wait_ge(own.sem, own.total())
                for k in range(l.K):
                    oh = (m.oh0, m.oh1)[k]
                    v_.tensor_reduce(m.mx[0:T], m.sel[0:T], AX_X, ALU.max).then_inc(own.sem, own.one())
                    dve.wait_ge(own.sem, own.total())
                    v_.tensor_tensor(m.eq[0:T], m.sel[0:T], over_e(m.mx[0:T]), ALU.is_equal).then_inc(own.sem, own.one())
                    dve.wait_ge(own.sem, own.total())
                    v_.tensor_tensor(m.eq[0:T], m.eq[0:T], over_b(m.rev[0:T]), ALU.mult).then_inc(own.sem, own.one())
                    dve.wait_ge(own.sem, own.total())
                    v_.tensor_reduce(m.mx[0:T], m.eq[0:T], AX_X, ALU.max).then_inc(own.sem, own.one())
                    dve.wait_ge(own.sem, own.total())
                    v_.tensor_tensor(oh[0:T], m.eq[0:T], over_e(m.mx[0:T]), ALU.is_equal).then_inc(own.sem, own.one())
                    dve.wait_ge(own.sem, own.total())
                    if k + 1 < l.K:
                        v_.scalar_tensor_tensor(be(m.sel), be(oh), -BIG, be(m.sel), ALU.mult, ALU.add).then_inc(own.sem, own.one())
                    v_.tensor_tensor(m.acc[0:T], oh[0:T], logits[0:T], ALU.mult).then_inc(own.sem, own.one())
                    dve.wait_ge(own.sem, own.total())
                    v_.tensor_reduce(m.lk[0:T, k], m.acc[0:T], AX_X, ALU.add).then_inc(own.sem, own.one())
                    dve.wait_ge(own.sem, own.total())
                if l.K == 1:
                    v_.tensor_copy(m.both[0:T], m.oh0[0:T]).then_inc(m.disp_sel.sem, 1)
                    v_.tensor_copy(m.lw[0:T, 0], m.lk[0:T, 0]).then_inc(m.lk_ready.sem, 1)
                else:
                    v_.tensor_tensor(m.both[0:T], m.oh0[0:T], m.oh1[0:T], ALU.add).then_inc(m.disp_sel.sem, 1)
                    v_.tensor_tensor(m.lw[0:T, 0], m.lk[0:T, 0], m.lk[0:T, 1], ALU.subtract)
                    v_.tensor_tensor(m.lw[0:T, 1], m.lk[0:T, 1], m.lk[0:T, 0], ALU.subtract).then_inc(m.lk_ready.sem, 1)
                v_.tensor_copy(m.thr[0:T, 0:14], m.thr_i[0:T]).then_inc(own.sem, own.one())
                v_.tensor_copy(m.tile_no[0:T], m.tile_i[0:T]).then_inc(own.sem, own.one())
                dve.wait_ge(m.disp_pe.sem, m.disp_pe.at(1))
                tot = ps[0:T, 5, 0:NB * E].rearrange("p (b e) -> p b e", b=NB)
                v_.tensor_copy(m.acc[0:T], tot).then_inc(own.sem, own.one())
                dve.wait_ge(own.sem, own.total())
                src, dst = m.acc, m.acc2
                d = 1
                while d < NB:
                    v_.tensor_copy(dst[0:T, 0:d], src[0:T, 0:d]).then_inc(own.sem, own.one())
                    v_.tensor_tensor(dst[0:T, d:NB], src[0:T, d:NB], src[0:T, 0:NB - d], ALU.add).then_inc(own.sem, own.one())
                    dve.wait_ge(own.sem, own.total())
                    src, dst = dst, src
                    d *= 2
                count = src[0:T, NB - 1].unsqueeze(2).to_broadcast([T, E, 14])
                v_.tensor_tensor(m.cmp[0:T], count, m.thr[0:T].unsqueeze(1).to_broadcast([T, E, 14]),
                                 ALU.is_gt).then_inc(own.sem, own.one())
                dve.wait_ge(own.sem, own.total())
                v_.tensor_reduce(m.ntile[0:T], m.cmp[0:T], AX_X, ALU.add).then_inc(own.sem, own.one())
                dve.wait_ge(own.sem, own.total())
                v_.tensor_copy(m.cum[0:T], m.ntile[0:T]).then_inc(own.sem, own.one())
                dve.wait_ge(own.sem, own.total())
                c1, c2 = m.cum, m.cum2
                d = 1
                while d < E:
                    v_.tensor_copy(c2[0:T, 0:d], c1[0:T, 0:d]).then_inc(own.sem, own.one())
                    v_.tensor_tensor(c2[0:T, d:E], c1[0:T, d:E], c1[0:T, 0:E - d], ALU.add).then_inc(own.sem, own.one())
                    dve.wait_ge(own.sem, own.total())
                    c1, c2 = c2, c1
                    d *= 2
                v_.tensor_tensor(c2[0:T], c1[0:T], m.ntile[0:T], ALU.subtract).then_inc(own.sem, own.one())
                dve.wait_ge(own.sem, own.total())
                v_.tensor_scalar(c2[0:T], c2[0:T], float(P), None, ALU.mult).then_inc(own.sem, own.one())
                dve.wait_ge(own.sem, own.total())
                v_.tensor_tensor(dst[0:T], src[0:T], tot, ALU.subtract).then_inc(own.sem, own.one())
                dve.wait_ge(own.sem, own.total())
                v_.tensor_tensor(src[0:T], dst[0:T], ps[0:T, 4, 0:NB * E].rearrange("p (b e) -> p b e", b=NB),
                                 ALU.add).then_inc(own.sem, own.one())
                dve.wait_ge(own.sem, own.total())
                v_.tensor_tensor(dst[0:T], src[0:T], over_b(c2[0:T]), ALU.add).then_inc(own.sem, own.one())
                dve.wait_ge(own.sem, own.total())
                for k in range(l.K):
                    oh = (m.oh0, m.oh1)[k]
                    v_.tensor_tensor(m.eq[0:T], oh[0:T], dst[0:T], ALU.mult).then_inc(own.sem, own.one())
                    dve.wait_ge(own.sem, own.total())
                    v_.tensor_reduce(m.posf[0:T], m.eq[0:T], AX_X, ALU.add).then_inc(own.sem, own.one())
                    dve.wait_ge(own.sem, own.total())
                    v_.tensor_copy(pos_i[0:T, 0:NB * l.K].rearrange("p (b k) -> p b k", k=l.K)[:, :, k],
                                   m.posf[0:T]).then_inc(own.sem, own.one())
                    dve.wait_ge(own.sem, own.total())
                v_.tensor_tensor(m.tcmp[0:T], m.tile_no[0:T].unsqueeze(2).to_broadcast([T, l.tiles, E]),
                                 c1[0:T].unsqueeze(1).to_broadcast([T, l.tiles, E]), ALU.is_ge).then_inc(own.sem, own.one())
                dve.wait_ge(own.sem, own.total())
                v_.tensor_reduce(m.tile_no[0:T], m.tcmp[0:T], AX_X, ALU.add).then_inc(own.sem, own.one())
                dve.wait_ge(own.sem, own.total())
                v_.tensor_scalar(tile_expert[0:T, 0:l.tiles], m.tile_no[0:T], float(E - 1), None, ALU.min
                                 ).then_inc(m.disp_ready.sem, 1)

            def shared(l):
                m = B[l.n]
                tanh_f = tanh_g[0:T, 2 + l.n:3 + l.n]

                def group(g):
                    for c in range(l.FC):
                        n = g * l.FC + c
                        r = l.rows(c)
                        dve.wait_ge(m.silu_ready.sem, m.silu_ready.at(n + 1))
                        dve.wait_ge(m.up_done.sem, m.up_done.at(n + 1))
                        if c == 0:
                            if due(g):
                                dve.wait_ge(m.shared_done.sem, m.shared_done.at(g))
                        v_.tensor_tensor(m.midT_s[0:r, c], m.silu_s[0:r, c % 2], ps[0:r, 2 + c % 2, 0:GN], ALU.mult
                                         ).then_inc(m.mid_ready.sem, 1)
                    dve.wait_ge(m.shared_done.sem, m.shared_done.at(g + 1))
                    for j in range(GT):
                        xt = tile_of(xs, g * GT + j)
                        v_.scalar_tensor_tensor(xt, ps[0:T, 4 + j, 0:D], tanh_f, xt, ALU.mult, ALU.add
                                                ).then_inc(m.shared_read.sem, 1)
                group(0)
                with dve.Fori(1, NB // GT) as g:
                    group(g)

            def routed(l):
                m = B[l.n]

                def out(i, u):
                    if has(i, l.tiles):
                        u = u % 4
                        dve.wait_ge(m.rout_done.sem, m.rout_done.at(i + 1))
                        if not isinstance(i, int) or i >= 2:
                            yscat = (m.yscat0, m.yscat1, m.yscat2, m.yscat3)[(u - 2) % 4]
                            j = i - 2
                            dve.wait_ge(yscat.sem, yscat.at(16 * (j // 4 + 1) if isinstance(j, int) else 4 * (j - (u - 2) % 4) + 16))
                        v_.tensor_copy(m.yo[:, u % 2], ps[:, 7, 0:D]).then_inc(m.y_ready.sem, 1)

                def body(i, u):
                    if has(i, l.tiles):
                        for h in range(l.halves):
                            dve.wait_ge(m.rsilu_ready.sem, m.rsilu_ready.at(i * l.halves + h + 1))
                            dve.wait_ge(m.rup_done.sem, m.rup_done.at(i * l.halves + h + 1))
                            if h == 0:
                                if due(i):
                                    dve.wait_ge(m.mturn_done.sem, m.mturn_done.at(i))
                            v_.tensor_tensor(m.mid[:, h * l.FH:(h + 1) * l.FH], m.silu[:, h * l.FH:(h + 1) * l.FH],
                                             ps[:, 2 + h, 0:l.FH], ALU.mult).then_inc(m.rmid_ready.sem, 1)
                    out(i - 1, u - 1)
                    if has(i, l.tiles) and l.FC > 4:
                        dve.wait_ge(m.mturn_done.sem, m.mturn_done.at(i + 1))
                        if due(i):
                            dve.wait_ge(m.rout_done.sem, m.rout_done.at(i))
                        v_.tensor_copy(m.midT[:, 4], ps[:, 6, 0:P])
                        r = l.rows(5)
                        v_.tensor_copy(m.midT[0:r, 5], ps[0:r, 6, P:2 * P]).then_inc(m.midT_d.sem, 1)
                run_tiles(dve, l, body, 0)

            attention(LAYERS[0])
            dispatch(LAYERS[0])
            shared(LAYERS[0])
            routed(LAYERS[0])
            attention(LAYERS[1])
            dispatch(LAYERS[1])
            shared(LAYERS[1])
            routed(LAYERS[1])
            l, m = LAYERS[1], B[1]
            own = Steps(Count(dve_last))
            dve.wait_ge(m.gate_ready.sem, m.gate_ready.at(1))
            v_.tensor_scalar(token_w[0:T], token_w[0:T], tanh_g[0:T, 3:4], None, ALU.mult).then_inc(own.sem, own.one())
            dve.wait_ge(own.sem, own.total())
            fin_in = (m.fin_in0, m.fin_in1, m.fin_in2, m.fin_in3)

            def add(j, u):
                dve.wait_ge(fin_in[u].sem, fin_in[u].at(16 * (j // 4 + 1) if isinstance(j, int) else 4 * (j - u) + 16))
                xt = tile_of(xs, j)
                tw = token_w[0:T, bass.ds(j, 1), :].rearrange("p a k -> p (a k)")
                v_.scalar_tensor_tensor(xt, m.fin[0:T, u, 0], tw[:, 0:1], xt, ALU.mult, ALU.add).then_inc(own.sem, own.one())
                dve.wait_ge(own.sem, own.total())
                v_.scalar_tensor_tensor(xt, m.fin[0:T, u, 1], tw[:, 1:2], xt, ALU.mult, ALU.add
                                        ).then_inc(m.fin_ready.sem, 1)
            n = own.n
            with dve.Fori(0, NB - 3, 4) as r:
                own.base = r
                for u in range(4):
                    add(r + u, u)

        @block.gpsimd
        def _(pool):
            g_ = nc.gpsimd
            g_.memset(ident, 0.0).then_inc(ident_ready, 1)
            g_.memset(ones, 1.0).then_inc(ident_ready, 1)
            pool.wait_ge(ident_ready, 2)
            g_.affine_select(out=ident, in_=ident, compare_op=ALU.not_equal, fill=1.0, base=0, pattern=[[-1, P]],
                             channel_multiplier=1).then_inc(ident_ready, 1)
            g_.affine_select(out=before, in_=ones[:, 0:T], compare_op=ALU.is_gt, fill=0.0, base=0, pattern=[[1, T]],
                             channel_multiplier=-1).then_inc(ident_ready, 1)
            g_.memset(zero, 0.0).then_inc(zeros_ready, 1)
            pool.wait_ge(zeros_ready, 1)
            for l in LAYERS:
                g_.iota(pad_rows[l.n], pattern=[[P, l.tiles]], base=NB * T * l.K, channel_multiplier=1
                        ).then_inc(pads_ready, 1)
                pool.wait_ge(pads_ready, l.n + 1)

            def zero_rows(l):
                rows = xg[l.n].rearrange("(j p) c -> p j c", p=P)
                pool.dma_start(rows[:, :, 0:D], zero.unsqueeze(1).to_broadcast([P, l.tiles, D])
                               ).then_inc(dispatch_zeroed, 16)
                pool.dma_start(rows[:, :, D:ROW].bitcast(I32), pad_rows[l.n].unsqueeze(2),
                               allow_slow_non_contiguous=True).then_inc(dispatch_zeroed, 16)

            def attention(l):
                a = A[l.n]

                def body(i, u):
                    if l.n == 0 and isinstance(i, int) and i in (2, 3):
                        zero_rows(LAYERS[i - 2])
                    b = i + 3
                    if has(b):
                        offset = a.bp if l.n == 0 else a.b2
                        if l.n == 0 and isinstance(b, int) and b == 0:
                            pool.wait_ge(a.setup_dve.sem, a.setup_dve.at(2))
                        pool.wait_ge(a.xt_ready.sem, a.xt_ready.at(b + 1))
                        g_.tensor_tensor(tile_of(xs, b), tile_of(xs, b), offset[0:T], ALU.add
                                         ).then_inc(a.xb_ready.sem, 1)
                    b = i - 4
                    if has(b):
                        pool.wait_ge(a.xnTb_ready.sem, a.xnTb_ready.at(b + 1))
                        g_.tensor_copy(xnT[:, :, bass.ds(b * T, T)], a.xnTb[:, u % 2]).then_inc(a.xnT_ready.sem, 1)
                loop(pool, body, Steps(None), 0)

            def dispatch(l):
                a, m = A[l.n], B[l.n]
                own = Steps(m.own_pool)
                pool.wait_ge(dispatch_zeroed, 64)
                attention_left(pool, l)
                g_.iota(m.rev_i, pattern=[[-1, E]], base=E, channel_multiplier=0).then_inc(m.iota_done.sem, 1)
                g_.iota(m.thr_i, pattern=[[P, 14]], base=0, channel_multiplier=0).then_inc(m.iota_done.sem, 1)
                g_.iota(m.tile_i, pattern=[[1, l.tiles]], base=0, channel_multiplier=0).then_inc(m.iota_done.sem, 1)
                g_.iota(m.dest, pattern=[[T * l.K, NB], [1, l.K]], base=0, channel_multiplier=l.K
                        ).then_inc(m.iota_done.sem, 1)
                pool.wait_ge(m.disp_ready.sem, m.disp_ready.at(1))
                pool.wait_ge(m.gate_ready.sem, m.gate_ready.at(1))
                pool.wait_ge(m.iota_done.sem, m.iota_done.at(4))
                rows_in = (m.rows_in0, m.rows_in1, m.rows_in2, m.rows_in3)
                scat = (m.scat0, m.scat1, m.scat2, m.scat3)
                per = 4 // l.K

                def four(j):
                    for u in range(4):
                        t, k = j + u // l.K, u % l.K
                        pool.wait_ge(rows_in[u].sem, rows_in[u].at(16 * (j * l.K // 4 + 1) if isinstance(j, int) else j * (4 * l.K) + 16))
                        row = m.rows[0:T, u]
                        q = t * l.K + k
                        g_.tensor_copy(row[:, D:ROW].bitcast(I32), m.dest[0:T, bass.ds(q, 1)]).then_inc(own.sem, own.one())
                        g_.tensor_copy(pos_ring[0:T, u:u + 1], pos_i[0:T, bass.ds(q, 1)]).then_inc(own.sem, own.one())
                        if l.n == 0:
                            gate = token_w[0:T, bass.ds(t, 1), :].rearrange("p a k -> p (a k)")[:, 0:1]
                            g_.tensor_copy(gate_ring[0:T, u:u + 1], gate).then_inc(own.sem, own.one())
                            pool.wait_ge(own.sem, own.total())
                            pool.nop(nofuse=True)
                            g_.tensor_scalar(row[:, 0:D], row[:, 0:D], gate_ring[0:T, u:u + 1], None,
                                             ALU.mult).then_inc(own.sem, own.one())
                        pool.wait_ge(own.sem, own.total())
                        pool.nop(nofuse=True)
                        g_.indirect_dma_start(out=xg[l.n][:, :],
                                              out_offset=bass.IndirectOffsetOnAxis(ap=pos_ring[0:T, u:u + 1], axis=0),
                                              in_=row, in_offset=None).then_inc(scat[u].sem, 16)
                four(0)
                n = own.n
                with pool.Fori(per, NB - per + 1, per) as r:
                    own.base = (r - per) * (n // per)
                    four(r)

            def routed(l):
                m = B[l.n]
                yscat = (m.yscat0, m.yscat1, m.yscat2, m.yscat3)

                def body(i, u):
                    if has(i, l.tiles):
                        pool.wait_ge(m.y_ready.sem, m.y_ready.at(i + 1))
                        pool.nop(nofuse=True)
                        g_.indirect_dma_start(out=yg[l.n][:, :],
                                              out_offset=bass.IndirectOffsetOnAxis(
                                                  ap=m.g[:, u, D:ROW].bitcast(I32), axis=0),
                                              in_=m.yo[:, u % 2], in_offset=None).then_inc(yscat[u].sem, 16)
                run_tiles(pool, l, body, 0)

            for l in LAYERS:
                if l.n == 1:
                    a = A[1]
                    pool.wait_ge(B[0].shared_done.sem, B[0].shared_done.at(NB // GT))
                    pool.wait_ge(a.consts_in.sem, a.consts_in.at(32))
                    pool.dma_start(a.b2, w2_b.partition_broadcast(P)).then_inc(a.b2_in.sem, 16)
                    pool.wait_ge(a.b2_in.sem, a.b2_in.at(16))
                    g_.tensor_scalar(a.b2, a.b2, tanh_g[:, 1:2], None, ALU.mult).then_inc(a.setup_dve.sem, 1)
                    pool.wait_ge(a.setup_dve.sem, a.setup_dve.at(1))
                attention(l)
                if l.n == 0:
                    attention_left(pool, l)
                    load_shared(pool, l)
                dispatch(l)
                routed(l)


_INS = ['x', 'ctx_1024', 'mask_BxS2_ik0', 'g_xattn', 'g_ffn', 'L0_xattn_ln_t_g', 'L0_xattn_ln_t_b',
        'L0_xattn_ln_a_g', 'L0_xattn_ln_a_b', 'L0_xattn_Wq', 'L0_xattn_bq', 'L0_xattn_Wk', 'L0_xattn_bk',
        'L0_xattn_Wv', 'L0_xattn_bv', 'L0_xattn_ln_p_g', 'L0_xattn_ln_p_b', 'L0_ffn_router_DE', 'L0_ffn_w1_eDF',
        'L0_ffn_w3_eDF', 'L0_ffn_w2_eFD', 'L0_ffn_ws1_DF', 'L0_ffn_ws3_DF', 'L0_ffn_ws2_FD', 'L1_xattn_w1_w',
        'L1_xattn_w1_b', 'L1_xattn_w2_w', 'L1_xattn_w2_b', 'L1_ffn_Wr', 'L1_ffn_rb', 'L1_ffn_W1', 'L1_ffn_W2',
        'L1_ffn_W3', 'L1_ffn_Ws1', 'L1_ffn_Ws2', 'L1_ffn_Ws3']
_OUTS = [((NB, T, D), 'float32')]


def kernel(**inputs):
    import numpy as _np
    import concourse.bacc as _bacc
    from concourse import mybir as _mybir
    from concourse.bass_utils import run_bass_kernel_spmd as _run

    nc = _bacc.Bacc("TRN2", target_bir_lowering=False, num_devices=1)
    arrays, args = {}, []
    for name in _INS:
        a = _np.ascontiguousarray(inputs[name])
        arrays[f"in_{name}_dram"] = a
        args.append(nc.dram_tensor(f"in_{name}_dram", a.shape, _mybir.dt.from_np(a.dtype), kind="ExternalInput").ap())
    for i, (shape, dtype) in enumerate(_OUTS):
        dt = _mybir.dt.from_np(_np.dtype(dtype))
        args.append(nc.dram_tensor(f"out_{i}_dram", shape, dt, kind="ExternalOutput").ap())
    flamingo(nc, *args)
    r = _run(nc, [arrays], core_ids=[0])
    got = tuple(r.results[0][f"out_{i}_dram"] for i in range(len(_OUTS)))
    return got[0]
```

```python
from contextlib import ExitStack

import concourse.bass as bass
from concourse import mybir

F32 = mybir.dt.float32
I32 = mybir.dt.int32
ACT = mybir.ActivationFunctionType
ALU = mybir.AluOpType
AX_X = mybir.AxisListType.X

P = 128
NB, T, S, D = 16, 112, 375, 256
KD = D // P
SJ = 3
SR = S // SJ
E = 8
SCALE = D ** -0.5
EPS = 1e-5
BIG = 3.0e38
ROW = D + 1
GT = 4
GN = GT * T
FIRST, LOOPED, LAST = -4, 8, NB + 5


class Layer:
    def __init__(self, n, F, K):
        self.n, self.F, self.K = n, F, K
        self.FC = -(-F // P)
        self.tiles = NB * T * K // P + E - 1
        self.halves = -(-F // 512)
        self.FH = F // self.halves
        self.loop_hi = 4 + (self.tiles - 4) // 4 * 4

    def rows(self, c):
        return min(P, self.F - c * P)


LAYERS = (Layer(0, 704, 1), Layer(1, 512, 2))


class Arena:

    def __init__(self, *parts):
        self.parts = [[t, a, b] for t, a, b in parts]

    def take(self, *shape):
        n = 1
        for s in shape:
            n *= s
        for part in self.parts:
            t, a, b = part
            if a + n <= b:
                part[1] = a + n
                v = t[:, a:a + n]
                if len(shape) == 2:
                    v = v.rearrange("p (a b) -> p a b", a=shape[0])
                if len(shape) == 3:
                    v = v.rearrange("p (a b c) -> p a b c", a=shape[0], b=shape[1])
                if len(shape) == 4:
                    v = v.rearrange("p (a b c d) -> p a b c d", a=shape[0], b=shape[1], c=shape[2])
                return v
        raise ValueError("arena is full")


class Count:

    def __init__(self, sem, start=0):
        self.sem, self.start = sem, start

    def at(self, value):
        return value + self.start if self.start else value


class Steps:

    def __init__(self, count):
        self.sem, self.n, self.base = count.sem if count else None, 0, 0

    def one(self):
        self.n += 1
        return 1

    def total(self):
        return self.n if isinstance(self.base, int) else self.base + self.n


def due(value):
    return not isinstance(value, int) or value > 0


def upto(value, most):
    return min(value, most) if isinstance(value, int) else value


def has(b, n=NB):
    return not isinstance(b, int) or 0 <= b < n


def tile_of(t, b):
    return t[0:T, bass.ds(b, 1), :].rearrange("p a d -> p (a d)")


def flamingo(nc, x, ctx, mask, g_xattn, g_ffn, ln_t_g, ln_t_b, ln_a_g, ln_a_b, Wq, bq, Wk, bk, Wv, bv, ln_p_g,
             ln_p_b, router0, w1_0, w3_0, w2_0, ws1_0, ws3_0, ws2_0, w1_w, w1_b, w2_w, w2_b, router1, rb, w1_1,
             w2_1, w3_1, ws1_1, ws2_1, ws3_1, out):
    expert_w = ((w1_0, w3_0, w2_0), (w3_1, w1_1, w2_1))
    shared_w = ((ws1_0, ws3_0, ws2_0), (ws3_1, ws1_1, ws2_1))
    router_w = (router0, router1)

    stack = ExitStack()
    with stack:
        def sb(name, cols, dt=F32):
            return stack.enter_context(nc.sbuf_tensor(name, [P, cols], dt))

        def sem(name):
            return stack.enter_context(nc.semaphore(name))

        xg = [nc.dram_tensor(f"dispatched{l.n}", [l.tiles * P, ROW], F32, kind="Internal").ap() for l in LAYERS]
        yg = [nc.dram_tensor(f"returned{l.n}", [NB * T * l.K + l.tiles * P, D], F32, kind="Internal").ap()
              for l in LAYERS]
        mask_rows = nc.dram_tensor("mask_rows", [NB, S], F32, kind="Internal").ap()
        xn_rows = [nc.dram_tensor(f"xn_rows{l.n}", [NB, T, D], F32, kind="Internal").ap() for l in LAYERS]

        WCOLS = LAYERS[0].F * 4 * E + LAYERS[0].FC * D * E
        W = sb("expert_weights", WCOLS)
        xs_t = sb("x_stream", NB * D)
        xnT_t = sb("xn_turned", KD * NB * T)
        R = sb("work", 7936)
        KT = sb("layer_constants", 1792)
        fixed = sb("fixed", 800)
        ints = sb("ints", 160, I32)
        ps = stack.enter_context(nc.psum_tensor("ps", [P, 8, 512], F32))

        xs = xs_t[:, :].rearrange("p (b d) -> p b d", b=NB)
        xnT = xnT_t[:, :].rearrange("p (k n) -> p k n", k=KD)

        def expert_views(l):
            n13 = E * 4 * l.F
            gu = W[:, 0:n13].rearrange("p (e m k f) -> p e m k f", e=E, m=2, k=KD)
            back = W[:, n13:n13 + E * l.FC * D].rearrange("p (e c d) -> p e c d", e=E, c=l.FC)
            return gu, back

        wgu, wback = zip(*[expert_views(l) for l in LAYERS])
        l0, l1 = LAYERS
        used1 = E * 4 * l1.F + E * l1.FC * D
        spare = (((W, (E - 1) * 4 * l0.F, E * 4 * l0.F), (W, WCOLS - l0.FC * D, WCOLS)), ((W, used1, WCOLS),))

        f = Arena((fixed, 0, 800))
        ident = f.take(P)
        ones = f.take(P)
        before = f.take(T)
        gt_c, bt_c, ga_c, ba_c = f.take(KD), f.take(KD), f.take(KD), f.take(KD)
        bq_c, bk_c, b1_c = f.take(KD), f.take(KD), f.take(KD)
        wqbk, qbias, c0 = f.take(KD), f.take(KD), f.take(1)
        bqbk = f.take(KD)
        gates_raw, tanh_g = f.take(4), f.take(4)
        route_w = [f.take(KD, E), f.take(KD, E)]
        rb_bc = f.take(E)
        logits = f.take(NB, E)
        mv = f.take(2, 6, 2)
        uvar, rstd, nmr = f.take(6), f.take(2, 6), f.take(2, 3)
        guess, newt = f.take(6), f.take(6)
        bn = f.take(6, 6)
        smax, nbias, rsum, rinv, cq = f.take(1), f.take(4), f.take(4), f.take(4), f.take(4)
        token_w = f.take(NB, 2)
        gate_ring = f.take(8)
        pos_i = ints[:, 0:NB * 2]
        tile_expert = ints[:, 32:32 + 40]
        pos_ring = ints[:, 80:88]
        pad_rows = (ints[:, 88:88 + l0.tiles], ints[:, 112:112 + l1.tiles])

        kept = {}

        def both_layers(name, l, total):
            if name not in kept:
                kept[name] = sem(name)
            return Count(kept[name], total * l.n)

        def one_layer(kind, name, l):
            return Count(sem(f"{kind}{l.n}_{name}"))

        class Attn:
            pass

        class Ffn:
            pass

        A, B = [], []
        for l in LAYERS:
            a = Attn()
            ar = Arena((R, 0, 7936), *spare[l.n])
            a.kv = ar.take(4, SJ, D)
            if l.n == 0:
                a.raw = ar.take(4, SJ, D)
            else:
                a.y = ar.take(2, D)
            a.kT = ar.take(2, KD, S)
            if l.n == 0:
                ar = Arena(*spare[0])
                a.mask_add = ar.take(2, S)
            a.probs = ar.take(S)
            a.pT = ar.take(SJ, T)
            a.crossT = ar.take(KD, T)
            a.tT = ar.take(KD, T)
            a.qT = ar.take(2, KD, T)
            a.xnTb = ar.take(2, KD, T)
            a.xt = ar.take(2, D)
            a.cross = ar.take(2, D)
            a.xn = ar.take(2, D)
            k = Arena((KT, 0, 1792))
            if l.n == 0:
                a.Aqk, a.Wv, a.gp, a.bp, a.vbias = k.take(KD, D), k.take(KD, D), k.take(D), k.take(D), k.take(D)
                tmp = Arena((xnT_t, 0, KD * NB * T))
                a.Wq_r, a.Wk_r, a.WqT, a.WkT = (tmp.take(KD, D) for _ in range(4))
                a.bvec = tmp.take(KD, P)
                a.mask_i = tmp.take(S).bitcast(I32)
                a.mask_f = tmp.take(S)
                zero = xnT_t[:, KD * NB * T - D:KD * NB * T]
            else:
                a.w1T, a.w2T, a.b2 = k.take(KD, D), k.take(2 * KD, D), k.take(D)
                tmp = Arena((xnT_t, 0, KD * NB * T))
                a.w1_r, a.w2_r = tmp.take(KD, D), tmp.take(KD, 2 * D)
            a.consts_in = one_layer("a", "consts_in", l)
            a.setup_pe = one_layer("a", "setup_pe", l)
            a.setup_act = one_layer("a", "setup_act", l)
            a.setup_dve = one_layer("a", "setup_dve", l)
            a.dve_own = one_layer("a", "dve_own", l)
            a.dve_chain = one_layer("a", "dve_chain", l)
            a.act_own = one_layer("a", "act_own", l)
            if l.n == 0:
                a.x_done = one_layer("a", "x_done", l)
                a.mask_all = one_layer("a", "mask_all", l)
                a.mask_sum = one_layer("a", "mask_sum", l)
                a.mask_stored = one_layer("a", "mask_stored", l)
            else:
                a.y_in0 = one_layer("a", "y_in0", l)
                a.y_in1 = one_layer("a", "y_in1", l)
                a.xpart_done = one_layer("a", "xpart_done", l)
                a.xpart_read = one_layer("a", "xpart_read", l)
                a.x2_done = one_layer("a", "x2_done", l)
                a.b2_in = one_layer("a", "b2_in", l)
            a.normed = both_layers("a_normed", l, NB)
            a.xt_ready = both_layers("a_xt_ready", l, NB)
            a.xb_ready = both_layers("a_xb_ready", l, NB)
            a.turned = both_layers("a_turned", l, NB)
            a.tT_ready = both_layers("a_tT_ready", l, NB)
            a.kT_ready = both_layers("a_kT_ready", l, NB)
            a.q_done = both_layers("a_q_done", l, NB)
            a.q_ready = both_layers("a_q_ready", l, NB)
            a.scores_done = both_layers("a_scores_done", l, NB)
            a.max_ready = both_layers("a_max_ready", l, NB)
            a.probs_ready = both_layers("a_probs_ready", l, NB)
            a.pT_done = both_layers("a_pT_done", l, NB)
            a.pT_ready = both_layers("a_pT_ready", l, NB)
            a.cross_done = both_layers("a_cross_done", l, NB)
            a.crossT_ready = both_layers("a_crossT_ready", l, NB)
            a.final_done = both_layers("a_final_done", l, NB)
            a.final_read = both_layers("a_final_read", l, NB)
            a.xn_centred = both_layers("a_xn_centred", l, NB)
            a.xn_ready = both_layers("a_xn_ready", l, NB)
            a.xnturn_done = both_layers("a_xnturn_done", l, NB)
            a.xnTb_ready = both_layers("a_xnTb_ready", l, NB)
            a.router_done = both_layers("a_router_done", l, NB)
            a.logits_ready = both_layers("a_logits_ready", l, NB)
            a.xnT_ready = both_layers("a_xnT_ready", l, NB)
            a.rstd_ready = both_layers("a_rstd_ready", l, NB + 7)
            a.mask_in0 = both_layers("a_mask_in0", l, 8 * NB)
            a.mask_in1 = both_layers("a_mask_in1", l, 8 * NB)
            a.raw_in0 = both_layers("a_raw_in0", l, 4 * NB)
            a.raw_in1 = both_layers("a_raw_in1", l, 4 * NB)
            a.raw_in2 = both_layers("a_raw_in2", l, 4 * NB)
            a.raw_in3 = both_layers("a_raw_in3", l, 4 * NB)
            a.rows_out0 = both_layers("a_rows_out0", l, 16 * NB // 2)
            a.rows_out1 = both_layers("a_rows_out1", l, 16 * NB // 2)
            A.append(a)

            m = Ffn()
            if l.n == 0:
                m.midT_s = Arena((R, 0, 3072)).take(l.FC, GN)
                m.ws_gu = Arena((R, 3072, 6144)).take(2, KD, l.F)
                m.ws_back = Arena((R, 6144, 7936)).take(l.FC, D)
                m.silu_s = Arena((KT, 0, 1024)).take(2, GN)
            else:
                far = Arena((W, used1 + 1024, WCOLS))
                m.ws_gu = far.take(2, KD, l.F)
                m.ws_back = far.take(l.FC, D)
                m.midT_s = far.take(l.FC, GN)
                m.silu_s = far.take(2, GN)
                m.fin = far.take(4, 2, D)
            sar = Arena(*spare[0]) if l.n == 0 else Arena((R, 0, 7936))
            m.rows = sar.take(8, ROW)
            m.sel, m.eq, m.oh0, m.oh1, m.both, m.acc, m.acc2 = (sar.take(NB, E) for _ in range(7))
            m.tot, m.rank = sar.take(NB, E), sar.take(NB, E)
            m.mx = sar.take(NB)
            m.lk, m.lw = sar.take(2, NB), sar.take(2, NB)
            m.rev = sar.take(E)
            m.thr = sar.take(14)
            m.cmp = sar.take(E, 14)
            m.ntile, m.cum, m.cum2 = sar.take(E), sar.take(E), sar.take(E)
            m.posf = sar.take(NB)
            m.tile_no = sar.take(l.tiles)
            m.tcmp = sar.take(l.tiles, E)
            m.dest = sar.take(NB * l.K).bitcast(I32)
            m.rev_i, m.thr_i, m.tile_i = (sar.take(n).bitcast(I32) for n in (E, 14, l.tiles))
            rar = Arena((R, 0, 7936))
            if l.n == 1:
                rar.take(7936 // 2)
            m.g = rar.take(4, ROW)
            m.gT = rar.take(2, KD, P)
            m.silu = rar.take(l.F)
            m.mid = rar.take(l.F)
            m.midT = rar.take(l.FC, P)
            m.yo = Arena((R, 0, 3968)).take(2, D) if l.n == 1 else rar.take(2, D)
            m.weights_in = one_layer("f", "weights_in", l)
            m.shared_in = one_layer("f", "shared_in", l)
            m.iota_done = one_layer("f", "iota_done", l)
            m.up_copied = one_layer("f", "up_copied", l)
            m.disp_sel = one_layer("f", "disp_sel", l)
            m.ranks_read = one_layer("f", "ranks_read", l)
            m.disp_pe = one_layer("f", "disp_pe", l)
            m.disp_ready = one_layer("f", "disp_ready", l)
            m.lk_ready = one_layer("f", "lk_ready", l)
            m.gate_ready = one_layer("f", "gate_ready", l)
            m.own_dve = one_layer("f", "own_dve", l)
            m.own_pool = one_layer("f", "own_pool", l)
            if l.n == 0:
                m.late_in = one_layer("f", "late_in", l)
                m.midT_d = one_layer("f", "midT_d", l)
            else:
                m.fin_in0 = one_layer("f", "fin_in0", l)
                m.fin_in1 = one_layer("f", "fin_in1", l)
                m.fin_in2 = one_layer("f", "fin_in2", l)
                m.fin_in3 = one_layer("f", "fin_in3", l)
                m.fin_ready = one_layer("f", "fin_ready", l)
                m.out_done = one_layer("f", "out_done", l)
            m.rows_in0 = both_layers("f_rows_in0", l, 16 * NB // 2)
            m.rows_in1 = both_layers("f_rows_in1", l, 16 * NB // 2)
            m.scat0 = both_layers("f_scat0", l, 16 * NB // 2)
            m.scat1 = both_layers("f_scat1", l, 16 * NB // 2)
            m.gate_done = both_layers("f_gate_done", l, NB // GT * l0.FC)
            m.up_done = both_layers("f_up_done", l, NB // GT * l0.FC)
            m.silu_ready = both_layers("f_silu_ready", l, NB // GT * l0.FC)
            m.mid_ready = both_layers("f_mid_ready", l, NB // GT * l0.FC)
            m.shared_done = both_layers("f_shared_done", l, NB // GT)
            m.shared_read = both_layers("f_shared_read", l, NB)
            m.gturn_done = both_layers("f_gturn_done", l, l0.tiles)
            m.gT_ready = both_layers("f_gT_ready", l, l0.tiles)
            m.mturn_done = both_layers("f_mturn_done", l, l0.tiles)
            m.midT_a = both_layers("f_midT_a", l, l0.tiles)
            m.rout_done = both_layers("f_rout_done", l, l0.tiles)
            m.y_ready = both_layers("f_y_ready", l, l0.tiles)
            m.rgate_done = both_layers("f_rgate_done", l, l0.tiles * l0.halves)
            m.rup_done = both_layers("f_rup_done", l, l0.tiles * l0.halves)
            m.rsilu_ready = both_layers("f_rsilu_ready", l, l0.tiles * l0.halves)
            m.rmid_ready = both_layers("f_rmid_ready", l, l0.tiles * l0.halves)
            m.g_in0 = both_layers("f_g_in0", l, 16 * len(range(0, l0.tiles, 4)))
            m.yscat0 = both_layers("f_yscat0", l, 16 * len(range(0, l0.tiles, 4)))
            m.g_in1 = both_layers("f_g_in1", l, 16 * len(range(1, l0.tiles, 4)))
            m.yscat1 = both_layers("f_yscat1", l, 16 * len(range(1, l0.tiles, 4)))
            m.g_in2 = both_layers("f_g_in2", l, 16 * len(range(2, l0.tiles, 4)))
            m.yscat2 = both_layers("f_yscat2", l, 16 * len(range(2, l0.tiles, 4)))
            m.g_in3 = both_layers("f_g_in3", l, 16 * len(range(3, l0.tiles, 4)))
            m.yscat3 = both_layers("f_yscat3", l, 16 * len(range(3, l0.tiles, 4)))
            B.append(m)

        ident_ready = sem("ident_ready")
        x_in = [sem(f"x_in{i}") for i in range(4)]
        small_in = sem("small_in")
        tanh_ready = sem("tanh_ready")
        pads_ready = sem("pads_ready")
        dispatch_zeroed = [sem(f"dispatch_zeroed{l.n}") for l in LAYERS]
        zeros_ready = sem("zeros_ready")
        init_dve = sem("init_dve")
        bias_own = sem("bias_own")
        dve_last = sem("dve_last")

        def load_expert(eng, l, e4, s):
            g_w, u_w, b_w = expert_w[l.n]
            gu = W[:, 0:E * 4 * l.F].rearrange("p (q f) -> p q f", f=l.F)
            q = l.FC * D // 4
            back = W[:, E * 4 * l.F:E * (4 * l.F + l.FC * D)]
            for m_, w in ((0, g_w), (1, u_w)):
                src = w.rearrange("e d f -> (e d) f")[bass.ds(e4 * (D // 4), D), :].rearrange("(k p) f -> p k f", p=P)
                eng.dma_start(gu[:, bass.ds(e4 + 2 * m_, 2)], src).then_inc(s.sem, 16)
            full = l.F // P
            rows = b_w.rearrange("e f d -> (e f) d")
            eng.dma_start(back[:, bass.ds(e4 * q, full * D)].rearrange("p (c d) -> p c d", d=D),
                          rows[bass.ds(e4 * (l.F // 4), full * P), :].rearrange("(c p) d -> p c d", p=P)
                          ).then_inc(s.sem, 16)
            if full < l.FC:
                r = l.rows(full)
                eng.dma_start(back[0:r, bass.ds(e4 * q + full * D, D)], rows[bass.ds(e4 * (l.F // 4) + full * P, r), :]
                              ).then_inc(s.sem, 16)

        DMAS = [3 + (l.F % P > 0) for l in LAYERS]

        def attention_left(eng, l):
            a = A[l.n]
            eng.wait_ge(a.final_read.sem, a.final_read.at(NB))
            eng.wait_ge(a.logits_ready.sem, a.logits_ready.at(NB))
            eng.wait_ge(a.xnT_ready.sem, a.xnT_ready.at(NB))
            if l.n == 0:
                eng.wait_ge(a.x_done.sem, a.x_done.at(NB))
            eng.wait_ge(a.xb_ready.sem, a.xb_ready.at(NB))
            for s in (a.rows_out0, a.rows_out1):
                eng.wait_ge(s.sem, s.at(16 * NB // 2))

        def loop(eng, body, lo, *steps):
            for i in range(FIRST, lo):
                body(i, i % 4)
            before_loop = [c.n for c, per in steps]
            with eng.Fori(lo, lo + LOOPED - 3, 4) as r:
                for c, per in steps:
                    c.base = (r - lo) * per
                for u in range(4):
                    body(r + u, (lo + u) % 4)
            for (c, per), n in zip(steps, before_loop):
                assert c.n == n + 4 * per, (c.n - n, per)
                c.base, c.n = 0, n + LOOPED * per
            for i in range(lo + LOOPED, LAST):
                body(i, i % 4)

        def run_tiles(eng, l, body, first):
            for i in range(first, 4):
                body(i, i % 4)
            with eng.Fori(4, l.loop_hi - 3, 4) as r:
                for u in range(4):
                    body(r + u, u)
            for i in range(l.loop_hi, l.tiles + 1):
                body(i, i % 4)

        def load_shared(eng, l):
            a, m = A[l.n], B[l.n]
            g_w, u_w, b_w = shared_w[l.n]
            if l.n == 0:
                eng.wait_ge(a.normed.sem, a.normed.at(NB))
            for k_, w in ((0, g_w), (1, u_w)):
                eng.dma_start(m.ws_gu[:, k_], w.rearrange("(k p) f -> p k f", p=P)).then_inc(m.shared_in.sem, 16)
            if l.n == 0:
                eng.wait_ge(a.scores_done.sem, a.scores_done.at(NB))
            full = l.F // P
            eng.dma_start(m.ws_back[:, 0:full], b_w[0:full * P].rearrange("(c p) d -> p c d", p=P)
                          ).then_inc(m.shared_in.sem, 16)
            if full < l.FC:
                eng.dma_start(m.ws_back[0:l.rows(full), full], b_w[full * P:l.F]).then_inc(m.shared_in.sem, 16)

        SMALL = 17
        block = stack.enter_context(nc.Block())

        @block.sync
        def _(sp):
            a = A[0]
            sp.dma_start(xs[0:T, 0:4], x[0:4].rearrange("b t d -> t b d")).then_inc(x_in[0], 16)
            sp.dma_start(a.mask_i[0:NB], mask).then_inc(a.mask_all.sem, 16)

            def ctx_load(l, b, u):
                if not has(b):
                    return
                a = A[l.n]
                if l.n == 0:
                    if due(b - 3):
                        sp.wait_ge(a.normed.sem, a.normed.at(b - 3))
                    sp.dma_start(a.raw[0:SR, u % 4], ctx_tile(b)).then_inc(
                        (a.raw_in0, a.raw_in1, a.raw_in2, a.raw_in3)[u % 4].sem, 16)
                else:
                    if due(b - 3):
                        sp.wait_ge(a.cross_done.sem, a.cross_done.at(b - 3))
                    sp.dma_start(a.kv[0:SR, u % 4], ctx_tile(b)).then_inc(
                        (a.raw_in0, a.raw_in1, a.raw_in2, a.raw_in3)[u % 4].sem, 16)

            def ctx_tile(b):
                return ctx[bass.ds(b, 1)].rearrange("a (j s) d -> s (a j) d", s=SR)

            def mask_load(l, b, u):
                if l.n == 1 or not has(b):
                    return
                a = A[l.n]
                if isinstance(b, int) and b == 0:
                    sp.wait_ge(a.mask_sum.sem, a.mask_sum.at(1))
                    sp.dma_start(mask_rows, a.mask_f[0:NB]).then_inc(a.mask_stored.sem, 16)
                    sp.wait_ge(a.mask_stored.sem, a.mask_stored.at(16))
                if due(b - 1):
                    sp.wait_ge(a.max_ready.sem, a.max_ready.at(b - 1))
                row = mask_rows[bass.ds(b, 1), :].rearrange("a s -> (a s)")
                mask_in = (a.mask_in0, a.mask_in1)
                sp.dma_start(a.mask_add[0:T, u % 2], row.partition_broadcast(T)).then_inc(mask_in[u % 2].sem, 16)

            def y_load(l, b, u):
                if l.n == 0 or not has(b):
                    return
                a = A[l.n]
                if due(b - 1):
                    sp.wait_ge(a.x2_done.sem, a.x2_done.at(b - 1))
                sp.dma_start(a.y[0:T, u % 2], yg[0][bass.ds(b * T, T), :]).then_inc((a.y_in0, a.y_in1)[u % 2].sem, 16)

            def attention(l):
                def body(i, u):
                    ctx_load(l, i + (4 if l.n == 0 else 1), u + (4 if l.n == 0 else 1))
                    y_load(l, i + 4, u + 4)
                    mask_load(l, i, u)
                for i in range(-4, 4):
                    body(i, i % 4)
                with sp.Fori(4, 9, 4) as r:
                    for u in range(4):
                        body(r + u, u)
                for i in range(12, NB):
                    body(i, i % 4)

            def experts(l):
                a, m = A[l.n], B[l.n]
                load_shared(sp, l)
                attention_left(sp, l)
                rows_in, scat = (m.rows_in0, m.rows_in1), (m.scat0, m.scat1)

                def rows(g, h):
                    if due(g - 1):
                        sp.wait_ge(scat[h].sem, scat[h].at(64 * (g // 2) if isinstance(g, int) else 32 * (g - h)))
                    for u in range(4):
                        j = g * (4 // l.K) + u // l.K
                        src = xn_rows[l.n][bass.ds(j, 1)].rearrange("a t d -> t (a d)")
                        sp.dma_start(m.rows[0:T, 4 * h + u, 0:D], src).then_inc(rows_in[h].sem, 16)
                rows(0, 0)
                rows(1, 1)
                with sp.Fori(2, NB * l.K // 4 - 1, 2) as r:
                    for h in range(2):
                        rows(r + h, h)
                for e in range(E // 2, E - 1 + l.n):
                    load_expert(sp, l, 4 * e, m.weights_in)
                for s in scat:
                    sp.wait_ge(s.sem, s.at(16 * NB * l.K // 2))
                if l.n == 0:
                    load_expert(sp, l, 4 * (E - 1), m.late_in)
                sp.wait_ge(m.shared_done.sem, m.shared_done.at(NB // GT))
                if l.n == 0:
                    b = A[1]
                    sp.dma_start(b.w1_r, w1_w.rearrange("(k p) d -> p k d", p=P)).then_inc(b.consts_in.sem, 16)
                    sp.dma_start(b.w2_r, w2_w.rearrange("(k p) f -> p k f", p=P)).then_inc(b.consts_in.sem, 16)
                g_in = (m.g_in0, m.g_in1, m.g_in2, m.g_in3)
                yscat = (m.yscat0, m.yscat1, m.yscat2, m.yscat3)

                def tile_load(i, u, first):
                    if not has(i, l.tiles):
                        return
                    if not first:
                        if due(16 * (i // 4) if isinstance(i, int) else 4 * (i - u)):
                            sp.wait_ge(yscat[u].sem, yscat[u].at(16 * (i // 4) if isinstance(i, int) else 4 * (i - u)))
                    sp.dma_start(m.g[:, u], xg[l.n][bass.ds(i * P, P), :]).then_inc(g_in[u].sem, 16)
                for i in range(4):
                    tile_load(i, i, True)
                with sp.Fori(4, l.loop_hi - 3, 4) as r:
                    for u in range(4):
                        tile_load(r + u, u, False)
                for i in range(l.loop_hi, l.tiles):
                    tile_load(i, i % 4, False)
                for u in range(4):
                    sp.wait_ge(yscat[u].sem, yscat[u].at(16 * len(range(u, l.tiles, 4))))

            for i in range(1, 4):
                sp.dma_start(xs[0:T, 4 * i:4 * i + 4], x[4 * i:4 * i + 4].rearrange("b t d -> t b d")).then_inc(x_in[i], 16)
            attention(LAYERS[0])
            experts(LAYERS[0])
            attention(LAYERS[1])
            l, m = LAYERS[1], B[1]
            experts(LAYERS[1])
            fin_in = (m.fin_in0, m.fin_in1, m.fin_in2, m.fin_in3)

            def back(j, u):
                if due(j - 3):
                    sp.wait_ge(m.fin_ready.sem, m.fin_ready.at(j - 3))
                src = yg[1][bass.ds(j * (2 * T), 2 * T), :].rearrange("(t k) d -> t k d", k=2)
                sp.dma_start(m.fin[0:T, u], src).then_inc(fin_in[u].sem, 16)

            def store(j, u):
                sp.wait_ge(m.fin_ready.sem, m.fin_ready.at(j + 1))
                sp.dma_start(out[bass.ds(j, 1)].rearrange("a t d -> t (a d)"), tile_of(xs, j)).then_inc(m.out_done.sem, 16)
            for j in range(4):
                back(j, j)
            with sp.Fori(4, NB - 3, 4) as r:
                for u in range(4):
                    store(r + (u - 4), u)
                    back(r + u, u)
            for j in range(NB - 4, NB):
                store(j, j % 4)
            sp.wait_ge(m.out_done.sem, m.out_done.at(16 * NB))

        @block.scalar
        def _(act):
            a0 = A[0]

            def col(dst, v, s):
                act.dma_start(dst, v.rearrange("(k p) -> p k", p=P), allow_slow_non_contiguous=True).then_inc(s, 16)

            act.dma_start(a0.Wq_r, Wq.rearrange("(k p) e -> p k e", p=P)).then_inc(a0.consts_in.sem, 16)
            act.dma_start(a0.Wk_r, Wk.rearrange("(k p) e -> p k e", p=P)).then_inc(a0.consts_in.sem, 16)
            act.dma_start(a0.Wv, Wv.rearrange("(k p) e -> p k e", p=P)).then_inc(a0.consts_in.sem, 16)
            for dst, v in ((gt_c, ln_t_g), (bt_c, ln_t_b), (ga_c, ln_a_g), (ba_c, ln_a_b), (bq_c, bq), (bk_c, bk),
                           (b1_c, w1_b)):
                col(dst, v, small_in)
            for n in range(2):
                act.dma_start(gates_raw[:, n:n + 1], g_xattn[n:n + 1].partition_broadcast(P)).then_inc(small_in, 16)
                act.dma_start(gates_raw[:, 2 + n:3 + n], g_ffn[n:n + 1].partition_broadcast(P)).then_inc(small_in, 16)
                act.dma_start(route_w[n], router_w[n].rearrange("(k p) e -> p k e", p=P)).then_inc(small_in, 16)
            act.dma_start(rb_bc, rb.partition_broadcast(P)).then_inc(small_in, 16)
            act.dma_start(a0.gp, ln_p_g.partition_broadcast(P)).then_inc(small_in, 16)
            act.dma_start(a0.bp, ln_p_b.partition_broadcast(P)).then_inc(small_in, 16)
            act.dma_start(a0.vbias, bv.partition_broadcast(P)).then_inc(small_in, 16)

            act.wait_ge(small_in, 16 * SMALL)
            nc.scalar.activation(tanh_g, gates_raw, ACT.Tanh).then_inc(tanh_ready, 1)

            def setup(l):
                a = A[l.n]
                if l.n == 0:
                    act.wait_ge(a.setup_pe.sem, a.setup_pe.at(1))
                    nc.scalar.copy(a.WqT, ps[:, 0, :].rearrange("p (k d) -> p k d", k=KD)).then_inc(a.setup_act.sem, 1)
                    nc.scalar.copy(a.WkT, ps[:, 1, :].rearrange("p (k d) -> p k d", k=KD)).then_inc(a.setup_act.sem, 1)
                    act.wait_ge(a.setup_pe.sem, a.setup_pe.at(2))
                    for k in range(KD):
                        nc.scalar.activation(a.Aqk[:, k], ps[:, 2, k * D:(k + 1) * D], ACT.Identity,
                                             scale=gt_c[:, k:k + 1])
                        nc.scalar.activation(wqbk[:, k:k + 1], ps[:, 3, 2 + k:3 + k], ACT.Identity,
                                             scale=gt_c[:, k:k + 1])
                        nc.scalar.activation(qbias[:, k:k + 1], ps[:, 3, k:k + 1], ACT.Identity,
                                             scale=ga_c[:, k:k + 1])
                    nc.scalar.copy(c0[0:T], ps[0:T, 3, 4:5]).then_inc(a.setup_act.sem, 1)
                else:
                    act.wait_ge(a.setup_pe.sem, a.setup_pe.at(1))
                    nc.scalar.copy(a.w1T, ps[:, 0, :].rearrange("p (k d) -> p k d", k=KD)).then_inc(a.setup_act.sem, 1)
                    for h in range(2):
                        nc.scalar.copy(a.w2T[:, 2 * h:2 * h + 2], ps[:, 1 + h, :].rearrange("p (k d) -> p k d", k=KD)
                                       ).then_inc(a.setup_act.sem, 1)

            def attention(l):
                a = A[l.n]

                def body(i, u):
                    if isinstance(i, int) and i in (0, 13):
                        load_expert(act, l, i // 13 * 12, B[l.n].weights_in)
                    elif not isinstance(i, int) and u == 1:
                        load_expert(act, l, i - 1, B[l.n].weights_in)
                    b = i + 2
                    if has(b):
                        act.wait_ge(a.turned.sem, a.turned.at(b + 1))
                        if due(b):
                            act.wait_ge(a.q_done.sem, a.q_done.at(b))
                        nc.scalar.copy(a.tT, ps[:, 2, 0:KD * T].rearrange("p (k t) -> p k t", k=KD)
                                       ).then_inc(a.tT_ready.sem, 1)
                    b, v = i - 5, (u - 5) % 4
                    if has(b):
                        act.wait_ge(a.xnturn_done.sem, a.xnturn_done.at(b + 1))
                        dst = xn_rows[l.n][bass.ds(b, 1)].rearrange("a t d -> t (a d)")
                        act.dma_start(dst, a.xn[0:T, v % 2]).then_inc((a.rows_out0, a.rows_out1)[v % 2].sem, 16)
                        nc.scalar.copy(a.xnTb[:, v % 2],
                                       ps[:, 2, KD * T:2 * KD * T].rearrange("p (k t) -> p k t", k=KD)
                                       ).then_inc(a.xnTb_ready.sem, 1)
                    b, v = i + 2, (u + 2) % 4
                    if has(b):
                        if due(b - 1):
                            act.wait_ge(a.scores_done.sem, a.scores_done.at(b - 1))
                        nc.scalar.copy(a.kT[:, v % 2], ps[:, 0:KD, 0:S]).then_inc(a.kT_ready.sem, 1)
                    b, v = i, u
                    if has(b):
                        act.wait_ge(a.max_ready.sem, a.max_ready.at(b + 1))
                        if l.n == 1:
                            if due(b):
                                act.wait_ge(a.pT_done.sem, a.pT_done.at(b))
                        raw = a.probs[0:T] if l.n == 0 else ps[0:T, 4, 0:S]
                        nc.scalar.activation(a.probs[0:T], raw, ACT.Exp, scale=SCALE,
                                             bias=nbias[0:T, v:v + 1], accum_out=rsum[0:T, v:v + 1]
                                             ).then_inc(a.probs_ready.sem, 1)
                    b = i - 1
                    if has(b):
                        act.wait_ge(a.cross_done.sem, a.cross_done.at(b + 1))
                        if due(b):
                            act.wait_ge(a.final_done.sem, a.final_done.at(b))
                        nc.scalar.copy(a.crossT, ps[:, 6, 0:KD * T].rearrange("p (k t) -> p k t", k=KD)
                                       ).then_inc(a.crossT_ready.sem, 1)
                    b, v = i + 3, (u + 3) % 4
                    if l.n == 0 and has(b):
                        act.wait_ge(a.rstd_ready.sem, a.rstd_ready.at(i + 4))
                        if due(b - 3):
                            act.wait_ge(a.cross_done.sem, a.cross_done.at(b - 3))
                        for j in range(SJ):
                            ins = nc.scalar.activation(a.kv[0:SR, v, j], a.raw[0:SR, v, j], ACT.Identity,
                                                       scale=rstd[0:SR, (u - 1) % 2, j:j + 1],
                                                       bias=nmr[0:SR, (u - 1) % 2, j:j + 1])
                        ins.then_inc(a.normed.sem, 1)
                    b = i
                    if has(b):
                        act.wait_ge(a.pT_done.sem, a.pT_done.at(b + 1))
                        if due(b):
                            act.wait_ge(a.cross_done.sem, a.cross_done.at(b))
                        nc.scalar.copy(a.pT[0:SR], ps[0:SR, 5, 0:SJ * T].rearrange("p (j t) -> p j t", j=SJ)
                                       ).then_inc(a.pT_ready.sem, 1)
                    b = i - 5
                    if has(b):
                        act.wait_ge(a.router_done.sem, a.router_done.at(b + 1))
                        nc.scalar.activation(tile_of(logits, b), ps[0:T, 3, 264:264 + E], ACT.Copy,
                                             scale=1.0 if l.n == 0 else SCALE).then_inc(a.logits_ready.sem, 1)
                    b, v = i + 2, (u + 2) % 4
                    if has(b):
                        act.wait_ge(a.q_done.sem, a.q_done.at(b + 1))
                        bias = qbias if l.n == 0 else b1_c
                        for k in range(KD):
                            ins = nc.scalar.activation(a.qT[:, v % 2, k], ps[:, 3, k * T:(k + 1) * T], ACT.Identity,
                                                       bias=bias[:, k:k + 1],
                                                       scale=ga_c[:, k:k + 1] if l.n == 0 else 1.0)
                        if l.n == 0:
                            ins = nc.scalar.activation(cq[0:T, v:v + 1], ps[0:T, 3, 256:257], ACT.Identity,
                                                       bias=c0[0:T])
                        ins.then_inc(a.q_ready.sem, 1)
                loop(act, body, 5)

            def gates(l):
                m = B[l.n]
                act.wait_ge(m.lk_ready.sem, m.lk_ready.at(1))
                nc.scalar.activation(token_w[0:T].rearrange("p b k -> p k b")[:, 0:l.K], m.lw[0:T, 0:l.K], ACT.Sigmoid
                                     ).then_inc(m.gate_ready.sem, 1)

            def shared(l):
                a, m = A[l.n], B[l.n]

                def group(g):
                    for c in range(l.FC):
                        n = g * l.FC + c
                        r = l.rows(c)
                        act.wait_ge(m.gate_done.sem, m.gate_done.at(n + 1))
                        if due(n - 1):
                            act.wait_ge(m.mid_ready.sem, m.mid_ready.at(n - 1))
                        nc.scalar.activation(m.silu_s[0:r, c % 2], ps[0:r, c % 2, 0:GN], ACT.Silu
                                             ).then_inc(m.silu_ready.sem, 1)
                        if isinstance(g, int):
                            act.wait_ge(m.up_done.sem, m.up_done.at(c + 1))
                            nc.scalar.copy(m.midT_s[0:r, c], ps[0:r, 2 + c % 2, 0:GN]).then_inc(m.up_copied.sem, 1)
                act.wait_ge(a.cross_done.sem, a.cross_done.at(NB))
                act.wait_ge(a.final_done.sem, a.final_done.at(NB))
                group(0)
                gates(l)
                with act.Fori(1, NB // GT) as g:
                    group(g)

            def routed(l):
                m = B[l.n]
                C1 = 4

                def turn(i, u):
                    if has(i, l.tiles):
                        act.wait_ge(m.gturn_done.sem, m.gturn_done.at(i + 1))
                        nc.scalar.copy(m.gT[:, u % 2], ps[:, 4, 0:KD * P].rearrange("p (k t) -> p k t", k=KD)
                                       ).then_inc(m.gT_ready.sem, 1)

                def body(i, u):
                    if has(i, l.tiles):
                        for h in range(l.halves):
                            act.wait_ge(m.rgate_done.sem, m.rgate_done.at(i * l.halves + h + 1))
                            if h == 0:
                                if due(i * l.halves):
                                    act.wait_ge(m.rmid_ready.sem, m.rmid_ready.at(i * l.halves))
                            nc.scalar.activation(m.silu[:, h * l.FH:(h + 1) * l.FH], ps[:, h, 0:l.FH], ACT.Silu
                                                 ).then_inc(m.rsilu_ready.sem, 1)
                    turn(i + 1, u + 1)
                    if has(i, l.tiles):
                        act.wait_ge(m.mturn_done.sem, m.mturn_done.at(i + 1))
                        if due(i):
                            act.wait_ge(m.rout_done.sem, m.rout_done.at(i))
                        nc.scalar.copy(m.midT[:, 0:C1], ps[:, 5, :].rearrange("p (c t) -> p c t", c=C1)
                                       ).then_inc(m.midT_a.sem, 1)
                turn(0, 0)
                run_tiles(act, l, body, 0)

            setup(LAYERS[0])
            attention(LAYERS[0])
            shared(LAYERS[0])
            routed(LAYERS[0])
            act.wait_ge(B[0].rout_done.sem, B[0].rout_done.at(LAYERS[0].tiles))
            a1, l = A[1], LAYERS[1]
            setup(l)
            attention(l)
            shared(l)
            routed(l)

        @block.tensor
        def _(pe):
            mm = nc.tensor.matmul

            def setup(l):
                a = A[l.n]
                pe.wait_ge(a.consts_in.sem, a.consts_in.at(16 * (3 if l.n == 0 else 2)))
                if l.n == 0:
                    pe.wait_ge(ident_ready, 4)
                    pe.wait_ge(small_in, 16 * SMALL)
                    for n, w, offset in ((0, a.Wq_r, bt_c), (1, a.Wk_r, ba_c)):
                        for c in range(KD):
                            for k in range(KD):
                                mm(ps[:, 3, 8 + 2 * n + c:9 + 2 * n + c], w[:, k, c * P:(c + 1) * P],
                                   offset[:, k:k + 1], start=(k == 0), stop=(k == KD - 1))
                    for n, w in ((0, a.Wq_r), (1, a.Wk_r)):
                        for r in range(KD):
                            for c in range(KD):
                                ins = nc.tensor.transpose(ps[:, n, c * D + r * P:c * D + (r + 1) * P],
                                                          w[:, r, c * P:(c + 1) * P], ident)
                    ins.then_inc(a.setup_pe.sem, 1)
                    pe.wait_ge(a.setup_act.sem, a.setup_act.at(2))
                    pe.wait_ge(a.setup_dve.sem, a.setup_dve.at(1))
                    for dc in range(KD):
                        for k in range(KD):
                            mm(ps[:, 2, dc * D:(dc + 1) * D], a.WqT[:, k, dc * P:(dc + 1) * P], a.WkT[:, k],
                               start=(k == 0), stop=(k == KD - 1))
                    for dc in range(KD):
                        for k in range(KD):
                            mm(ps[:, 3, dc:dc + 1], a.WkT[:, k, dc * P:(dc + 1) * P], bq_c[:, k:k + 1],
                               start=(k == 0), stop=(k == KD - 1))
                        for k in range(KD):
                            mm(ps[:, 3, 2 + dc:3 + dc], a.WqT[:, k, dc * P:(dc + 1) * P], bk_c[:, k:k + 1],
                               start=(k == 0), stop=(k == KD - 1))
                    for k in range(KD):
                        mm(ps[0:T, 3, 4:5], ones[:, 0:T], bqbk[:, k:k + 1], start=(k == 0), stop=(k == KD - 1))
                    for k in range(KD):
                        ins = mm(ps[0:T, 4, 0:D], a.bvec[:, k, 0:T], a.Wv[:, k], start=(k == 0), stop=(k == KD - 1))
                    ins.then_inc(a.setup_pe.sem, 1)
                    pe.wait_ge(a.setup_act.sem, a.setup_act.at(3))
                else:
                    for r in range(KD):
                        for c in range(KD):
                            nc.tensor.transpose(ps[:, 0, c * D + r * P:c * D + (r + 1) * P],
                                                a.w1_r[:, r, c * P:(c + 1) * P], ident)
                    for r in range(KD):
                        for c in range(2 * KD):
                            ins = nc.tensor.transpose(
                                ps[:, 1 + c // 2, (c % 2) * D + r * P:(c % 2) * D + (r + 1) * P],
                                a.w2_r[:, r, c * P:(c + 1) * P], ident)
                    ins.then_inc(a.setup_pe.sem, 1)
                    pe.wait_ge(a.setup_act.sem, a.setup_act.at(3))

            def attention(l):
                a = A[l.n]

                def body(i, u):
                    b, v = i, u
                    if has(b):
                        if l.n == 0 and isinstance(b, int) and b == 0:
                            pe.wait_ge(a.setup_dve.sem, a.setup_dve.at(3))
                        pe.wait_ge(a.q_ready.sem, a.q_ready.at(b + 1))
                        pe.wait_ge(a.kT_ready.sem, a.kT_ready.at(b + 1))
                        if due(b):
                            pe.wait_ge(a.probs_ready.sem, a.probs_ready.at(b))
                        for k in range(KD):
                            ins = mm(ps[0:T, 4, 0:S], a.qT[:, v % 2, k], a.kT[:, v % 2, k], start=(k == 0),
                                     stop=(k == KD - 1))
                        ins.then_inc(a.scores_done.sem, 1)
                    if due(upto(i + 2, NB)):
                        pe.wait_ge(a.tT_ready.sem, a.tT_ready.at(upto(i + 2, NB)))
                    if isinstance(i, int) and due(upto(i - 5, NB)):
                        pe.wait_ge(a.xnTb_ready.sem, a.xnTb_ready.at(upto(i - 5, NB)))
                    b, v = i - 5, (u - 5) % 4
                    if has(b):
                        pe.wait_ge(a.xn_ready.sem, a.xn_ready.at(b + 1))
                        for k in range(KD):
                            ins = nc.tensor.transpose(ps[:, 2, (KD + k) * T:(KD + k + 1) * T],
                                                      a.xn[0:T, v % 2, k * P:(k + 1) * P], ident[0:T, 0:T])
                        ins.then_inc(a.xnturn_done.sem, 1)
                    b, v = i + 2, (u + 2) % 4
                    if has(b):
                        pe.wait_ge(a.xt_ready.sem, a.xt_ready.at(b + 1))
                        if l.n == 0:
                            pe.wait_ge(a.normed.sem, a.normed.at(b + 1))
                        if l.n == 1:
                            raw_in = (a.raw_in0, a.raw_in1, a.raw_in2, a.raw_in3)
                            pe.wait_ge(raw_in[v].sem, raw_in[v].at(16 * (b // 4 + 1) if isinstance(b, int) else 4 * (b - v) + 16))
                        for k in range(KD):
                            nc.tensor.transpose(ps[:, 2, k * T:(k + 1) * T], a.xt[0:T, v % 2, k * P:(k + 1) * P],
                                                ident[0:T, 0:T])
                        if due(b):
                            pe.wait_ge(a.kT_ready.sem, a.kT_ready.at(b))
                        for k in range(KD):
                            for j in range(SJ):
                                ins = nc.tensor.transpose(ps[:, k, j * SR:(j + 1) * SR],
                                                          a.kv[0:SR, v, j, k * P:(k + 1) * P], ident[0:SR, 0:SR])
                        ins.then_inc(a.turned.sem, 1)
                    b = i - 2
                    if has(b):
                        pe.wait_ge(a.crossT_ready.sem, a.crossT_ready.at(b + 1))
                        if due(b):
                            pe.wait_ge(a.final_read.sem, a.final_read.at(b))
                        if l.n == 1:
                            if due(upto(i + 2, NB)):
                                pe.wait_ge(a.xpart_read.sem, a.xpart_read.at(upto(i + 2, NB)))
                        w = a.Wv if l.n == 0 else a.w2T[:, KD:2 * KD]
                        for k in range(KD):
                            ins = mm(ps[0:T, 7, 0:D], a.crossT[:, k], w[:, k], start=(k == 0), stop=(k == KD - 1))
                        ins.then_inc(a.final_done.sem, 1)
                    b, v = i - 1, (u - 1) % 4
                    if has(b):
                        pe.wait_ge(a.pT_ready.sem, a.pT_ready.at(b + 1))
                        if due(b):
                            pe.wait_ge(a.crossT_ready.sem, a.crossT_ready.at(b))
                        for k in range(KD):
                            for j in range(SJ):
                                ins = mm(ps[:, 6, k * T:(k + 1) * T], a.kv[0:SR, v, j, k * P:(k + 1) * P],
                                         a.pT[0:SR, j], start=(j == 0), stop=(j == SJ - 1))
                        ins.then_inc(a.cross_done.sem, 1)
                    b = i - 5
                    if due(upto(i + 2, NB)):
                        pe.wait_ge(a.q_ready.sem, a.q_ready.at(upto(i + 2, NB)))
                    if isinstance(i, int) and due(upto(b, NB)):
                        pe.wait_ge(a.logits_ready.sem, a.logits_ready.at(upto(b, NB)))
                    if has(b):
                        pe.wait_ge(a.xnTb_ready.sem, a.xnTb_ready.at(b + 1))
                        for k in range(KD):
                            ins = mm(ps[0:T, 3, 264:264 + E], a.xnTb[:, (u - 5) % 2, k], route_w[l.n][:, k], start=(k == 0),
                                     stop=(k == KD - 1))
                        ins.then_inc(a.router_done.sem, 1)
                    b = i + 2
                    if has(b):
                        pe.wait_ge(a.tT_ready.sem, a.tT_ready.at(b + 1))
                        if l.n == 1:
                            if due(i - 1):
                                pe.wait_ge(a.final_read.sem, a.final_read.at(i - 1))
                            if due(b):
                                pe.wait_ge(a.xpart_read.sem, a.xpart_read.at(b))
                            for k in range(KD):
                                ins = mm(ps[0:T, 7, D:2 * D], a.tT[:, k], a.w2T[:, k], start=(k == 0),
                                         stop=(k == KD - 1))
                            ins.then_inc(a.xpart_done.sem, 1)
                        w = a.Aqk if l.n == 0 else a.w1T
                        for h in range(KD):
                            for k in range(KD):
                                ins = mm(ps[:, 3, h * T:(h + 1) * T], w[:, k, h * P:(h + 1) * P], a.tT[:, k],
                                         start=(k == 0), stop=(k == KD - 1))
                        if l.n == 0:
                            for k in range(KD):
                                ins = mm(ps[0:T, 3, 256:257], a.tT[:, k], wqbk[:, k:k + 1], start=(k == 0),
                                         stop=(k == KD - 1))
                        ins.then_inc(a.q_done.sem, 1)
                    b = i
                    if has(b):
                        pe.wait_ge(a.probs_ready.sem, a.probs_ready.at(b + 1))
                        if due(b):
                            pe.wait_ge(a.pT_ready.sem, a.pT_ready.at(b))
                        for j in range(SJ):
                            ins = nc.tensor.transpose(ps[0:SR, 5, j * T:(j + 1) * T],
                                                      a.probs[0:T, j * SR:(j + 1) * SR], ident[0:T, 0:T])
                        ins.then_inc(a.pT_done.sem, 1)
                loop(pe, body, 5)

            def ranks(l):
                m = B[l.n]
                pe.wait_ge(m.disp_sel.sem, m.disp_sel.at(1))
                sel = m.both[0:T].rearrange("p b e -> p (b e)")
                mm(ps[0:T, 4, 0:NB * E], before[0:T], sel, start=True, stop=True)
                mm(ps[0:T, 5, 0:NB * E], ones[0:T, 0:T], sel, start=True, stop=True).then_inc(m.disp_pe.sem, 1)

            def shared(l):
                a, m = A[l.n], B[l.n]
                pe.wait_ge(a.xnTb_ready.sem, a.xnTb_ready.at(NB))
                pe.wait_ge(a.logits_ready.sem, a.logits_ready.at(NB))
                pe.wait_ge(a.crossT_ready.sem, a.crossT_ready.at(NB))
                pe.wait_ge(a.final_read.sem, a.final_read.at(NB))
                pe.wait_ge(m.shared_in.sem, m.shared_in.at(16 * DMAS[l.n]))
                pe.wait_ge(a.xnT_ready.sem, a.xnT_ready.at(NB))

                def back(g, c):
                    pe.wait_ge(m.mid_ready.sem, m.mid_ready.at(g * l.FC + c + 1))
                    if c == 0 and isinstance(g, int):
                        pe.wait_ge(m.ranks_read.sem, m.ranks_read.at(2))
                    elif c == 0:
                        pe.wait_ge(m.shared_read.sem, m.shared_read.at(g * GT))
                    r = l.rows(c)
                    for j in range(GT):
                        ins = mm(ps[0:T, 4 + j, 0:D], m.midT_s[0:r, c, j * T:(j + 1) * T], m.ws_back[0:r, c],
                                 start=(c == 0), stop=(c == l.FC - 1))
                    if c == l.FC - 1:
                        ins.then_inc(m.shared_done.sem, 1)

                def group(g):
                    for c in range(l.FC):
                        n = g * l.FC + c
                        r = l.rows(c)
                        for half, up_bank, free, done in ((0, c % 2, m.silu_ready, m.gate_done),
                                                          (1, 2 + c % 2, m.mid_ready, m.up_done)):
                            if due(n - 1):
                                pe.wait_ge(free.sem, free.at(n - 1))
                            pe.nop(nofuse=True)
                            for k in range(KD):
                                ins = mm(ps[0:r, up_bank, 0:GN], m.ws_gu[:, half, k, c * P:c * P + r],
                                         xnT[:, k, bass.ds(g * GN, GN)], start=(k == 0), stop=(k == KD - 1))
                            ins.then_inc(done.sem, 1)
                        if isinstance(g, int) and c == 1:
                            ranks(l)
                        if c:
                            back(g, c - 1)
                    back(g, l.FC - 1)
                group(0)
                with pe.Fori(1, NB // GT) as g:
                    group(g)

            def routed(l):
                m = B[l.n]
                g_in = (m.g_in0, m.g_in1, m.g_in2, m.g_in3)
                pe.wait_ge(m.weights_in.sem, m.weights_in.at(16 * DMAS[l.n] * (E - 1 + l.n)))
                if l.n == 0:
                    pe.wait_ge(m.late_in.sem, m.late_in.at(16 * DMAS[0]))
                pe.wait_ge(m.shared_read.sem, m.shared_read.at(NB))
                C1 = 4

                def turn(i, u):
                    if has(i, l.tiles):
                        u = u % 4
                        pe.wait_ge(g_in[u].sem, g_in[u].at(16 * (i // 4 + 1) if isinstance(i, int) else 4 * (i - u) + 16))
                        if due(i):
                            pe.wait_ge(m.gT_ready.sem, m.gT_ready.at(i))
                        for k in range(KD):
                            ins = nc.tensor.transpose(ps[:, 4, k * P:(k + 1) * P], m.g[:, u, k * P:(k + 1) * P], ident)
                        ins.then_inc(m.gturn_done.sem, 1)

                def body(i, u):
                    turn(i + 1, u + 1)
                    if has(i, l.tiles):
                        e = pe.value_load(tile_expert[0:1, bass.ds(i, 1)], min_val=0, max_val=E - 1)
                        pe.wait_ge(m.gT_ready.sem, m.gT_ready.at(i + 1))
                        for half, free, done in ((0, m.rsilu_ready, m.rgate_done), (1, m.rmid_ready, m.rup_done)):
                            for h in range(l.halves):
                                if h == 0:
                                    if due(i * l.halves):
                                        pe.wait_ge(free.sem, free.at(i * l.halves))
                                for k in range(KD):
                                    w = wgu[l.n][:, bass.ds(e, 1), half, k, h * l.FH:(h + 1) * l.FH]
                                    ins = mm(ps[:, 2 * half + h, 0:l.FH], m.gT[:, u % 2, k],
                                             w.rearrange("p a f -> p (a f)"), start=(k == 0), stop=(k == KD - 1))
                                ins.then_inc(done.sem, 1)
                    if has(i - 1, l.tiles):
                        e = pe.value_load(tile_expert[0:1, bass.ds(i - 1, 1)], min_val=0, max_val=E - 1)
                        if due(i):
                            pe.wait_ge(m.midT_a.sem, m.midT_a.at(i))
                        if l.FC > C1:
                            if due(i):
                                pe.wait_ge(m.midT_d.sem, m.midT_d.at(i))
                        if due(i - 1):
                            pe.wait_ge(m.y_ready.sem, m.y_ready.at(i - 1))
                        for c in range(l.FC):
                            r = l.rows(c)
                            w = wback[l.n][0:r, bass.ds(e, 1), c, :].rearrange("p a d -> p (a d)")
                            ins = mm(ps[:, 7, 0:D], m.midT[0:r, c], w, start=(c == 0), stop=(c == l.FC - 1))
                        ins.then_inc(m.rout_done.sem, 1)
                    if has(i, l.tiles):
                        pe.wait_ge(m.rmid_ready.sem, m.rmid_ready.at((i + 1) * l.halves))
                        if due(i):
                            pe.wait_ge(m.midT_a.sem, m.midT_a.at(i))
                        for c in range(l.FC):
                            r = l.rows(c)
                            ins = nc.tensor.transpose(ps[0:r, 5 + c // C1, (c % C1) * P:(c % C1 + 1) * P],
                                                      m.mid[:, c * P:c * P + r], ident)
                        ins.then_inc(m.mturn_done.sem, 1)
                turn(0, 0)
                run_tiles(pe, l, body, 0)

            for l in LAYERS:
                setup(l)
                attention(l)
                shared(l)
                routed(l)

        @block.vector
        def _(dve):
            v_ = nc.vector

            v_.memset(mv, 1.0).then_inc(init_dve, 1)
            v_.memset(uvar, 1.0).then_inc(init_dve, 1)

            def masks(a):
                dve.wait_ge(a.mask_all.sem, a.mask_all.at(16))
                v_.tensor_scalar(a.mask_f[0:NB], a.mask_i[0:NB], 0.0, -BIG, ALU.is_equal, ALU.mult
                                 ).then_inc(a.mask_sum.sem, 1)

            def weights_before(a):
                dve.wait_ge(small_in, 16 * SMALL)
                dve.wait_ge(ident_ready, 4)
                dve.wait_ge(tanh_ready, 1)
                dve.wait_ge(a.setup_pe.sem, a.setup_pe.at(1))
                v_.tensor_tensor(bq_c, bq_c, ps[:, 3, 8:10], ALU.add).then_inc(bias_own, 1)
                v_.tensor_tensor(bk_c, bk_c, ps[:, 3, 10:12], ALU.add).then_inc(bias_own, 1)
                dve.wait_ge(bias_own, 2)
                v_.tensor_tensor(bqbk, bq_c, bk_c, ALU.mult)
                for k in range(KD):
                    ins = v_.tensor_scalar(a.bvec[:, k], ones, ba_c[:, k:k + 1], None, ALU.mult)
                ins.then_inc(a.setup_dve.sem, 1)
                v_.tensor_scalar(a.gp, a.gp, tanh_g[:, 0:1], None, ALU.mult)
                v_.tensor_scalar(a.bp, a.bp, tanh_g[:, 0:1], None, ALU.mult).then_inc(a.setup_dve.sem, 1)

            def weights_after(a):
                dve.wait_ge(a.consts_in.sem, a.consts_in.at(48))
                dve.wait_ge(a.setup_pe.sem, a.setup_pe.at(2))
                v_.tensor_tensor(a.vbias[0:T], a.vbias[0:T], ps[0:T, 4, 0:D], ALU.add)
                for k in range(KD):
                    ins = v_.tensor_scalar(a.Wv[:, k], a.Wv[:, k], ga_c[:, k:k + 1], None, ALU.mult)
                ins.then_inc(a.setup_dve.sem, 1)
                dve.wait_ge(a.setup_dve.sem, a.setup_dve.at(3))

            def attention(l):
                a = A[l.n]
                own, chain = Steps(a.dve_own), Steps(a.dve_chain)
                tanh_a = tanh_g[0:T, l.n:l.n + 1]
                lo = 4

                def body(i, u):
                    if l.n == 0 and isinstance(i, int):
                        if i == -3:
                            weights_before(a)
                        if i == -2:
                            masks(a)
                            weights_after(a)
                    roots = not isinstance(i, int) or FIRST < i <= NB + 3
                    w, w1 = u % 2, (u - 1) % 2

                    def newton(n):
                        if not roots:
                            return
                        dve.wait_ge(chain.sem, chain.total())
                        if n % 3 == 0:
                            v_.scalar_tensor_tensor(newt, guess, -0.5, guess, ALU.mult, ALU.mult
                                                    ).then_inc(chain.sem, chain.one())
                        elif n % 3 == 1:
                            v_.tensor_tensor(newt, newt, uvar, ALU.mult).then_inc(chain.sem, chain.one())
                        else:
                            v_.scalar_tensor_tensor(rstd[:, w1, :] if n == 8 else guess, newt, 1.5, guess,
                                                    ALU.add, ALU.mult).then_inc(chain.sem, chain.one())

                    newton(0)
                    b, v = i, u
                    if has(b):
                        dve.wait_ge(a.scores_done.sem, a.scores_done.at(b + 1))
                        if l.n == 1:
                            v_.tensor_reduce(smax[0:T], ps[0:T, 4, 0:S], AX_X, ALU.max).then_inc(own.sem, own.one())
                        else:
                            mask_in = (a.mask_in0, a.mask_in1)[v % 2]
                            dve.wait_ge(mask_in.sem, mask_in.at(16 * (b // 2 + 1) if isinstance(b, int)
                                                                else 8 * (b - v % 2) + 16))
                            if due(b):
                                dve.wait_ge(a.pT_done.sem, a.pT_done.at(b))
                            dve.nop(nofuse=True)
                            v_.tensor_tensor_reduce(a.probs[0:T], ps[0:T, 4, 0:S], a.mask_add[0:T, v % 2],
                                                    1.0, -BIG, ALU.add, ALU.max, smax[0:T]).then_inc(own.sem, own.one())
                    newton(1)
                    if has(b) and l.n == 0:
                        dve.wait_ge(own.sem, own.total())
                        v_.scalar_tensor_tensor(smax[0:T], smax[0:T], cq[0:T, v:v + 1], cq[0:T, v:v + 1],
                                                ALU.add, ALU.subtract).then_inc(own.sem, own.one())
                    newton(2)
                    if has(b):
                        dve.wait_ge(own.sem, own.total())
                        v_.tensor_scalar(nbias[0:T, v:v + 1], smax[0:T], -SCALE, None, ALU.mult
                                         ).then_inc(a.max_ready.sem, 1)
                    b, v = i + 4, u
                    if has(b) and l.n == 1:
                        y_in = (a.y_in0, a.y_in1)[v % 2]
                        dve.wait_ge(y_in.sem, y_in.at(16 * (b // 2 + 1) if isinstance(b, int)
                                                      else 8 * (b - v % 2) + 16))
                        v_.scalar_tensor_tensor(tile_of(xs, b), a.y[0:T, v % 2], tanh_g[0:T, 2:3],
                                                tile_of(xs, b), ALU.mult, ALU.add).then_inc(a.x2_done.sem, 1)
                    if has(b) and l.n == 0:
                        raw_in = (a.raw_in0, a.raw_in1, a.raw_in2, a.raw_in3)[v]
                        dve.wait_ge(raw_in.sem, raw_in.at(16 * (b // 4 + 1) if isinstance(b, int)
                                                          else 4 * (b - v) + 16))
                    for j in range(SJ):
                        if has(b) and l.n == 0:
                            v_.bn_stats(bn[0:SR, j], a.raw[0:SR, v, j]).then_inc(own.sem, own.one())
                        newton(3 + j)
                    if has(b):
                        if l.n == 1:
                            dve.wait_ge(a.x2_done.sem, a.x2_done.at(b + 1))
                            dve.nop(nofuse=True)
                        elif isinstance(b, int):
                            dve.wait_ge(x_in[b // 4], 16)
                        elif u == lo % 4:
                            for s in x_in:
                                dve.wait_ge(s, 16)
                        v_.bn_stats(bn[0:T, 5], tile_of(xs, b)).then_inc(own.sem, own.one())
                    newton(6)
                    if has(i - 2):
                        v = (u - 2) % 4
                        dve.wait_ge(a.probs_ready.sem, a.probs_ready.at(i - 1))
                        v_.reciprocal(rinv[0:T, v:v + 1], rsum[0:T, v:v + 1]).then_inc(own.sem, own.one())
                    newton(7)
                    if has(i - 2):
                        final(i - 2, (u - 2) % 4)
                    newton(8)
                    if has(i - 2) and l.n == 0:
                        dve.wait_ge(a.final_read.sem, a.final_read.at(i - 1))
                        dve.nop(nofuse=True)
                        v_.bn_stats(bn[0:T, 3], a.cross[0:T, u % 2]).then_inc(own.sem, own.one())
                    if roots:
                        dve.wait_ge(chain.sem, chain.total())
                        v_.scalar_tensor_tensor(nmr[:, w1, :], mv[:, w1, 0:SJ, 0], -1.0, rstd[:, w1, 0:SJ],
                                                ALU.mult, ALU.mult).then_inc(a.rstd_ready.sem, 1)
                        dve.wait_ge(a.rstd_ready.sem, a.rstd_ready.at(i + 4))
                    b, v = i + 3, (u + 3) % 4
                    if has(b):
                        if due(b - 1):
                            dve.wait_ge(a.turned.sem, a.turned.at(b - 1))
                        v_.tensor_scalar(a.xt[0:T, v % 2], tile_of(xs, b), mv[0:T, w1, 5, 0:1], rstd[0:T, w1, 5:6],
                                         ALU.subtract, ALU.mult).then_inc(a.xt_ready.sem, 1)
                    b = i - 3
                    if has(b) and l.n == 0:
                        dve.wait_ge(a.xb_ready.sem, a.xb_ready.at(b + 1))
                        v_.scalar_tensor_tensor(a.cross[0:T, w1], a.cross[0:T, w1], mv[0:T, w1, 3, 0:1],
                                                a.gp[0:T], ALU.subtract, ALU.mult).then_inc(own.sem, own.one())
                        dve.wait_ge(own.sem, own.total())
                        v_.scalar_tensor_tensor(tile_of(xs, b), a.cross[0:T, w1], rstd[0:T, w1, 3:4], tile_of(xs, b),
                                                ALU.mult, ALU.add).then_inc(a.x_done.sem, 1)
                    stats = not isinstance(i, int) or i <= NB + 2
                    if stats:
                        dve.wait_ge(own.sem, own.total())
                        if l.n == 0 and due(upto(i + 3, NB)):
                            dve.wait_ge(a.normed.sem, a.normed.at(upto(i + 3, NB)))
                        if isinstance(i, int) and due(upto(i - 4, NB)):
                            dve.wait_ge(a.xn_ready.sem, a.xn_ready.at(upto(i - 4, NB)))
                        dve.nop(nofuse=True)
                    if has(i + 4):
                        if l.n == 0:
                            for j in range(SJ):
                                v_.bn_aggr(mv[0:SR, w, j], bn[0:SR, j]).then_inc(own.sem, own.one())
                        v_.bn_aggr(mv[0:T, w, 5], bn[0:T, 5]).then_inc(own.sem, own.one())
                    if has(i - 2) and l.n == 0:
                        v_.bn_aggr(mv[0:T, w, 3], bn[0:T, 3]).then_inc(own.sem, own.one())
                    if has(i - 3):
                        x_is_final = a.final_read if l.n else a.x_done
                        dve.wait_ge(x_is_final.sem, x_is_final.at(i - 2))
                        dve.nop(nofuse=True)
                        v_.bn_stats(bn[0:T, 4], tile_of(xs, i - 3)).then_inc(own.sem, own.one())
                    tail(i, u)
                    if not stats:
                        return
                    dve.wait_ge(own.sem, own.total())
                    dve.nop(nofuse=True)
                    if has(i - 3):
                        v_.bn_aggr(mv[0:T, w, 4], bn[0:T, 4]).then_inc(own.sem, own.one())
                        dve.wait_ge(own.sem, own.total())
                    if l.n == 0:
                        v_.tensor_scalar(uvar[:, 0:5], mv[:, w, 0:5, 1], EPS, None, ALU.add
                                         ).then_inc(own.sem, own.one())
                        v_.tensor_scalar(uvar[:, 5:6], mv[:, w, 5:6, 1], 1.0 + EPS, EPS * EPS, ALU.mult,
                                         ALU.add).then_inc(own.sem, own.one())
                    else:
                        v_.tensor_scalar(uvar, mv[:, w, :, 1], EPS, None, ALU.add).then_inc(own.sem, own.one())
                    dve.wait_ge(own.sem, own.total())
                    v_.tensor_scalar(guess.bitcast(I32), uvar.bitcast(I32), -0.5, float(0x5f3759df), ALU.mult,
                                     ALU.add).then_inc(chain.sem, chain.one())

                def final(b, v):
                    dve.wait_ge(a.final_done.sem, a.final_done.at(b + 1))
                    dve.wait_ge(own.sem, own.total())
                    if l.n == 0:
                        if due(b - 1):
                            dve.wait_ge(a.x_done.sem, a.x_done.at(b - 1))
                        v_.scalar_tensor_tensor(a.cross[0:T, v % 2], ps[0:T, 7, 0:D], rinv[0:T, v:v + 1],
                                                a.vbias[0:T], ALU.mult, ALU.add).then_inc(a.final_read.sem, 1)
                    else:
                        v_.tensor_scalar(rinv[0:T, v:v + 1], rinv[0:T, v:v + 1], tanh_a, None, ALU.mult
                                         ).then_inc(own.sem, own.one())
                        dve.wait_ge(own.sem, own.total())
                        dve.wait_ge(a.xpart_read.sem, a.xpart_read.at(b + 1))
                        v_.scalar_tensor_tensor(tile_of(xs, b), ps[0:T, 7, 0:D], rinv[0:T, v:v + 1],
                                                tile_of(xs, b), ALU.mult, ALU.add).then_inc(a.final_read.sem, 1)

                def tail(i, u):
                    b = i + 2
                    if l.n == 1 and has(b):
                        dve.wait_ge(a.xpart_done.sem, a.xpart_done.at(b + 1))
                        dve.wait_ge(a.xb_ready.sem, a.xb_ready.at(b + 1))
                        v_.scalar_tensor_tensor(tile_of(xs, b), ps[0:T, 7, D:2 * D], tanh_a, tile_of(xs, b), ALU.mult,
                                                ALU.add).then_inc(a.xpart_read.sem, 1)
                loop(dve, body, lo, (own, (18, 8)[l.n]), (chain, 10))

            def dispatch(l):
                a, m = A[l.n], B[l.n]
                own = Steps(m.own_dve)
                dve.wait_ge(m.iota_done.sem, m.iota_done.at(4))
                attention_left(dve, l)

                def be(v):
                    return v[0:T].rearrange("p b e -> p (b e)")

                def over_e(v):
                    return v.unsqueeze(2).to_broadcast([T, NB, E])

                def over_b(v):
                    return v.unsqueeze(1).to_broadcast([T, NB, E])

                v_.tensor_copy(m.rev[0:T], m.rev_i[0:T]).then_inc(own.sem, own.one())
                (v_.tensor_tensor(m.sel[0:T], logits[0:T], over_b(rb_bc[0:T]), ALU.add) if l.n else
                v_.tensor_copy(m.sel[0:T], logits[0:T])).then_inc(own.sem, own.one())
                dve.wait_ge(own.sem, own.total())
                for k in range(l.K):
                    oh = (m.oh0, m.oh1)[k]
                    v_.tensor_reduce(m.mx[0:T], m.sel[0:T], AX_X, ALU.max).then_inc(own.sem, own.one())
                    dve.wait_ge(own.sem, own.total())
                    v_.tensor_tensor(m.eq[0:T], m.sel[0:T], over_e(m.mx[0:T]), ALU.is_equal).then_inc(own.sem, own.one())
                    dve.wait_ge(own.sem, own.total())
                    v_.tensor_tensor(m.eq[0:T], m.eq[0:T], over_b(m.rev[0:T]), ALU.mult).then_inc(own.sem, own.one())
                    dve.wait_ge(own.sem, own.total())
                    v_.tensor_reduce(m.mx[0:T], m.eq[0:T], AX_X, ALU.max).then_inc(own.sem, own.one())
                    dve.wait_ge(own.sem, own.total())
                    v_.tensor_tensor(oh[0:T], m.eq[0:T], over_e(m.mx[0:T]), ALU.is_equal).then_inc(own.sem, own.one())
                    dve.wait_ge(own.sem, own.total())
                    if k + 1 < l.K:
                        v_.scalar_tensor_tensor(be(m.sel), be(oh), -BIG, be(m.sel), ALU.mult, ALU.add).then_inc(own.sem, own.one())
                    v_.tensor_tensor(m.acc[0:T], oh[0:T], logits[0:T], ALU.mult).then_inc(own.sem, own.one())
                    dve.wait_ge(own.sem, own.total())
                    v_.tensor_reduce(m.lk[0:T, k], m.acc[0:T], AX_X, ALU.add).then_inc(own.sem, own.one())
                    dve.wait_ge(own.sem, own.total())
                if l.K == 1:
                    v_.tensor_copy(m.both[0:T], m.oh0[0:T]).then_inc(m.disp_sel.sem, 1)
                    v_.tensor_copy(m.lw[0:T, 0], m.lk[0:T, 0]).then_inc(m.lk_ready.sem, 1)
                else:
                    v_.tensor_tensor(m.both[0:T], m.oh0[0:T], m.oh1[0:T], ALU.add).then_inc(m.disp_sel.sem, 1)
                    v_.tensor_tensor(m.lw[0:T, 0], m.lk[0:T, 0], m.lk[0:T, 1], ALU.subtract)
                    v_.tensor_tensor(m.lw[0:T, 1], m.lk[0:T, 1], m.lk[0:T, 0], ALU.subtract).then_inc(m.lk_ready.sem, 1)
                v_.tensor_copy(m.thr[0:T, 0:14], m.thr_i[0:T]).then_inc(own.sem, own.one())
                v_.tensor_copy(m.tile_no[0:T], m.tile_i[0:T]).then_inc(own.sem, own.one())
                dve.wait_ge(m.disp_pe.sem, m.disp_pe.at(1))
                tot = m.tot[0:T]
                v_.tensor_copy(tot, ps[0:T, 5, 0:NB * E].rearrange("p (b e) -> p b e", b=NB)
                               ).then_inc(m.ranks_read.sem, 1)
                v_.tensor_copy(m.rank[0:T], ps[0:T, 4, 0:NB * E].rearrange("p (b e) -> p b e", b=NB)
                               ).then_inc(m.ranks_read.sem, 1)
                dve.wait_ge(m.ranks_read.sem, m.ranks_read.at(2))
                v_.tensor_copy(m.acc[0:T], tot).then_inc(own.sem, own.one())
                dve.wait_ge(own.sem, own.total())
                src, dst = m.acc, m.acc2
                d = 1
                while d < NB:
                    v_.tensor_copy(dst[0:T, 0:d], src[0:T, 0:d]).then_inc(own.sem, own.one())
                    v_.tensor_tensor(dst[0:T, d:NB], src[0:T, d:NB], src[0:T, 0:NB - d], ALU.add).then_inc(own.sem, own.one())
                    dve.wait_ge(own.sem, own.total())
                    src, dst = dst, src
                    d *= 2
                count = src[0:T, NB - 1].unsqueeze(2).to_broadcast([T, E, 14])
                v_.tensor_tensor(m.cmp[0:T], count, m.thr[0:T].unsqueeze(1).to_broadcast([T, E, 14]),
                                 ALU.is_gt).then_inc(own.sem, own.one())
                dve.wait_ge(own.sem, own.total())
                v_.tensor_reduce(m.ntile[0:T], m.cmp[0:T], AX_X, ALU.add).then_inc(own.sem, own.one())
                dve.wait_ge(own.sem, own.total())
                v_.tensor_copy(m.cum[0:T], m.ntile[0:T]).then_inc(own.sem, own.one())
                dve.wait_ge(own.sem, own.total())
                c1, c2 = m.cum, m.cum2
                d = 1
                while d < E:
                    v_.tensor_copy(c2[0:T, 0:d], c1[0:T, 0:d]).then_inc(own.sem, own.one())
                    v_.tensor_tensor(c2[0:T, d:E], c1[0:T, d:E], c1[0:T, 0:E - d], ALU.add).then_inc(own.sem, own.one())
                    dve.wait_ge(own.sem, own.total())
                    c1, c2 = c2, c1
                    d *= 2
                v_.tensor_tensor(c2[0:T], c1[0:T], m.ntile[0:T], ALU.subtract).then_inc(own.sem, own.one())
                dve.wait_ge(own.sem, own.total())
                v_.tensor_scalar(c2[0:T], c2[0:T], float(P), None, ALU.mult).then_inc(own.sem, own.one())
                dve.wait_ge(own.sem, own.total())
                v_.tensor_tensor(dst[0:T], src[0:T], tot, ALU.subtract).then_inc(own.sem, own.one())
                dve.wait_ge(own.sem, own.total())
                v_.tensor_tensor(src[0:T], dst[0:T], m.rank[0:T], ALU.add).then_inc(own.sem, own.one())
                dve.wait_ge(own.sem, own.total())
                v_.tensor_tensor(dst[0:T], src[0:T], over_b(c2[0:T]), ALU.add).then_inc(own.sem, own.one())
                dve.wait_ge(own.sem, own.total())
                for k in range(l.K):
                    oh = (m.oh0, m.oh1)[k]
                    v_.tensor_tensor(m.eq[0:T], oh[0:T], dst[0:T], ALU.mult).then_inc(own.sem, own.one())
                    dve.wait_ge(own.sem, own.total())
                    v_.tensor_reduce(m.posf[0:T], m.eq[0:T], AX_X, ALU.add).then_inc(own.sem, own.one())
                    dve.wait_ge(own.sem, own.total())
                    v_.tensor_copy(pos_i[0:T, 0:NB * l.K].rearrange("p (b k) -> p b k", k=l.K)[:, :, k],
                                   m.posf[0:T]).then_inc(own.sem, own.one())
                    dve.wait_ge(own.sem, own.total())
                v_.tensor_tensor(m.tcmp[0:T], m.tile_no[0:T].unsqueeze(2).to_broadcast([T, l.tiles, E]),
                                 c1[0:T].unsqueeze(1).to_broadcast([T, l.tiles, E]), ALU.is_ge).then_inc(own.sem, own.one())
                dve.wait_ge(own.sem, own.total())
                v_.tensor_reduce(m.tile_no[0:T], m.tcmp[0:T], AX_X, ALU.add).then_inc(own.sem, own.one())
                dve.wait_ge(own.sem, own.total())
                v_.tensor_scalar(tile_expert[0:T, 0:l.tiles], m.tile_no[0:T], float(E - 1), None, ALU.min
                                 ).then_inc(m.disp_ready.sem, 1)

            def shared(l):
                m = B[l.n]
                tanh_f = tanh_g[0:T, 2 + l.n:3 + l.n]

                def middles(g):
                    for c in range(l.FC):
                        n = g * l.FC + c
                        r = l.rows(c)
                        dve.wait_ge(m.silu_ready.sem, m.silu_ready.at(n + 1))
                        dve.wait_ge(m.up_done.sem, m.up_done.at(n + 1))
                        if c == 0:
                            dve.wait_ge(m.shared_done.sem, m.shared_done.at(g))
                        v_.tensor_tensor(m.midT_s[0:r, c], m.silu_s[0:r, c % 2], ps[0:r, 2 + c % 2, 0:GN], ALU.mult
                                         ).then_inc(m.mid_ready.sem, 1)

                def results(g):
                    dve.wait_ge(m.shared_done.sem, m.shared_done.at(g + 1))
                    for j in range(GT):
                        xt = tile_of(xs, g * GT + j)
                        v_.scalar_tensor_tensor(xt, ps[0:T, 4 + j, 0:D], tanh_f, xt, ALU.mult, ALU.add
                                                ).then_inc(m.shared_read.sem, 1)
                results(0)
                with dve.Fori(1, NB // GT) as g:
                    middles(g)
                    results(g)

            def routed(l):
                m = B[l.n]

                def out(i, u):
                    if has(i, l.tiles):
                        u = u % 4
                        dve.wait_ge(m.rout_done.sem, m.rout_done.at(i + 1))
                        if not isinstance(i, int) or i >= 2:
                            yscat = (m.yscat0, m.yscat1, m.yscat2, m.yscat3)[(u - 2) % 4]
                            j = i - 2
                            dve.wait_ge(yscat.sem, yscat.at(16 * (j // 4 + 1) if isinstance(j, int) else 4 * (j - (u - 2) % 4) + 16))
                        v_.tensor_copy(m.yo[:, u % 2], ps[:, 7, 0:D]).then_inc(m.y_ready.sem, 1)

                def body(i, u):
                    if has(i, l.tiles):
                        for h in range(l.halves):
                            dve.wait_ge(m.rsilu_ready.sem, m.rsilu_ready.at(i * l.halves + h + 1))
                            dve.wait_ge(m.rup_done.sem, m.rup_done.at(i * l.halves + h + 1))
                            if h == 0:
                                if due(i):
                                    dve.wait_ge(m.mturn_done.sem, m.mturn_done.at(i))
                            v_.tensor_tensor(m.mid[:, h * l.FH:(h + 1) * l.FH], m.silu[:, h * l.FH:(h + 1) * l.FH],
                                             ps[:, 2 + h, 0:l.FH], ALU.mult).then_inc(m.rmid_ready.sem, 1)
                    out(i - 1, u - 1)
                    if has(i, l.tiles) and l.FC > 4:
                        dve.wait_ge(m.mturn_done.sem, m.mturn_done.at(i + 1))
                        if due(i):
                            dve.wait_ge(m.rout_done.sem, m.rout_done.at(i))
                        v_.tensor_copy(m.midT[:, 4], ps[:, 6, 0:P])
                        r = l.rows(5)
                        v_.tensor_copy(m.midT[0:r, 5], ps[0:r, 6, P:2 * P]).then_inc(m.midT_d.sem, 1)
                run_tiles(dve, l, body, 0)

            attention(LAYERS[0])
            dispatch(LAYERS[0])
            shared(LAYERS[0])
            routed(LAYERS[0])
            attention(LAYERS[1])
            dispatch(LAYERS[1])
            shared(LAYERS[1])
            routed(LAYERS[1])
            l, m = LAYERS[1], B[1]
            own = Steps(Count(dve_last))
            dve.wait_ge(m.gate_ready.sem, m.gate_ready.at(1))
            v_.tensor_scalar(token_w[0:T], token_w[0:T], tanh_g[0:T, 3:4], None, ALU.mult).then_inc(own.sem, own.one())
            dve.wait_ge(own.sem, own.total())
            fin_in = (m.fin_in0, m.fin_in1, m.fin_in2, m.fin_in3)

            def add(j, u):
                dve.wait_ge(fin_in[u].sem, fin_in[u].at(16 * (j // 4 + 1) if isinstance(j, int) else 4 * (j - u) + 16))
                xt = tile_of(xs, j)
                tw = token_w[0:T, bass.ds(j, 1), :].rearrange("p a k -> p (a k)")
                v_.scalar_tensor_tensor(xt, m.fin[0:T, u, 0], tw[:, 0:1], xt, ALU.mult, ALU.add).then_inc(own.sem, own.one())
                dve.wait_ge(own.sem, own.total())
                v_.scalar_tensor_tensor(xt, m.fin[0:T, u, 1], tw[:, 1:2], xt, ALU.mult, ALU.add
                                        ).then_inc(m.fin_ready.sem, 1)
            n = own.n
            with dve.Fori(0, NB - 3, 4) as r:
                own.base = r
                for u in range(4):
                    add(r + u, u)

        @block.gpsimd
        def _(pool):
            g_ = nc.gpsimd
            g_.memset(ident, 0.0).then_inc(ident_ready, 1)
            g_.memset(ones, 1.0).then_inc(ident_ready, 1)
            pool.wait_ge(ident_ready, 2)
            g_.affine_select(out=ident, in_=ident, compare_op=ALU.not_equal, fill=1.0, base=0, pattern=[[-1, P]],
                             channel_multiplier=1).then_inc(ident_ready, 1)
            g_.affine_select(out=before, in_=ones[:, 0:T], compare_op=ALU.is_gt, fill=0.0, base=0, pattern=[[1, T]],
                             channel_multiplier=-1).then_inc(ident_ready, 1)
            g_.memset(zero, 0.0).then_inc(zeros_ready, 1)
            pool.wait_ge(zeros_ready, 1)
            for l in LAYERS:
                g_.iota(pad_rows[l.n], pattern=[[P, l.tiles]], base=NB * T * l.K, channel_multiplier=1
                        ).then_inc(pads_ready, 1)
                pool.wait_ge(pads_ready, l.n + 1)

            def zero_rows(l, zeros, lo, hi):
                rows = xg[l.n].rearrange("(j p) c -> p j c", p=P)
                pool.dma_start(rows[:, lo:hi, 0:D], zeros.unsqueeze(1).to_broadcast([P, hi - lo, D])
                               ).then_inc(dispatch_zeroed[l.n], 16)
                pool.dma_start(rows[:, lo:hi, D:ROW].bitcast(I32), pad_rows[l.n][:, lo:hi].unsqueeze(2),
                               allow_slow_non_contiguous=True).then_inc(dispatch_zeroed[l.n], 16)

            def attention(l):
                a = A[l.n]

                def body(i, u):
                    if l.n == 0 and isinstance(i, int) and i in (1, 2, 3):
                        part = l.tiles // 3
                        zero_rows(l, zero, (i - 1) * part, i * part)
                    b, v = i - 4, u
                    if has(b):
                        pool.wait_ge(a.rstd_ready.sem, a.rstd_ready.at(i + 4))
                        g_.tensor_tensor(a.xn[0:T, v % 2], tile_of(xs, b),
                                         mv[0:T, (u - 1) % 2, 4, 0:1].to_broadcast([T, D]), ALU.subtract
                                         ).then_inc(a.xn_centred.sem, 1)
                        pool.wait_ge(a.xn_centred.sem, a.xn_centred.at(b + 1))
                        g_.tensor_tensor(a.xn[0:T, v % 2], a.xn[0:T, v % 2],
                                         rstd[0:T, (u - 1) % 2, 4:5].to_broadcast([T, D]), ALU.mult
                                         ).then_inc(a.xn_ready.sem, 1)
                    b = i + 3
                    if has(b):
                        offset = a.bp if l.n == 0 else a.b2
                        if l.n == 0 and isinstance(b, int) and b == 0:
                            pool.wait_ge(a.setup_dve.sem, a.setup_dve.at(2))
                        pool.wait_ge(a.xt_ready.sem, a.xt_ready.at(b + 1))
                        g_.tensor_tensor(tile_of(xs, b), tile_of(xs, b), offset[0:T], ALU.add
                                         ).then_inc(a.xb_ready.sem, 1)
                    b, v = i - 5, (u - 5) % 4
                    if has(b):
                        if l.n == 0 and isinstance(b, int) and b == 13:
                            pool.wait_ge(dispatch_zeroed[0], 96)
                        pool.wait_ge(a.xnTb_ready.sem, a.xnTb_ready.at(b + 1))
                        g_.tensor_copy(xnT[:, :, bass.ds(b * T, T)], a.xnTb[:, v % 2]).then_inc(a.xnT_ready.sem, 1)
                        pool.wait_ge(a.xnT_ready.sem, a.xnT_ready.at(b + 1))
                        rows_out = (a.rows_out0, a.rows_out1)[v % 2]
                        pool.wait_ge(rows_out.sem, rows_out.at(16 * (b // 2 + 1) if isinstance(b, int)
                                                               else 8 * (b - v % 2) + 16))
                loop(pool, body, 5)

            def dispatch(l):
                a, m = A[l.n], B[l.n]
                own = Steps(m.own_pool)
                pool.wait_ge(dispatch_zeroed[l.n], 96 if l.n == 0 else 32)
                attention_left(pool, l)
                g_.iota(m.rev_i, pattern=[[-1, E]], base=E, channel_multiplier=0).then_inc(m.iota_done.sem, 1)
                g_.iota(m.thr_i, pattern=[[P, 14]], base=0, channel_multiplier=0).then_inc(m.iota_done.sem, 1)
                g_.iota(m.tile_i, pattern=[[1, l.tiles]], base=0, channel_multiplier=0).then_inc(m.iota_done.sem, 1)
                g_.iota(m.dest, pattern=[[T * l.K, NB], [1, l.K]], base=0, channel_multiplier=l.K
                        ).then_inc(m.iota_done.sem, 1)
                for c in range(l.FC):
                    r = l.rows(c)
                    pool.wait_ge(m.silu_ready.sem, m.silu_ready.at(c + 1))
                    pool.wait_ge(m.up_copied.sem, m.up_copied.at(c + 1))
                    g_.tensor_tensor(m.midT_s[0:r, c], m.silu_s[0:r, c % 2], m.midT_s[0:r, c], ALU.mult
                                     ).then_inc(m.mid_ready.sem, 1)
                pool.wait_ge(m.disp_ready.sem, m.disp_ready.at(1))
                pool.wait_ge(m.gate_ready.sem, m.gate_ready.at(1))
                pool.wait_ge(m.iota_done.sem, m.iota_done.at(4))
                rows_in, scat = (m.rows_in0, m.rows_in1), (m.scat0, m.scat1)

                def four(g, h):
                    pool.wait_ge(rows_in[h].sem, rows_in[h].at(64 * (g // 2 + 1) if isinstance(g, int)
                                                               else 32 * (g - h) + 64))
                    rows = m.rows[0:T, 4 * h:4 * h + 4]
                    at = bass.ds(g * 4, 4)
                    g_.tensor_copy(rows[:, :, D].bitcast(I32), m.dest[0:T, at]
                                   ).then_inc(own.sem, own.one())
                    g_.tensor_copy(pos_ring[0:T, 4 * h:4 * h + 4], pos_i[0:T, at]).then_inc(own.sem, own.one())
                    if l.n == 0:
                        g_.tensor_copy(gate_ring[0:T, 4 * h:4 * h + 4],
                                       token_w[0:T, at, 0:1].rearrange("p a k -> p (a k)")
                                       ).then_inc(own.sem, own.one())
                    pool.wait_ge(own.sem, own.total())
                    for u in range(4):
                        pos = pos_ring[0:T, 4 * h + u:4 * h + u + 1]
                        pool.nop(nofuse=True)
                        if l.n == 0:
                            g_.tensor_scalar(rows[:, u, 0:D], rows[:, u, 0:D], gate_ring[0:T, 4 * h + u:4 * h + u + 1],
                                             None, ALU.mult).then_inc(own.sem, own.one())
                            pool.wait_ge(own.sem, own.total())
                            pool.nop(nofuse=True)
                        g_.indirect_dma_start(out=xg[l.n][:, :],
                                              out_offset=bass.IndirectOffsetOnAxis(ap=pos, axis=0),
                                              in_=rows[:, u], in_offset=None).then_inc(scat[h].sem, 16)
                four(0, 0)
                per = own.n
                four(1, 1)
                with pool.Fori(2, NB * l.K // 4 - 1, 2) as r:
                    own.base = (r - 2) * per
                    for h in range(2):
                        four(r + h, h)

            def routed(l):
                m = B[l.n]
                yscat = (m.yscat0, m.yscat1, m.yscat2, m.yscat3)

                def body(i, u):
                    if has(i, l.tiles):
                        pool.wait_ge(m.y_ready.sem, m.y_ready.at(i + 1))
                        pool.nop(nofuse=True)
                        g_.indirect_dma_start(out=yg[l.n][:, :],
                                              out_offset=bass.IndirectOffsetOnAxis(
                                                  ap=m.g[:, u, D:ROW].bitcast(I32), axis=0),
                                              in_=m.yo[:, u % 2], in_offset=None).then_inc(yscat[u].sem, 16)
                run_tiles(pool, l, body, 0)

            for l in LAYERS:
                if l.n == 1:
                    a = A[1]
                    pool.wait_ge(B[0].shared_done.sem, B[0].shared_done.at(NB // GT))
                    pool.wait_ge(a.consts_in.sem, a.consts_in.at(32))
                    pool.dma_start(a.b2, w2_b.partition_broadcast(P)).then_inc(a.b2_in.sem, 16)
                    pool.wait_ge(a.b2_in.sem, a.b2_in.at(16))
                    g_.tensor_scalar(a.b2, a.b2, tanh_g[:, 1:2], None, ALU.mult).then_inc(a.setup_dve.sem, 1)
                    pool.wait_ge(a.setup_dve.sem, a.setup_dve.at(1))
                attention(l)
                dispatch(l)
                if l.n == 0:
                    g_.memset(R[:, 5888:6144], 0.0).then_inc(zeros_ready, 1)
                    pool.wait_ge(zeros_ready, 2)
                    zero_rows(LAYERS[1], R[:, 5888:6144], 0, LAYERS[1].tiles)
                routed(l)


_INS = ['x', 'ctx_1024', 'mask_BxS2_ik0', 'g_xattn', 'g_ffn', 'L0_xattn_ln_t_g', 'L0_xattn_ln_t_b',
        'L0_xattn_ln_a_g', 'L0_xattn_ln_a_b', 'L0_xattn_Wq', 'L0_xattn_bq', 'L0_xattn_Wk', 'L0_xattn_bk',
        'L0_xattn_Wv', 'L0_xattn_bv', 'L0_xattn_ln_p_g', 'L0_xattn_ln_p_b', 'L0_ffn_router_DE', 'L0_ffn_w1_eDF',
        'L0_ffn_w3_eDF', 'L0_ffn_w2_eFD', 'L0_ffn_ws1_DF', 'L0_ffn_ws3_DF', 'L0_ffn_ws2_FD', 'L1_xattn_w1_w',
        'L1_xattn_w1_b', 'L1_xattn_w2_w', 'L1_xattn_w2_b', 'L1_ffn_Wr', 'L1_ffn_rb', 'L1_ffn_W1', 'L1_ffn_W2',
        'L1_ffn_W3', 'L1_ffn_Ws1', 'L1_ffn_Ws2', 'L1_ffn_Ws3']
_OUTS = [((NB, T, D), 'float32')]


def kernel(**inputs):
    import numpy as _np
    import concourse.bacc as _bacc
    from concourse import mybir as _mybir
    from concourse.bass_utils import run_bass_kernel_spmd as _run

    nc = _bacc.Bacc("TRN2", target_bir_lowering=False, num_devices=1)
    arrays, args = {}, []
    for name in _INS:
        a = _np.ascontiguousarray(inputs[name])
        arrays[f"in_{name}_dram"] = a
        args.append(nc.dram_tensor(f"in_{name}_dram", a.shape, _mybir.dt.from_np(a.dtype), kind="ExternalInput").ap())
    for i, (shape, dtype) in enumerate(_OUTS):
        dt = _mybir.dt.from_np(_np.dtype(dtype))
        args.append(nc.dram_tensor(f"out_{i}_dram", shape, dt, kind="ExternalOutput").ap())
    flamingo(nc, *args)
    r = _run(nc, [arrays], core_ids=[0])
    got = tuple(r.results[0][f"out_{i}_dram"] for i in range(len(_OUTS)))
    return got[0]
```
